# Optimizing a Trainium2 kernel written in Bass

```python
import numpy as np
import jax
import jax.numpy as jnp

def _softmax(x, axis=-1):
    return jax.nn.softmax(x, axis=axis)

def _gelu(x):
    return jax.nn.gelu(x, approximate=True)

def _silu(x):
    return jax.nn.silu(x)

def _sigmoid(x):
    return jax.nn.sigmoid(x)

def _layernorm(x, axis=-1, eps=1e-05):
    m = jnp.mean(x, axis=axis, keepdims=True)
    v = jnp.var(x, axis=axis, keepdims=True)
    return (x - m) / jnp.sqrt(v + eps)

def _scatter_add(tgt, idx, src, axis=0):
    return tgt.at[idx].add(src)

def _segment_sum(src, seg, n):
    return jax.ops.segment_sum(src, seg, n)
kernel_name = 'mk_xattn_ffn_d4_seqx_r8_ff7ce0'

def setup_inputs(seed: int=0):
    np.random.seed(seed)
    _w = jnp.asarray

    def _rec_inputs():
        import jax
        import jax.numpy as jnp
        _rk = jax.random.key(seed)
        x = 7.22e-05 + 1 * jax.random.normal(jax.random.fold_in(_rk, 1), (32, 64, 128), jnp.float32)
        _lenS = 64 - jax.random.randint(jax.random.fold_in(_rk, 7), (32,), 0, max(1, 64 // 4) + 1, jnp.int32)
        _lenS2 = 64 - jax.random.randint(jax.random.fold_in(_rk, 8), (32,), 0, max(1, 64 // 4) + 1, jnp.int32)
        _ctx_1024P = jax.random.normal(jax.random.fold_in(_rk, 11), (32, 16, 128), jnp.float32)
        _ctx_1024c = jax.random.dirichlet(jax.random.fold_in(_rk, 511), 0.3 * jnp.ones((16,), jnp.float32), (32, 64))
        _ctx_1024t = jnp.einsum('bsk,bkd->bsd', _ctx_1024c, _ctx_1024P)
        _ctx_1024t = _ctx_1024t * jax.lax.rsqrt(jnp.mean(jnp.square(_ctx_1024t)) + 1e-12) * 0.953939
        ctx_1024 = 4.13588e-05 + 0.999923 * (_ctx_1024t + 0.3 * jax.random.normal(jax.random.fold_in(_rk, 611), (32, 64, 128), jnp.float32))
        fside_Bx16xSxS2_0 = 9.80324e-06 + 0.100009 * jax.random.normal(jax.random.fold_in(_rk, 13), (32, 16, 64, 64), jnp.float32)
        fside_SxS2_0 = -2.64403e-05 + 0.100002 * jax.random.normal(jax.random.fold_in(_rk, 15), (64, 64), jnp.float32)
        _validS = jnp.arange(64)[None, :] < _lenS[:, None]
        _validS2 = jnp.arange(64)[None, :] < _lenS2[:, None]
        _causal = jnp.tril(jnp.ones((64, 64), dtype=bool))
        mask_BxSxS2_bf1 = jnp.ones((32, 64, 64), dtype=bool)
        mask_BxS2_bf0 = jnp.logical_not(jnp.ones((32, 64), dtype=bool))
        return (x, ctx_1024, fside_Bx16xSxS2_0, fside_SxS2_0, mask_BxSxS2_bf1, mask_BxS2_bf0)
    x, ctx_1024, fside_Bx16xSxS2_0, fside_SxS2_0, mask_BxSxS2_bf1, mask_BxS2_bf0 = _rec_inputs()

    def _L0_xattn_setup():
        import jax, jax.numpy as jnp
        import numpy as np
        D_MODEL = 128
        KEY_DIM = 128
        VALUE_DIM = 128
        N_HEADS = 16
        key = jax.random.key(seed)
        ks = jax.random.split(key, 12)
        B, S = (4, 256)
        s = 0.02
        return {'queries': jax.random.normal(ks[0], (B, S, D_MODEL), jnp.float32), 'keys': jax.random.normal(ks[1], (B, S, D_MODEL), jnp.float32), 'values': jax.random.normal(ks[2], (B, S, D_MODEL), jnp.float32), 'masks': jnp.ones((B, S, S), dtype=bool), 'Wq': jax.random.normal(ks[3], (D_MODEL, KEY_DIM), jnp.float32) * s, 'bq': jnp.zeros((KEY_DIM,), jnp.float32), 'Wk': jax.random.normal(ks[4], (D_MODEL, KEY_DIM), jnp.float32) * s, 'bk': jnp.zeros((KEY_DIM,), jnp.float32), 'Wv': jax.random.normal(ks[5], (D_MODEL, VALUE_DIM), jnp.float32) * s, 'bv': jnp.zeros((VALUE_DIM,), jnp.float32), 'Wo': jax.random.normal(ks[6], (VALUE_DIM, D_MODEL), jnp.float32) * s, 'bo': jnp.zeros((D_MODEL,), jnp.float32)}
    _L0_xattn_all = _L0_xattn_setup()
    _L0_xattn_in = {k: v for k, v in _L0_xattn_all.items() if k in ('Wq', 'bq', 'Wk', 'bk', 'Wv', 'bv', 'Wo', 'bo')}
    del _L0_xattn_all

    def _L0_ffn_setup():
        import jax, jax.numpy as jnp
        import numpy as np
        B, S, H, FFN, E = (2, 256, 128, 512, 8)
        key = jax.random.key(seed)
        k0, k1, k2, k3 = jax.random.split(key, 4)
        return {'hidden_states': jax.random.normal(k0, (B, S, H), dtype=jnp.float32), 'Wr': jax.random.normal(k1, (H, E), dtype=jnp.float32) * 0.02, 'br': jnp.zeros((E,), dtype=jnp.float32), 'W1': jax.random.normal(k2, (E, H, FFN), dtype=jnp.float32) * 0.02, 'W2': jax.random.normal(k3, (E, FFN, H), dtype=jnp.float32) * 0.02}
    _L0_ffn_all = _L0_ffn_setup()
    _L0_ffn_in = {k: v for k, v in _L0_ffn_all.items() if k in ('Wr', 'br', 'W1', 'W2')}
    del _L0_ffn_all

    def _L1_xattn_setup():
        import jax, jax.numpy as jnp
        import numpy as np
        D1, D2, D3 = (128, 128, 128)
        key = jax.random.key(seed)
        k1, k2, kw, kb = jax.random.split(key, 4)
        x1 = jax.random.normal(k1, (8, 256, D1), dtype=jnp.float32)
        x2 = jax.random.normal(k2, (8, 256, D2), dtype=jnp.float32)
        bound = 1.0 / np.sqrt(D1 + D2)
        W = jax.random.uniform(kw, (D3, D1 + D2), minval=-bound, maxval=bound, dtype=jnp.float32)
        b = jax.random.uniform(kb, (D3,), minval=-bound, maxval=bound, dtype=jnp.float32)
        return {'x1': x1, 'x2': x2, 'W': W, 'b': b}
    _L1_xattn_all = _L1_xattn_setup()
    _L1_xattn_in = {k: v for k, v in _L1_xattn_all.items() if k in ('W', 'b')}
    del _L1_xattn_all

    def _L1_ffn_setup():
        import jax, jax.numpy as jnp
        import numpy as np

        def _bitlinear(x, w_latent):
            scale = jax.lax.stop_gradient(jnp.clip(jnp.mean(jnp.abs(w_latent), axis=1, keepdims=True), 1e-05, None))
            tern = jnp.clip(jnp.round(w_latent / scale), -1.0, 1.0)
            w = w_latent + jax.lax.stop_gradient(tern - w_latent)
            return x @ (w * scale).T
        key = jax.random.key(seed)
        ks = jax.random.split(key, 6)
        dim, hidden, rank = (128, 512, 16)
        B, S = (4, 512)
        x = jax.random.normal(ks[0], (B, S, dim), dtype=jnp.float32)
        w_fc = 0.02 * jax.random.normal(ks[1], (hidden, dim), dtype=jnp.float32)
        w_proj = 0.02 * jax.random.normal(ks[2], (dim, hidden), dtype=jnp.float32)
        u = 0.02 * jax.random.normal(ks[3], (hidden, rank), dtype=jnp.float32)
        v = 0.02 * jax.random.normal(ks[4], (rank, dim), dtype=jnp.float32)
        fast_b = jax.random.normal(ks[5], (rank, rank), dtype=jnp.float32)
        gate = jnp.float32(0.05)
        return {'x': x, 'fast_b': fast_b, 'w_fc': w_fc, 'w_proj': w_proj, 'u': u, 'v': v, 'gate': gate}
    _L1_ffn_all = _L1_ffn_setup()
    _L1_ffn_in = {k: v for k, v in _L1_ffn_all.items() if k in ('fast_b', 'w_fc', 'w_proj', 'u', 'v', 'gate')}
    del _L1_ffn_all

    def _L2_xattn_setup():
        import jax, jax.numpy as jnp
        import numpy as np
        E = 128
        H = 16
        D = E // H
        NUM_BUCKETS = 32
        MAX_DISTANCE = 128

        def _relative_position_bucket(rel, num_buckets=NUM_BUCKETS, max_distance=MAX_DISTANCE):
            nb = num_buckets // 2
            buckets = (rel > 0).astype(jnp.int32) * nb
            rel = jnp.abs(rel)
            max_exact = nb // 2
            is_small = rel < max_exact
            rel_f = jnp.maximum(rel, 1).astype(jnp.float32)
            large = max_exact + (jnp.log(rel_f / max_exact) / np.log(max_distance / max_exact) * (nb - max_exact)).astype(jnp.int32)
            large = jnp.minimum(large, nb - 1)
            return buckets + jnp.where(is_small, rel, large)
        key = jax.random.key(seed)
        ks = jax.random.split(key, 6)
        B, S, K = (2, 256, 256)
        w = 0.02
        return {'hidden_states': jax.random.normal(ks[0], (B, S, E), jnp.float32), 'key_value_states': jax.random.normal(ks[1], (B, K, E), jnp.float32), 'Wq': jax.random.normal(ks[2], (E, E), jnp.float32) * w, 'Wkv': jax.random.normal(ks[3], (E, 2 * E), jnp.float32) * w, 'Wo': jax.random.normal(ks[4], (E, E), jnp.float32) * w, 'rel_bias': jax.random.normal(ks[5], (NUM_BUCKETS, H), jnp.float32) * w}
    _L2_xattn_all = _L2_xattn_setup()
    _L2_xattn_in = {k: v for k, v in _L2_xattn_all.items() if k in ('Wq', 'Wkv', 'Wo', 'rel_bias')}
    del _L2_xattn_all

    def _L2_ffn_setup():
        import jax, jax.numpy as jnp
        import numpy as np
        D_MODEL, D_FF, RANK = (128, 512, 32)
        B, S = (4, 512)
        key = jax.random.key(seed)
        ks = jax.random.split(key, 7)
        return {'x': jax.random.normal(ks[0], (B, S, D_MODEL), dtype=jnp.float32), 'U1': jax.random.normal(ks[1], (D_MODEL, RANK), dtype=jnp.float32) * 0.02, 'V1': jax.random.normal(ks[2], (RANK, D_FF), dtype=jnp.float32) * 0.02, 'b1': jnp.zeros((D_FF,), dtype=jnp.float32), 'U2': jax.random.normal(ks[3], (D_FF, RANK), dtype=jnp.float32) * 0.02, 'V2': jax.random.normal(ks[4], (RANK, D_MODEL), dtype=jnp.float32) * 0.02, 'b2': jnp.zeros((D_MODEL,), dtype=jnp.float32)}
    _L2_ffn_all = _L2_ffn_setup()
    _L2_ffn_in = {k: v for k, v in _L2_ffn_all.items() if k in ('U1', 'V1', 'b1', 'U2', 'V2', 'b2')}
    del _L2_ffn_all

    def _L3_xattn_setup():
        import jax, jax.numpy as jnp
        import numpy as np
        E = 128
        H = 16
        D = E // H
        key = jax.random.key(seed)
        ks = jax.random.split(key, 12)
        B, T, S = (2, 256, 256)
        inp = {'query': jax.random.normal(ks[0], (B, T, E), jnp.float32), 'key': jax.random.normal(ks[1], (B, S, E), jnp.float32), 'value': jax.random.normal(ks[2], (B, S, E), jnp.float32), 'spatial_bias': jax.random.normal(ks[3], (B, H, T, S), jnp.float32) * 0.1, 'directional_bias': jax.random.normal(ks[4], (B, H, T, S), jnp.float32) * 0.1, 'key_padding_mask': jnp.zeros((B, S), dtype=bool), 'attn_mask': jax.random.normal(ks[5], (T, S), jnp.float32) * 0.1, 'Wq': jax.random.normal(ks[6], (E, E), jnp.float32) / np.sqrt(E), 'bq': jnp.zeros((E,), jnp.float32), 'Wk': jax.random.normal(ks[7], (E, E), jnp.float32) / np.sqrt(E), 'bk': jnp.zeros((E,), jnp.float32), 'Wv': jax.random.normal(ks[8], (E, E), jnp.float32) / np.sqrt(E), 'bv': jnp.zeros((E,), jnp.float32), 'Wo': jax.random.normal(ks[9], (E, E), jnp.float32) / np.sqrt(E), 'bo': jnp.zeros((E,), jnp.float32)}
        return inp
    _L3_xattn_all = _L3_xattn_setup()
    _L3_xattn_in = {k: v for k, v in _L3_xattn_all.items() if k in ('Wq', 'bq', 'Wk', 'bk', 'Wv', 'bv', 'Wo', 'bo')}
    del _L3_xattn_all

    def _L3_ffn_setup():
        import jax, jax.numpy as jnp
        import numpy as np
        HIDDEN = 128
        N_EXPERTS = 8
        TOP_K = 2
        INTER = 176
        N_SHARED = 2
        SCALE = 1.0
        key = jax.random.key(seed)
        ks = jax.random.split(key, 9)
        s_h = 1.0 / np.sqrt(HIDDEN)
        s_i = 1.0 / np.sqrt(INTER)
        x = jax.random.normal(ks[0], (2, 256, HIDDEN), dtype=jnp.float32)
        gate_w = jax.random.uniform(ks[1], (N_EXPERTS, HIDDEN), jnp.float32, -s_h, s_h)
        wg = jax.random.uniform(ks[2], (N_EXPERTS, HIDDEN, INTER), jnp.float32, -s_h, s_h)
        wu = jax.random.uniform(ks[3], (N_EXPERTS, HIDDEN, INTER), jnp.float32, -s_h, s_h)
        wd = jax.random.uniform(ks[4], (N_EXPERTS, INTER, HIDDEN), jnp.float32, -s_i, s_i)
        si = INTER * N_SHARED
        s_si = 1.0 / np.sqrt(si)
        swg = jax.random.uniform(ks[5], (HIDDEN, si), jnp.float32, -s_h, s_h)
        swu = jax.random.uniform(ks[6], (HIDDEN, si), jnp.float32, -s_h, s_h)
        swd = jax.random.uniform(ks[7], (si, HIDDEN), jnp.float32, -s_si, s_si)
        return {'x': x, 'gate_w': gate_w, 'wg': wg, 'wu': wu, 'wd': wd, 'swg': swg, 'swu': swu, 'swd': swd}
    _L3_ffn_all = _L3_ffn_setup()
    _L3_ffn_in = {k: v for k, v in _L3_ffn_all.items() if k in ('gate_w', 'wg', 'wu', 'wd', 'swg', 'swu', 'swd')}
    del _L3_ffn_all
    return {'x': x, 'ctx_1024': ctx_1024, 'fside_Bx16xSxS2_0': fside_Bx16xSxS2_0, 'fside_SxS2_0': fside_SxS2_0, 'mask_BxSxS2_bf1': mask_BxSxS2_bf1, 'mask_BxS2_bf0': mask_BxS2_bf0, 'L0_xattn_Wq': _L0_xattn_in['Wq'], 'L0_xattn_bq': _L0_xattn_in['bq'], 'L0_xattn_Wk': _L0_xattn_in['Wk'], 'L0_xattn_bk': _L0_xattn_in['bk'], 'L0_xattn_Wv': _L0_xattn_in['Wv'], 'L0_xattn_bv': _L0_xattn_in['bv'], 'L0_xattn_Wo': _L0_xattn_in['Wo'], 'L0_xattn_bo': _L0_xattn_in['bo'], 'L0_ffn_Wr': _L0_ffn_in['Wr'], 'L0_ffn_br': _L0_ffn_in['br'], 'L0_ffn_W1': _L0_ffn_in['W1'], 'L0_ffn_W2': _L0_ffn_in['W2'], 'L1_xattn_W': _L1_xattn_in['W'], 'L1_xattn_b': _L1_xattn_in['b'], 'L1_ffn_fast_b': _L1_ffn_in['fast_b'], 'L1_ffn_w_fc': _L1_ffn_in['w_fc'], 'L1_ffn_w_proj': _L1_ffn_in['w_proj'], 'L1_ffn_u': _L1_ffn_in['u'], 'L1_ffn_v': _L1_ffn_in['v'], 'L1_ffn_gate': _L1_ffn_in['gate'], 'L2_xattn_Wq': _L2_xattn_in['Wq'], 'L2_xattn_Wkv': _L2_xattn_in['Wkv'], 'L2_xattn_Wo': _L2_xattn_in['Wo'], 'L2_xattn_rel_bias': _L2_xattn_in['rel_bias'], 'L2_ffn_U1': _L2_ffn_in['U1'], 'L2_ffn_V1': _L2_ffn_in['V1'], 'L2_ffn_b1': _L2_ffn_in['b1'], 'L2_ffn_U2': _L2_ffn_in['U2'], 'L2_ffn_V2': _L2_ffn_in['V2'], 'L2_ffn_b2': _L2_ffn_in['b2'], 'L3_xattn_Wq': _L3_xattn_in['Wq'], 'L3_xattn_bq': _L3_xattn_in['bq'], 'L3_xattn_Wk': _L3_xattn_in['Wk'], 'L3_xattn_bk': _L3_xattn_in['bk'], 'L3_xattn_Wv': _L3_xattn_in['Wv'], 'L3_xattn_bv': _L3_xattn_in['bv'], 'L3_xattn_Wo': _L3_xattn_in['Wo'], 'L3_xattn_bo': _L3_xattn_in['bo'], 'L3_ffn_gate_w': _L3_ffn_in['gate_w'], 'L3_ffn_wg': _L3_ffn_in['wg'], 'L3_ffn_wu': _L3_ffn_in['wu'], 'L3_ffn_wd': _L3_ffn_in['wd'], 'L3_ffn_swg': _L3_ffn_in['swg'], 'L3_ffn_swu': _L3_ffn_in['swu'], 'L3_ffn_swd': _L3_ffn_in['swd']}

def reference(x, ctx_1024, fside_Bx16xSxS2_0, fside_SxS2_0, mask_BxSxS2_bf1, mask_BxS2_bf0, L0_xattn_Wq, L0_xattn_bq, L0_xattn_Wk, L0_xattn_bk, L0_xattn_Wv, L0_xattn_bv, L0_xattn_Wo, L0_xattn_bo, L0_ffn_Wr, L0_ffn_br, L0_ffn_W1, L0_ffn_W2, L1_xattn_W, L1_xattn_b, L1_ffn_fast_b, L1_ffn_w_fc, L1_ffn_w_proj, L1_ffn_u, L1_ffn_v, L1_ffn_gate, L2_xattn_Wq, L2_xattn_Wkv, L2_xattn_Wo, L2_xattn_rel_bias, L2_ffn_U1, L2_ffn_V1, L2_ffn_b1, L2_ffn_U2, L2_ffn_V2, L2_ffn_b2, L3_xattn_Wq, L3_xattn_bq, L3_xattn_Wk, L3_xattn_bk, L3_xattn_Wv, L3_xattn_bv, L3_xattn_Wo, L3_xattn_bo, L3_ffn_gate_w, L3_ffn_wg, L3_ffn_wu, L3_ffn_wd, L3_ffn_swg, L3_ffn_swu, L3_ffn_swd):
    import jax
    import jax.numpy as jnp

    def _L0_xattn_ref(queries, keys, values, masks, Wq, bq, Wk, bk, Wv, bv, Wo, bo):
        import jax, jax.numpy as jnp
        import numpy as np
        D_MODEL = 128
        KEY_DIM = 128
        VALUE_DIM = 128
        N_HEADS = 16
        B, S, _ = queries.shape
        H = N_HEADS
        dk = KEY_DIM // H
        dv = VALUE_DIM // H
        q = (queries @ Wq + bq).reshape(B, S, H, dk).transpose(0, 2, 1, 3)
        k = (keys @ Wk + bk).reshape(B, S, H, dk).transpose(0, 2, 1, 3)
        v = (values @ Wv + bv).reshape(B, S, H, dv).transpose(0, 2, 1, 3)
        scores = jnp.einsum('bhqd,bhkd->bhqk', q, k) / jnp.sqrt(jnp.float32(dk))
        scores = jnp.where(masks[:, None, :, :], scores, jnp.float32(-1000000000.0))
        attn = jax.nn.softmax(scores, axis=-1)
        out = jnp.einsum('bhqk,bhkd->bhqd', attn, v)
        cat = out.transpose(0, 2, 1, 3).reshape(B, S, VALUE_DIM)
        cat = cat.transpose(0, 2, 1).reshape(B, S, VALUE_DIM)
        return cat @ Wo + bo

    def _L0_ffn_ref(hidden_states, Wr, br, W1, W2):
        import jax, jax.numpy as jnp
        import numpy as np
        B, S, H, FFN, E = (2, 256, 128, 512, 8)
        b, s, h = hidden_states.shape
        x = hidden_states.reshape(-1, h)
        route = jax.nn.sigmoid(x @ Wr + br)
        max_prob = jnp.max(route, axis=1, keepdims=True)
        max_ind = jnp.argmax(route, axis=1)
        out = jnp.zeros_like(x)
        n_experts = Wr.shape[1]
        for e in range(n_experts):
            mask = (max_ind == e)[:, None].astype(x.dtype)
            y = jax.nn.gelu(x @ W1[e], approximate=False) @ W2[e]
            out = out + mask * y
        out = out * max_prob
        return out.reshape(b, s, h)

    def _L1_xattn_ref(x1, x2, W, b):
        import jax, jax.numpy as jnp
        import numpy as np
        D1, D2, D3 = (128, 128, 128)
        d1 = x1.shape[-1]
        W1 = W[:, :d1]
        W2 = W[:, d1:]
        part1 = jnp.einsum('bld,ed->ble', x1, W1)
        part2 = jnp.einsum('bld,ed->be', x2, W2) / x2.shape[1]
        return part1 + part2[:, None, :] + b

    def _L1_ffn_ref(x, fast_b, w_fc, w_proj, u, v, gate):
        import jax, jax.numpy as jnp
        import numpy as np

        def _bitlinear(x, w_latent):
            scale = jax.lax.stop_gradient(jnp.clip(jnp.mean(jnp.abs(w_latent), axis=1, keepdims=True), 1e-05, None))
            tern = jnp.clip(jnp.round(w_latent / scale), -1.0, 1.0)
            w = w_latent + jax.lax.stop_gradient(tern - w_latent)
            return x @ (w * scale).T
        h = _bitlinear(x, w_fc) + gate * (x @ v.T @ fast_b.T @ u.T)
        r = jnp.maximum(h, 0.0)
        return _bitlinear(r * r, w_proj)

    def _L2_xattn_ref(hidden_states, key_value_states, Wq, Wkv, Wo, rel_bias):
        import jax, jax.numpy as jnp
        import numpy as np
        E = 128
        H = 16
        D = E // H
        NUM_BUCKETS = 32
        MAX_DISTANCE = 128

        def _relative_position_bucket(rel, num_buckets=NUM_BUCKETS, max_distance=MAX_DISTANCE):
            nb = num_buckets // 2
            buckets = (rel > 0).astype(jnp.int32) * nb
            rel = jnp.abs(rel)
            max_exact = nb // 2
            is_small = rel < max_exact
            rel_f = jnp.maximum(rel, 1).astype(jnp.float32)
            large = max_exact + (jnp.log(rel_f / max_exact) / np.log(max_distance / max_exact) * (nb - max_exact)).astype(jnp.int32)
            large = jnp.minimum(large, nb - 1)
            return buckets + jnp.where(is_small, rel, large)
        B, S, _ = hidden_states.shape
        K = key_value_states.shape[1]
        q = (hidden_states @ Wq).reshape(B, S, H, D).transpose(0, 2, 1, 3)
        kv = (key_value_states @ Wkv).reshape(B, K, 2, H, D)
        k = kv[:, :, 0].transpose(0, 2, 1, 3)
        v = kv[:, :, 1].transpose(0, 2, 1, 3)
        scores = jnp.einsum('bhsd,bhkd->bhsk', q, k)
        rel = jnp.arange(K)[None, :] - jnp.arange(S)[:, None]
        buckets = _relative_position_bucket(rel)
        bias = rel_bias[buckets].transpose(2, 0, 1)[None]
        scores = scores + bias
        attn = jax.nn.softmax(scores.astype(jnp.float32), axis=-1).astype(scores.dtype)
        out = jnp.einsum('bhsk,bhkd->bshd', attn, v).reshape(B, S, E)
        return out @ Wo

    def _L2_ffn_ref(x, U1, V1, b1, U2, V2, b2):
        import jax, jax.numpy as jnp
        import numpy as np
        D_MODEL, D_FF, RANK = (128, 512, 32)
        B, S = (4, 512)
        P = jnp.einsum('bsd,dr->bsr', x, U1)
        H = jax.nn.gelu(jnp.einsum('bsr,rf->bsf', P, V1) + b1)
        Q = jnp.einsum('bsf,fr->bsr', H, U2)
        return jnp.einsum('bsr,rd->bsd', Q, V2) + b2

    def _L3_xattn_ref(query, key, value, spatial_bias, directional_bias, key_padding_mask, attn_mask, Wq, bq, Wk, bk, Wv, bv, Wo, bo):
        import jax, jax.numpy as jnp
        import numpy as np
        E = 128
        H = 16
        D = E // H
        B, T, _ = query.shape
        S = key.shape[1]
        scale = D ** (-0.5)
        q = (query @ Wq.T + bq).reshape(B, T, H, D).transpose(0, 2, 1, 3)
        k = (key @ Wk.T + bk).reshape(B, S, H, D).transpose(0, 2, 1, 3)
        v = (value @ Wv.T + bv).reshape(B, S, H, D).transpose(0, 2, 1, 3)
        scores = jnp.einsum('bhtd,bhsd->bhts', q, k) * scale
        scores = scores + attn_mask[None, None, :, :]
        pad = key_padding_mask[:, None, None, :]
        scores = jnp.where(pad, -jnp.inf, scores)
        if T == S:
            scores = scores + spatial_bias + directional_bias
        probs = jax.nn.softmax(scores, axis=-1)
        out = jnp.einsum('bhts,bhsd->bhtd', probs, v)
        out = out.transpose(0, 2, 1, 3).reshape(B, T, E)
        return out @ Wo.T + bo

    def _L3_ffn_ref(x, gate_w, wg, wu, wd, swg, swu, swd):
        import jax, jax.numpy as jnp
        import numpy as np
        HIDDEN = 128
        N_EXPERTS = 8
        TOP_K = 2
        INTER = 176
        N_SHARED = 2
        SCALE = 1.0
        B, S, H = x.shape
        xf = x.reshape(-1, H)
        T = xf.shape[0]
        logits = xf.astype(jnp.float32) @ gate_w.astype(jnp.float32).T
        scores = jax.nn.softmax(logits, axis=-1)
        topw, topi = jax.lax.top_k(scores, TOP_K)
        denom = topw.sum(axis=-1, keepdims=True) + 1e-20
        topw = topw / denom * SCALE
        wdense = jnp.zeros((T, N_EXPERTS), jnp.float32).at[jnp.arange(T)[:, None], topi].set(topw)
        hg = jnp.einsum('th,ehi->eti', xf, wg)
        hu = jnp.einsum('th,ehi->eti', xf, wu)
        eo = jnp.einsum('eti,eih->eth', jax.nn.silu(hg) * hu, wd)
        y = jnp.einsum('te,eth->th', wdense, eo)
        shared = jax.nn.silu(xf @ swg) * (xf @ swu) @ swd
        return (y + shared).reshape(B, S, H)
    x = x + _L0_xattn_ref(_layernorm(x, axis=-1), ctx_1024, ctx_1024, mask_BxSxS2_bf1, L0_xattn_Wq, L0_xattn_bq, L0_xattn_Wk, L0_xattn_bk, L0_xattn_Wv, L0_xattn_bv, L0_xattn_Wo, L0_xattn_bo)
    x = x + _L0_ffn_ref(_layernorm(x, axis=-1), L0_ffn_Wr, L0_ffn_br, L0_ffn_W1, L0_ffn_W2)
    x = x + _L1_xattn_ref(_layernorm(x, axis=-1), ctx_1024, L1_xattn_W, L1_xattn_b)
    x = x + _L1_ffn_ref(_layernorm(x, axis=-1), L1_ffn_fast_b, L1_ffn_w_fc, L1_ffn_w_proj, L1_ffn_u, L1_ffn_v, L1_ffn_gate)
    x = x + _L2_xattn_ref(_layernorm(x, axis=-1), ctx_1024, L2_xattn_Wq, L2_xattn_Wkv, L2_xattn_Wo, L2_xattn_rel_bias)
    x = x + _L2_ffn_ref(_layernorm(x, axis=-1), L2_ffn_U1, L2_ffn_V1, L2_ffn_b1, L2_ffn_U2, L2_ffn_V2, L2_ffn_b2)
    x = x + _L3_xattn_ref(_layernorm(x, axis=-1), ctx_1024, ctx_1024, fside_Bx16xSxS2_0, fside_Bx16xSxS2_0, mask_BxS2_bf0, fside_SxS2_0, L3_xattn_Wq, L3_xattn_bq, L3_xattn_Wk, L3_xattn_bk, L3_xattn_Wv, L3_xattn_bv, L3_xattn_Wo, L3_xattn_bo)
    x = x + _L3_ffn_ref(_layernorm(x, axis=-1), L3_ffn_gate_w, L3_ffn_wg, L3_ffn_wu, L3_ffn_wd, L3_ffn_swg, L3_ffn_swu, L3_ffn_swd)
    return x

_drawn_inputs = setup_inputs


def setup_inputs(seed=0):
    import zlib

    import numpy as np

    out = dict(_drawn_inputs(seed))
    spreads = {'L0_xattn_bq': (0.0, 2.0),
     'L0_xattn_bk': (0.0, 2.0),
     'L0_xattn_bv': (0.0, 0.32),
     'L0_xattn_bo': (0.0, 0.1),
     'L0_ffn_br': (0.0, 0.293),
     'L2_ffn_b1': (0.0, 0.8),
     'L2_ffn_b2': (0.0, 0.701),
     'L3_xattn_bq': (0.0, 2.0),
     'L3_xattn_bk': (0.0, 2.0),
     'L3_xattn_bv': (0.0, 0.735),
     'L3_xattn_bo': (0.0, 0.68)}
    factors = {'fside_SxS2_0': 30.032,
     'L0_xattn_Wq': 8.0,
     'L0_xattn_Wk': 8.0,
     'L1_ffn_fast_b': 8.0,
     'L1_ffn_w_fc': 5.334,
     'L1_ffn_w_proj': 4.275,
     'L1_ffn_u': 8.0,
     'L1_ffn_v': 8.0,
     'L2_xattn_Wq': 64.0,
     'L2_xattn_rel_bias': 64.0,
     'L2_ffn_U1': 8.0,
     'L2_ffn_V1': 8.0,
     'L2_ffn_U2': 8.0,
     'L2_ffn_V2': 8.0,
     'fside_Bx16xSxS2_0': 8.0,
     'L2_xattn_Wkv': 8.0,
     'L2_xattn_Wo': 8.0,
     'L3_ffn_gate_w': 6.938,
     'L3_ffn_wg': 6.72,
     'L3_ffn_wu': 6.53,
     'L3_ffn_wd': 6.555,
     'L3_ffn_swg': 4.681,
     'L3_ffn_swu': 4.45,
     'L3_ffn_swd': 4.339}
    for name, (base, spread) in spreads.items():
        noise = np.random.default_rng([zlib.crc32(name.encode()), seed]).standard_normal(out[name].shape)
        drawn = base * np.exp(spread * noise) if base else spread * noise
        out[name] = jnp.asarray(drawn.astype(out[name].dtype))
    for name, factor in factors.items():
        out[name] = (out[name] * factor).astype(out[name].dtype)
    return out
```

```python
from contextlib import ExitStack

import numpy as np

import concourse.bass as bass
from concourse import mybir

ALU = mybir.AluOpType
ACT = mybir.ActivationFunctionType
AX_X = mybir.AxisListType.X
F32 = mybir.dt.float32
F16 = mybir.dt.float16
U8 = mybir.dt.uint8
U32 = mybir.dt.uint32
ds = bass.ds

P = 128
B, S, D = 32, 64, 128
H, DH = 16, 8
TILES = B * S // P
CH = 2 * P
GR = 4 * P
GROUPS = TILES // 4
FF = 512
FT = FF // P
E = 8
MI = 176
MC = 88
EPS = 1e-5
QK_SCALE = float(DH) ** -0.5
NEG = -1e9
SATURATED = 16.635532
BUCKETS = 32
REL = 2 * S - 1
TOK = B * S
REGION = TOK + P
ROW = D + 2
NX = 8
NOWHERE = 1 << 20
RT = {"iota": (0, E), "base": (8, E), "k128": (16, TILES), "le": (32, E * E), "k": (96, 40), "part": (136, 1)}


PHASES = [0, "moe0", "lin1", "ffn1", 2, "ffn2", 3, "moe3"]


def bass_transformer(nc, A, K, out):
    ctx = ExitStack()
    with ctx:
        def sb(name, shape, dt=F32):
            return ctx.enter_context(nc.sbuf_tensor(name, shape, dt))

        def sem(name):
            return ctx.enter_context(nc.semaphore(name))

        def row(ap):
            return ap.rearrange("(a n) -> a n", a=1)

        ident = sb("ident", [P, P])
        head_mask = sb("head_mask", [P, 8])
        dup_mask = sb("dup_mask", [P, P])
        route_tab = sb("route_tab", [P, 137])
        place_tab = sb("place_tab", [P, 2 * TILES + 1], U32)
        before = sb("before", [P, P])
        ones = sb("ones", [P, P])
        rel_onehot = sb("rel_onehot", [BUCKETS, REL + 1])
        minus_half = sb("minus_half", [P, 4])
        x = sb("x", [P, TILES * D])
        ctxT = sb("ctxT", [P, B * S])
        tok_in = sb("tok_in", [P, TILES * D])
        wqk0 = sb("wqk0", [P, 3, D])
        wo0 = sb("wo0", [P, 2, D])
        wqkv2 = sb("wqkv2", [P, 3, D])
        wo2 = sb("wo2", [P, D])
        wraw3 = sb("wraw3", [P, 4, D])
        w3T = sb("w3T", [P, 4, D])
        w1raw = sb("w1raw", [P, 2 * D])
        w1T = sb("w1T", [P, 2, D])
        bq = sb("bq", [P, 2, 2])
        bk = sb("bk", [P, 2, 2])
        bv_row = sb("bv_row", [P, D])
        bv_col = sb("bv_col", [P, 1])
        bias_out = sb("bias_out", [P, 4, D])
        router0 = sb("router0", [P, E])
        br0 = sb("br0", [P, E])
        gate3 = sb("gate3", [E, D])
        gate3T = sb("gate3T", [P, E])
        expert_w = sb("expert_w", [P, 2 * E * FF])
        e_up = expert_w[:, 0:E * FF].rearrange("p (e f) -> p e f", e=E)
        e_down = expert_w[:, E * FF:2 * E * FF].rearrange("p (e t d) -> p e t d", e=E, t=FT)

        def carve(at, parts, *shape):
            n = int(np.prod(shape))
            v = expert_w[0:parts, at:at + n]
            return v.rearrange("p (a b) -> p a b", a=shape[0]) if len(shape) == 2 else v, at + n
        m_gu, at = carve(0, P, E, 2 * MI)
        m_down, at = carve(at, MC, 2 * E, D)
        s_gu, at = carve(at, P, 2, 4 * MC)
        s_down, at = carve(at, MC, 4, D)
        fc_raw = sb("fc_raw", [P, FT, D])
        proj_raw = sb("proj_raw", [P, FF])
        u_raw = sb("u_raw", [P, FT, 16])
        v_raw = sb("v_raw", [16, D])
        fast_raw = sb("fast_raw", [16, 16])
        fastT = sb("fastT", [16, 16])
        uT = sb("uT", [16, FF])
        fast_v = sb("fast_v", [16, D])
        gate_col = sb("gate_col", [P, 1])
        tern = sb("tern", [P, FT, P])
        row_scale = sb("row_scale", [P, 8])
        w1eff = sb("w1eff", [P, FF])
        w1out = sb("w1out", [P, FT, D])
        u1 = sb("u1", [P, 32])
        u1T = sb("u1T", [32, D])
        v1r = sb("v1r", [32, FF])
        u2 = sb("u2", [P, FT, 32])
        u2T = sb("u2T", [32, FF])
        v2r = sb("v2r", [32, D])
        b1 = sb("b1", [P, FT])
        w2in = sb("w2in", [P, FF])
        w2out = sb("w2out", [P, FT, D])
        rel_bias = sb("rel_bias", [BUCKETS, H])
        rel_row = sb("rel_row", [H, P])
        ctx_sum = sb("ctx_sum", [P, B])
        per_batch = sb("per_batch", [B, D])
        mask_words = sb("mask_words", [P, TILES, S // 4], U32)
        pad_words = sb("pad_words", [P, TILES, S // 4], U32)
        cap0 = sb("cap0", [P, TILES * S])
        add3 = sb("add3", [P, TILES * S])
        amask = sb("amask", [P, S])
        bias2 = sb("bias2", [P, H, S])

        xnA = sb("xnA", [P, 2, D])
        lnA = sb("lnA", [P, CH])
        stA = sb("stA", [P, 2, 6])
        mvA = sb("mvA", [P, 2, 2])
        rsA = sb("rsA", [P, 2, 2])
        ctxc = [sb(f"ctxc{n}", [P, 4, 2, S]) for n in range(2)]
        q_diag = [sb(f"q_diag{n}", [P, 2, 2, P]) for n in range(2)]
        kT = sb("kT", [P, 2, 2, S])
        k_heads = [sb(f"k_heads{n}", [P, 2, 2, 8, S]) for n in range(2)]
        v_f32 = sb("v_f32", [P, 4, D])
        v_hi = [sb(f"v_hi{n}", [P, 2, 2, H, 9], F16) for n in range(2)]
        v_lo = [sb(f"v_lo{n}", [P, 2, 2, H, 9], F16) for n in range(2)]
        work = sb("work", [P, 4 * H * S])
        sc = [work[:, n * H * S:(n + 1) * H * S].rearrange("p (h k) -> p h k", h=H) for n in range(4)]
        pay = sb("pay", [P, TILES, 2, ROW])
        pay_row = pay[:, :, :, :].rearrange("p t c r -> p (t c r)")
        side = [pay_row[:, n * H * S:(n + 1) * H * S].rearrange("p (h k) -> p h k", h=H) for n in range(4)]
        mx = [sb(f"mx{n}", [P, H]) for n in range(4)]
        p_hi = sb("p_hi", [P, 8, P], F16)
        p_lo = sb("p_lo", [P, 8, P], F16)
        rsum = sb("rsum", [P, H])
        cat = [sb(f"cat{n}", [P, 2, P]) for n in range(2)]
        catT = sb("catT", [P, P])
        xnF = sb("xnF", [P, 4, D])
        lnF = sb("lnF", [P, GR])
        stF = sb("stF", [P, 4, 6])
        mvF = sb("mvF", [P, 4, 2])
        rsF = sb("rsF", [P, 4, 2])
        hT = sb("hT", [P, FT, GR])
        pad_row = sb("pad_row", [P, ROW])
        logit = sb("logit", [P, 4, E])
        top8 = sb("top8", [P, 4, E])
        idx8 = sb("idx8", [P, 4, E], U32)
        idxf = sb("idxf", [P, 2, 4])
        chosen = sb("chosen", [P, 2, 4, E])
        counted = sb("counted", [P, 4, E])
        prob = sb("prob", [P, 4, E])
        psum8 = sb("psum8", [P, 4])
        pw = sb("pw", [P, 4, 2])
        run = sb("run", [P, 5, E])
        spot = sb("spot", [P, 2, 4, E])
        slotf = sb("slotf", [P, 2, 4])
        slot = sb("slot", [P, 2, TILES], U32)
        tail = sb("tail", [P, E], U32)
        cnt = sb("cnt", [P, E])
        nblk = sb("nblk", [P, E])
        cumb = sb("cumb", [P, E])
        cmp8 = sb("cmp8", [P, 40, E])
        blkf = sb("blkf", [P, 2, 40])
        blk = sb("blk", [P, 2, 40], U32)
        xin = [work[:, n * (ROW + D):n * (ROW + D) + ROW] for n in range(NX)]
        xbT = [xnF[:, n, :] for n in range(2)]
        gated = [sb(f"gated{n}", [P, 4 * MC]) for n in range(2)]
        hb = [hT[:, n, :] for n in range(2)]
        hbT = [hT[:, 2 + n, :] for n in range(2)]
        yb = [work[:, n * (ROW + D) + ROW:(n + 1) * (ROW + D)] for n in range(NX)]

        psS = ctx.enter_context(nc.psum_tensor("psS", [P, 2, 512], F32))
        psT = ctx.enter_context(nc.psum_tensor("psT", [P, 2, 512], F32))
        psO = ctx.enter_context(nc.psum_tensor("psO", [P, 512], F32))
        psL = ctx.enter_context(nc.psum_tensor("psL", [P, 512], F32))
        psQ = ctx.enter_context(nc.psum_tensor("psQ", [P, 512], F32))
        psC = ctx.enter_context(nc.psum_tensor("psC", [P, 512], F32))

        rel_dram = nc.dram_tensor("rel_scratch", (H, S, P), F32).ap()
        batch_dram = nc.dram_tensor("batch_scratch", (B, D), F32).ap()

        dispatched = nc.dram_tensor("dispatched", (E * REGION + P, ROW), F32).ap()
        results = nc.dram_tensor("results", (2 * TOK, D), F32).ap()

        r_rt = sem("r_rt")
        r_e = sem("r_e")
        r_cnt = sem("r_cnt")
        r_oh = sem("r_oh")
        r_dup = sem("r_dup")
        r_top = sem("r_top")
        r_slot = sem("r_slot")
        r_sent = sem("r_sent")
        r_tab = sem("r_tab")
        r_tail = sem("r_tail")
        pad_ready = sem("pad_ready")
        pad_out = sem("pad_out")
        b_ld = [sem(f"b_ld{n}") for n in range(NX)]
        b_xt = sem("b_xt")
        b_xc = sem("b_xc")
        b_m1 = sem("b_m1")
        b_sg = sem("b_sg")
        b_hd = sem("b_hd")
        b_t2 = sem("b_t2")
        b_hc = sem("b_hc")
        b_m2 = sem("b_m2")
        b_ye = sem("b_ye")
        b_sc = [sem(f"b_sc{n}") for n in range(NX)]
        b_res = [sem(f"b_res{g}") for g in range(GROUPS)]
        ld_const = sem("ld_const")
        ld_x = sem("ld_x")
        ld_ctx = sem("ld_ctx")
        ld_a0 = sem("ld_a0")
        ld_mask = sem("ld_mask")
        ld_prep = sem("ld_prep")
        ld_moe0 = sem("ld_moe0")
        ld_moe3 = sem("ld_moe3")
        zeroed = sem("zeroed")
        setup_pe = sem("setup_pe")
        setup_ev = sem("setup_ev")
        dve_prep = sem("dve_prep")
        rel_out = sem("rel_out")
        rel_in = sem("rel_in")
        batch_out = sem("batch_out")
        batch_in = sem("batch_in")
        a_stat = sem("a_stat")
        a_rstd = sem("a_rstd")
        a_xn = sem("a_xn")
        a_lnp = sem("a_lnp")
        a_ln = sem("a_ln")
        a_xb = sem("a_xb")
        a_ctx = [sem(f"a_ctx{n}") for n in range(2)]
        a_qkp = sem("a_qkp")
        a_q = sem("a_q")
        a_km = sem("a_km")
        a_vp = sem("a_vp")
        a_v = sem("a_v")
        a_vhi = sem("a_vhi")
        a_vlo = sem("a_vlo")
        a_sc = sem("a_sc")
        a_ev = sem("a_ev")
        a_side = [sem(f"a_side{n}") for n in range(4)]
        a_sidef = sem("a_sidef")
        a_mx = sem("a_mx")
        a_sub = sem("a_sub")
        a_exp = sem("a_exp")
        a_tr = sem("a_tr")
        a_hi = sem("a_hi")
        a_lo = sem("a_lo")
        a_pv = sem("a_pv")
        a_rs = sem("a_rs")
        a_cat = sem("a_cat")
        a_ctp = sem("a_ctp")
        a_ct = sem("a_ct")
        a_out = sem("a_out")
        a_x = sem("a_x")
        f_stat = sem("f_stat")
        f_rstd = sem("f_rstd")
        f_xn = sem("f_xn")
        f_lnp = sem("f_lnp")
        f_ln = sem("f_ln")
        f_xb = sem("f_xb")
        f_bn = sem("f_bn")
        f_x = sem("f_x")
        a_bn = sem("a_bn")
        zeroed_v = sem("zeroed_v")
        cap_ready = sem("cap_ready")
        bv_ready = sem("bv_ready")
        fs = {}
        for k in ("lin1", "ffn1", "ffn2"):
            fs[k] = [sem(f"{k}_{w}") for w in (("up", "read", "hidden", "down") if k != "lin1" else ("down",))]
        fs["lin1"] = [None, None, None, fs["lin1"][0]]
        fs["ffn2"][2] = fs["ffn2"][1]
        stored = sem("stored")

        ATT = {0: 0, 2: 1, 3: 2}
        KIND = {"moe0": "moe", "lin1": "lin", "ffn1": "plain", "ffn2": "plain", "moe3": "moe"}
        FFN = {k: n for n, k in enumerate(p for p in PHASES if p in KIND)}
        F_BEFORE = {p: sum(q in KIND for q in PHASES[:n]) for n, p in enumerate(PHASES) if p in ATT}
        F_AFTER_A = {p: ATT[PHASES[n - 1]] + 1 for n, p in enumerate(PHASES) if p in KIND and PHASES[n - 1] in ATT}

        MOE = {"moe0": 0, "moe3": 1}
        CHOICES = {"moe0": 1, "moe3": 2}
        NBLOCKS = {k: -(-((CHOICES[k] * TOK + E * (P - 1)) // P) // NX) * NX for k in MOE}
        NBLOCKS["shared"] = TILES
        BLOCK0 = {"moe0": 0, "shared": NBLOCKS["moe0"], "moe3": NBLOCKS["moe0"] + TILES}
        SCATTERED = {"moe0": 0, "moe3": NBLOCKS["moe0"] // NX}
        SENT = {"moe0": 16 * TILES, "moe3": 16 * 3 * TILES}
        psH = [psO, psL]

        def tab(name):
            at, n = RT[name]
            return route_tab[:, at:at + n]

        set_ps = [psQ, psC]
        bv_twice = xnF[:, 0:2, :]

        def tr(pe, dst, src, k):
            return nc.tensor.transpose(dst, src, ident[0:k, 0:k])

        w1T_ps = w1T[:, :, :]

        def setup_jobs():
            mm = nc.tensor.matmul
            add, mul = ALU.add, ALU.mult
            jobs = []
            for q in range(4):
                def pe(ps, q=q):
                    for t in range(4):
                        r = tr(None, ps[:, t * P:(t + 1) * P], tok_in[:, (4 * q + t) * P:(4 * q + t + 1) * P], P)
                    return r
                jobs.append(([(ld_ctx, 16)], pe,
                             lambda ps, q=q: nc.vector.tensor_copy(ctxT[:, q * 512:(q + 1) * 512], ps[:, :])))

            def pe(ps):
                for h2 in range(2):
                    r = mm(ps[:, 0:D], bv_twice[0:64, h2, :], wo0[0:64, h2, :], start=(h2 == 0), stop=(h2 == 1))
                return r
            jobs.append(([(ld_a0, 16 * 9), (bv_ready, 1)], pe,
                         lambda ps: nc.vector.tensor_tensor(bias_out[:, 0, :], ps[:, 0:D], bias_out[:, 0, :], add)))

            def pe(ps):
                for n in range(4):
                    r = tr(None, ps[:, n * P:(n + 1) * P], wraw3[:, n, :], P)
                return r
            jobs.append(([(ld_prep, 16 * 24)], pe,
                         lambda ps: nc.vector.tensor_copy(w3T[:, :, :].rearrange("p a b -> p (a b)"), ps[:, :])))

            def pe(ps):
                return mm(ps[:, 0:D], bv_col[:, 0:1].broadcast_to([P, P]), w3T[:, 3, :], start=True, stop=True)
            jobs.append(([], pe,
                         lambda ps: nc.vector.tensor_tensor(bias_out[:, 1, :], ps[:, 0:D], bias_out[:, 1, :], add)))

            def pe(ps):
                for n in range(2):
                    r = tr(None, ps[:, n * P:(n + 1) * P], w1raw[:, n * P:(n + 1) * P], P)
                return r
            jobs.append(([], pe,
                         lambda ps: nc.vector.tensor_copy(w1T_ps.rearrange("p a b -> p (a b)"), ps[:, 0:2 * P])))
            jobs.append(([], lambda ps: tr(None, ps[0:32, 0:P], u1[:, :], P),
                         lambda ps: nc.vector.tensor_copy(u1T[:, :], ps[0:32, 0:P])))
            jobs.append(([], lambda ps: tr(None, ps[:, 0:E], gate3[:, :], E),
                         lambda ps: nc.vector.tensor_copy(gate3T[:, :], ps[:, 0:E])))

            def pe(ps):
                for n in range(FT):
                    r = tr(None, ps[0:32, n * P:(n + 1) * P], u2[:, n, :], P)
                return r
            jobs.append(([], pe, lambda ps: nc.vector.tensor_copy(u2T[:, :], ps[0:32, :])))

            def pe(ps):
                for n in range(FT):
                    r = tr(None, ps[0:16, n * P:(n + 1) * P], u_raw[:, n, :], P)
                return r
            jobs.append(([], pe, lambda ps: nc.vector.tensor_copy(uT[:, :], ps[0:16, :])))
            jobs.append(([], lambda ps: tr(None, ps[0:16, 0:16], fast_raw[:, :], 16),
                         lambda ps: nc.vector.tensor_copy(fastT[:, :], ps[0:16, 0:16])))
            jobs.append(([], lambda ps: mm(ps[0:16, 0:D], fastT[:, :], v_raw[:, :], start=True, stop=True),
                         lambda ps: nc.vector.tensor_copy(fast_v[:, :], ps[0:16, 0:D])))

            def pe(ps):
                for n in range(FT):
                    r = tr(None, ps[:, n * P:(n + 1) * P], tern[:, n, :], P)
                return r
            jobs.append(([(dve_prep, PREP["fc"])], pe, lambda ps: nc.vector.tensor_copy(w1eff[:, :], ps[:, :])))
            jobs.append(([], lambda ps: mm(ps[:, :], fast_v[:, :], uT[:, :], start=True, stop=True),
                         lambda ps: nc.vector.scalar_tensor_tensor(w1eff[:, :], ps[:, :], gate_col[:, 0:1], w1eff[:, :], mul, add)))

            def pe(ps):
                for n in range(FT):
                    r = tr(None, ps[:, n * P:(n + 1) * P], proj_raw[:, n * P:(n + 1) * P], P)
                return r
            jobs.append(([(dve_prep, PREP["proj"])], pe,
                         lambda ps: nc.vector.tensor_copy(w1out[:, :, :].rearrange("p a b -> p (a b)"), ps[:, :])))

            jobs.append(([], lambda ps: mm(ps[:, :], u1T[:, :], v1r[:, :], start=True, stop=True),
                         lambda ps: nc.vector.tensor_copy(w2in[:, :], ps[:, :])))

            def pe(ps):
                for n in range(FT):
                    r = mm(ps[:, n * P:(n + 1) * P], u2T[:, n * P:(n + 1) * P], v2r[:, :], start=True, stop=True)
                return r
            jobs.append(([], pe, lambda ps: nc.vector.tensor_copy(w2out[:, :, :].rearrange("p a b -> p (a b)"), ps[:, :])))
            jobs.append(([], lambda ps: mm(ps[0:H, 0:REL], rel_bias[:, :], rel_onehot[:, 0:REL], start=True, stop=True),
                         lambda ps: nc.vector.tensor_copy(rel_row[:, 0:REL], ps[0:H, 0:REL])))
            jobs.append(([(dve_prep, PREP["ctx_sum"])],
                         lambda ps: mm(ps[0:B, 0:D], ctx_sum[:, :], w1T[:, 1, :], start=True, stop=True),
                         lambda ps: nc.vector.scalar_tensor_tensor(per_batch[:, :], ps[0:B, 0:D], 1.0 / S,
                                                                   bias_out[0:B, 3, :], mul, add)))
            return jobs

        PREP = {"ctx_sum": 1, "fc": 12, "proj": 21}
        JOBS = setup_jobs()
        NJ = len(JOBS)
        J_REL, J_BATCH = NJ - 1, NJ
        J_CTX, J_OUT_BIAS, J_FC = 4, 5, 15

        def staggered(engine, nb, step):
            for s in (-2, -1, 0):
                step(s % NX, s, lo=s)
            with engine.Fori(0, nb // NX - 1) as j:
                for u in range(NX):
                    step((u + 1) % NX, NX * j + (u + 1), lo=1)
            for s in range(nb - NX + 1, nb + 1):
                step(s % NX, s, lo=1, hi=True)

        def wait_apart(engine, s, value):
            at = value if isinstance(value, int) else engine.to_reg(value)
            engine.wait_ge(ld_const, 16 * 7)
            engine.wait_ge(s, at)

        block = ctx.enter_context(nc.Block())

        @block.sync
        def _(sp):
            for t, k in ((ident, "ident"), (head_mask, "head_mask"), (dup_mask, "dup_mask"), (route_tab, "route_tab"),
                         (place_tab, "place_tab"), (before, "before")):
                sp.dma_start(t[:], K[k]).then_inc(ld_const, 16)
            sp.dma_start(rel_onehot[:, 0:REL], K["rel_onehot"]).then_inc(ld_const, 16)
            sp.dma_start(tok_in[:].rearrange("p (t d) -> p t d", t=TILES),
                         A["ctx_1024"].rearrange("(t b) s d -> (b s) t d", b=2)).then_inc(ld_ctx, 16)
            sp.dma_start(x[:].rearrange("p (t d) -> p t d", t=TILES),
                         A["x"].rearrange("(t b) s d -> (b s) t d", b=2)).then_inc(ld_x, 16)
            for b in range(2):
                sp.dma_start(mask_words[b * S:(b + 1) * S], A["mask_BxSxS2_bf1"].rearrange(
                    "(t b) q k -> b q t k", b=2)[b]).then_inc(ld_mask, 16)
                sp.dma_start(pad_words[b * S:(b + 1) * S], A["mask_BxS2_bf0"].rearrange(
                    "(t b) k -> b t k", b=2)[b].partition_broadcast(S)).then_inc(ld_mask, 16)
                sp.dma_start(amask[b * S:(b + 1) * S], A["fside_SxS2_0"]).then_inc(ld_mask, 16)
            sp.dma_start(e_up, A["L0_ffn_W1"].rearrange("e h f -> h e f")).then_inc(ld_moe0, 16)
            for e in range(E):
                sp.dma_start(e_down[:, e], A["L0_ffn_W2"][e].rearrange("(f p) h -> p f h", p=P)).then_inc(ld_moe0, 16)
            sp.wait_ge(setup_ev, J_REL)
            sp.dma_start(rel_dram[:, :, 0:REL], rel_row[:, 0:REL].unsqueeze(1).broadcast_to([H, S, REL])).then_inc(rel_out, 16)
            sp.wait_ge(rel_out, 16)
            skew = rel_dram.rearrange("h q j -> h (q j)")[:, 0:S * (P - 1)].rearrange("h (q j) -> q h j", j=P - 1)
            for b in range(2):
                sp.dma_start(bias2[b * S:(b + 1) * S], skew[:, :, S - 1:2 * S - 1]).then_inc(rel_in, 16)
            sp.wait_ge(setup_ev, J_BATCH)
            sp.dma_start(batch_dram, per_batch[:, :]).then_inc(batch_out, 16)
            sp.wait_ge(batch_out, 16)
            for b in range(2):
                sp.dma_start(tok_in[b * S:(b + 1) * S].rearrange("p (t d) -> p t d", t=TILES),
                             batch_dram.rearrange("(t b) d -> b t d", b=2)[b].partition_broadcast(S)).then_inc(batch_in, 16)

            def chunk_load(n, c, cg):
                sp.wait_ge(a_vp, cg - 1)
                for d in range(2):
                    sp.dma_start(ctxc[n][:, :, d, :], ctxT[:, ds(c * CH, CH)].rearrange("p (b s) -> p b s", b=4)).then_inc(a_ctx[n], 16)

            def side_load(n, i):
                sp.wait_ge(a_ev, 2 * (32 + i - 4 + 1))
                for b in range(2):
                    sp.dma_start(side[n][b * S:(b + 1) * S],
                                 A["fside_Bx16xSxS2_0"][ds(2 * i + b, 1)].rearrange("a h q k -> q (a h) k"))\
                      .then_inc(a_side[n], 16)

            def moe(kind):
                m = MOE[kind]
                if kind == "moe3":
                    def load_tile(n, t, k):
                        if isinstance(t, int):
                            if t % 4 == 0:
                                sp.wait_ge(f_xn, GROUPS * FFN[kind] + t // 4 + 1)
                        wait_apart(sp, b_xt, k - (NX - 1))
                        sp.dma_start(xin[n][:, 0:D], pay_row[:, ds(t * 2 * ROW, D)]).then_inc(b_ld[n], 16)
                    b0 = BLOCK0["shared"]
                    for t in range(NX):
                        if t == 0:
                            sp.wait_ge(f_xn, GROUPS * FFN[kind] + GROUPS)
                        load_tile(t, t, b0 + t)
                    with sp.Fori(1, TILES // NX) as j:
                        for n in range(NX):
                            load_tile(n, NX * j + n, NX * j + (b0 + n))
                b0, nb = BLOCK0[kind], NBLOCKS[kind]
                sp.wait_ge(r_tab, m + 1)
                sp.wait_ge(r_sent, SENT[kind])
                sp.wait_ge(r_tail, 16 * E * (m + 1))
                sp.wait_ge(pad_out, 16)
                sc0 = SCATTERED[kind]

                def load_block(n, b, first):
                    row_at = sp.value_load(blk[0:1, 0, ds(b, 1)], min_val=0, max_val=E * REGION)
                    if not (first and b0 == 0):
                        wait_apart(sp, b_xt, b + (b0 - NX + 1))
                    if not first:
                        sp.wait_ge(b_sc[n], (b - n) * (16 // NX) + 16 * sc0)
                    sp.dma_start(xin[n], dispatched[ds(row_at, P), :]).then_inc(b_ld[n], 16)
                for n in range(NX):
                    load_block(n, n, True)
                with sp.Fori(1, nb // NX) as j:
                    for n in range(NX):
                        load_block(n, NX * j + n, False)
                for n in range(NX):
                    sp.wait_ge(b_sc[n], 16 * (sc0 + nb // NX))
                for g in range(GROUPS):
                    for c in range(CHOICES[kind]):
                        sp.dma_start(pay_row[:, c * TOK + g * GR:c * TOK + (g + 1) * GR].rearrange("p (t d) -> p t d", t=4),
                                     results[c * TOK + g * GR:c * TOK + (g + 1) * GR].rearrange("(t p) d -> p t d", p=P))\
                          .then_inc(b_res[g], 16)

            sp.wait_ge(pad_ready, 1)
            sp.dma_start(dispatched[E * REGION:E * REGION + P, :], pad_row[:, :]).then_inc(pad_out, 16)

            for a in range(3):
                if a == 1 and "moe0" in FFN:
                    moe("moe0")
                    for o, i in ((m_gu[:, :, 0:MI], A["L3_ffn_wg"].rearrange("e h i -> h e i")),
                                 (m_gu[:, :, MI:2 * MI], A["L3_ffn_wu"].rearrange("e h i -> h e i")),
                                 (m_down, A["L3_ffn_wd"].rearrange("e (c p) h -> p (e c) h", p=MC)),
                                 (s_gu[:, 0, :], A["L3_ffn_swg"]), (s_gu[:, 1, :], A["L3_ffn_swu"]),
                                 (s_down, A["L3_ffn_swd"].rearrange("(c p) h -> p c h", p=MC))):
                        sp.dma_start(o, i).then_inc(ld_moe3, 16)
                for n in range(2):
                    if a == 0:
                        if n == 0:
                            sp.wait_ge(setup_ev, J_CTX)
                        for d in range(2):
                            sp.dma_start(ctxc[n][:, :, d, :], ctxT[:, n * CH:(n + 1) * CH].rearrange("p (b s) -> p b s", b=4))\
                              .then_inc(a_ctx[n], 16)
                    else:
                        chunk_load(n, n, 8 * a + n)
                if a == 2:
                    for n in range(4):
                        for b in range(2):
                            sp.dma_start(side[n][b * S:(b + 1) * S],
                                         A["fside_Bx16xSxS2_0"][2 * n + b].rearrange("h q k -> q h k")).then_inc(a_side[n], 16)
                with sp.Fori(1, 4) as j:
                    for n in range(2):
                        chunk_load(n, 2 * j + n, 2 * j + (8 * a + n))
                        if a == 2:
                            for u in range(2):
                                side_load(2 * n + u, 4 * j + (2 * n + u))

            if "moe3" in FFN:
                moe("moe3")
            sp.wait_ge(f_x, GROUPS * len(FFN))
            sp.wait_ge(a_x, 3 * TILES)
            sp.dma_start(out.rearrange("(t b) s d -> (b s) t d", b=2),
                         x[:].rearrange("p (t d) -> p t d", t=TILES)).then_inc(stored, 16)
            sp.wait_ge(stored, 16)

        mm = nc.tensor.matmul

        @block.tensor
        def _(pe):
            pe.wait_ge(ld_const, 16 * 7)
            for n, (waits, job, _) in enumerate(JOBS):
                for s, v in waits:
                    pe.wait_ge(s, v)
                if n:
                    pe.wait_ge(setup_ev, n)
                job(set_ps[n % 2]).then_inc(setup_pe, 1)

            def ln_transposes(cg):
                pe.wait_ge(a_xn, cg + 1)
                if not (isinstance(cg, int) and cg == 0):
                    pe.wait_ge(a_ln, cg)
                for t in range(2):
                    r = tr(pe, psL[:, t * P:(t + 1) * P], xnA[:, t, :], P)
                r.then_inc(a_lnp, 1)

            def project(a, n, cg):
                w = (wqk0, wqkv2, w3T)[a]
                pe.wait_ge(a_ln, cg + 1)
                pe.wait_ge(a_ctx[n], ctx_count(cg, n))
                if not (isinstance(cg, int) and cg == 0):
                    pe.wait_ge(a_q, cg)
                    if not (isinstance(cg, int) and cg == 1):
                        pe.wait_ge(a_v, cg if isinstance(cg, int) and cg % 8 == 0 else cg - 1)
                for qk in range(2):
                    toks = lnA[:, :] if qk == 0 else ctxc[n][:, :, 0, :]
                    toks = toks.rearrange("p (u b s) -> p u b s" if qk == 0 else "p (u b) s -> p u b s", u=2, b=2)
                    for half in range(2):
                        for b in range(2):
                            r = mm(psQ[b * 64:(b + 1) * 64, (2 * qk + half) * P:(2 * qk + half + 1) * P],
                                   w[:, qk, half * 64:(half + 1) * 64], toks[:, :, b, :], start=True, stop=True)
                r.then_inc(a_qkp, 1)

            def ctx_count(cg, n):
                if isinstance(cg, int):
                    return 32 * (cg // 2 + 1)
                return (cg - n) * 16 + 32

            def values(a, n, cg, more):
                w = (wqk0, wqkv2, w3T)[a]
                pe.wait_ge(a_q, cg + (2 if more else 1))
                pe.wait_ge(a_ctx[n], ctx_count(cg, n))
                for u in range(2):
                    for b in range(2):
                        tok = ctxc[n][:, 2 * u + b, :, :].rearrange("p d s -> p (d s)")
                        r = mm(psQ[:, (2 * u + b) * P:(2 * u + b + 1) * P], tok, w[:, 2, :], start=True, stop=True)
                r.then_inc(a_vp, 1)

            def scores(n, u, i, cg):
                pe.wait_ge(a_km, 2 * cg + 2)
                for half in range(2):
                    if not (isinstance(i, int) and i == 0):
                        pe.wait_ge(a_ev, 2 * i - 1 + half)
                    mm(psS[:, half, :], q_diag[n][:, half, u, :], k_heads[n][:, half, u, :, :],
                       start=True, stop=True).then_inc(a_sc, 1)

            def transposes(m, i):
                pe.wait_ge(a_exp, i + 1)
                for half in range(2):
                    if not (isinstance(i, int) and i == 0):
                        pe.wait_ge(a_lo, 2 * i - 1 + half)
                    for j in range(4):
                        g = 4 * half + j
                        r = tr(pe, psT[:, half, j * P:(j + 1) * P],
                               sc[m][:, 2 * g:2 * g + 2, :].rearrange("p h k -> p (h k)"), P)
                    r.then_inc(a_tr, 1)

            def apply_probs(n, u, i, cg):
                pe.wait_ge(a_lo, 2 * i + 2)
                pe.wait_ge(a_vlo, cg + 1)
                pe.wait_ge(a_vhi, cg + 1)
                if not (isinstance(i, int) and i == 0):
                    pe.wait_ge(a_cat, i)
                o = psO[:, 0:2 * H * 9].rearrange("p (b h e) -> p b h e", b=2, h=H)
                for j in range(8):
                    for k, (pp, vv) in enumerate(((p_hi, v_hi), (p_hi, v_lo), (p_lo, v_hi))):
                        r = mm(o[:, :, 2 * j:2 * j + 2, :], pp[:, j, :], vv[n][:, u, :, 2 * j:2 * j + 2, :],
                               start=(k == 0), stop=(k == 2))
                r.then_inc(a_pv, 1)

            def cat_transpose(m, i):
                pe.wait_ge(a_cat, i + 1)
                if not (isinstance(i, int) and i == 0):
                    pe.wait_ge(a_x, i)
                tr(pe, psC[:, 0:P], cat[m][:, 0, :], P).then_inc(a_ctp, 1)

            def project_out(a, m, i, ia):
                if a == 0:
                    pe.wait_ge(a_cat, i + 1)
                    if not (isinstance(i, int) and i == 0):
                        pe.wait_ge(a_x, i)
                    for h2 in range(2):
                        r = mm(psC[:, P:2 * P], cat[m][:, h2, :], wo0[:, h2, :], start=(h2 == 0), stop=(h2 == 1))
                else:
                    pe.wait_ge(a_ct, ia + 1)
                    r = mm(psC[:, P:2 * P], catT[:, :], wo2[:, :] if a == 1 else w3T[:, 3, :], start=True, stop=True)
                r.then_inc(a_out, 1)

            def attention(a):
                def step(u, j, first=False, more=True, live=True):
                    i = 4 * j + u + 16 * a
                    c, n = 2 * j + u // 2 + 8 * a, u // 2
                    if not (first and u < 2):
                        transposes((u - 2) % 4, i - 2)
                    if live and u % 2 == 0 and more:
                        ln_transposes(c + 1)
                    if a and not (first and u < 3):
                        cat_transpose((u - 3) % 2, i - 3)
                    if live:
                        if u % 2 == 1:
                            values(a, n, c, more)
                        scores(n, u % 2, i, c)
                    if not (first and u < 3):
                        project_out(a, (u - 3) % 2, i - 3, i - 19)
                    if live and u % 2 == 0 and more:
                        project(a, 1 - n, c + 1)
                    if not (first and u < 2):
                        apply_probs(1 - n, u % 2, i - 2, c - 1)

                ln_transposes(8 * a)
                project(a, 0, 8 * a)
                for u in range(4):
                    step(u, 0, first=True)
                with pe.Fori(1, 3) as j:
                    for u in range(4):
                        step(u, j)
                for u in range(4):
                    step(u, 3, more=(u < 2))
                for u in range(3):
                    step_tail(a, u)

            def step_tail(a, u):
                i = 16 + u + 16 * a
                if u < 2:
                    transposes((u - 2) % 4, i - 2)
                if a:
                    cat_transpose((u - 3) % 2, i - 3)
                project_out(a, (u - 3) % 2, i - 3, i - 19)
                if u < 2:
                    apply_probs(1, u % 2, i - 2, 8 * a + 7)

            def ffn_ln(G):
                pe.wait_ge(f_xn, G + 1)
                if not (isinstance(G, int) and G == 0):
                    pe.wait_ge(f_ln, G)
                for t in range(4):
                    r = tr(pe, psL[:, t * P:(t + 1) * P], xnF[:, t, :], P)
                r.then_inc(f_lnp, 1)

            def plain(kind):
                f0 = GROUPS * FFN[kind]
                win, wout = (w1eff, w1out) if kind == "ffn1" else (w2in, w2out)
                up, read, hid, y = fs[kind]

                def group(g, last):
                    pe.wait_ge(f_ln, g + (f0 + 1))
                    for f in range(FT):
                        if f >= 2 or not isinstance(g, int) or g > 0:
                            pe.wait_ge(read, g * FT + (f - 1))
                        mm(psS[:, f % 2, :], win[:, f * P:(f + 1) * P], lnF[:, :], start=True, stop=True).then_inc(up, 1)
                    if not last:
                        ffn_ln(g + (f0 + 1))
                    pe.wait_ge(hid, g * FT + FT)
                    if not (isinstance(g, int) and g == 0):
                        pe.wait_ge(f_x, g + f0)
                    for t in range(4):
                        for f in range(FT):
                            r = mm(psT[:, 0, t * P:(t + 1) * P], hT[:, f, t * P:(t + 1) * P], wout[:, f, :],
                                   start=(f == 0), stop=(f == FT - 1))
                    r.then_inc(y, 1)

                ffn_ln(f0)
                group(0, False)
                with pe.Fori(1, GROUPS - 1) as g:
                    group(g, False)
                group(GROUPS - 1, True)

            def linear():
                f0 = GROUPS * FFN["lin1"]
                y = fs["lin1"][3]

                def group(g, last):
                    pe.wait_ge(f_ln, g + (f0 + 1))
                    if not (isinstance(g, int) and g == 0):
                        pe.wait_ge(f_x, g + f0)
                    for t in range(4):
                        r = mm(psT[:, 0, t * P:(t + 1) * P], lnF[:, t * P:(t + 1) * P], w1T[:, 0, :], start=True, stop=True)
                    r.then_inc(y, 1)
                    if not last:
                        ffn_ln(g + (f0 + 1))

                ffn_ln(f0)
                group(0, False)
                with pe.Fori(1, GROUPS - 1) as g:
                    group(g, False)
                group(GROUPS - 1, True)

            def blocks(kind):
                b0, nb = BLOCK0[kind], NBLOCKS[kind]
                m = 0 if kind == "moe0" else 1
                chunks, kk = {"moe0": (FT, P), "moe3": (2, MC), "shared": (4, MC)}[kind]

                def expert(b):
                    if kind == "shared":
                        return 0
                    return pe.value_load(blk[0:1, 1, ds(b, 1)], min_val=0, max_val=E - 1)

                def since(k, sm, v):
                    if not (isinstance(k, int) and k < 0):
                        pe.wait_ge(sm, v)

                def x_transpose(q, b):
                    k = b + b0
                    pe.wait_ge(b_ld[q], (k - q) * (16 // NX) + 16)
                    since(k - 1, b_xc, k)
                    tr(pe, psQ[:, 0:P], xin[q][:, 0:D], P).then_inc(b_xt, 1)

                def up(q, b):
                    k = b + b0
                    pe.wait_ge(b_xc, k + 1)
                    since(k - 2, b_hd, k - 1)
                    if kind == "shared":
                        mm(psT[:, q % 2, 0:4 * MC], xbT[q % 2], s_gu[:, 1, :], start=True, stop=True)
                        r = mm(psS[:, q % 2, 0:4 * MC], xbT[q % 2], s_gu[:, 0, :], start=True, stop=True)
                    else:
                        w = FF if kind == "moe0" else 2 * MI
                        r = mm(psS[:, q % 2, 0:w], xbT[q % 2], expert_w[:, ds(expert(b) * w, w)], start=True, stop=True)
                    r.then_inc(b_m1, 1)

                def h_transpose(q, b):
                    k = b + b0
                    pe.wait_ge(b_hd, k + 1)
                    since(k - 2, b_hc, k - 1)
                    for f in range(chunks):
                        r = tr(pe, psH[q % 2][0:kk, f * P:(f + 1) * P], hb[q % 2][:, f * kk:(f + 1) * kk], P)
                    r.then_inc(b_t2, 1)

                def down(q, b):
                    k = b + b0
                    e = expert(b)
                    pe.wait_ge(b_hc, k + 1)
                    since(k - 1, b_ye, k)
                    for f in range(chunks):
                        if kind == "shared":
                            w = s_down[:, f, :]
                        elif kind == "moe0":
                            w = expert_w[:, ds(e * (FT * D) + (E * FF + f * D), D)]
                        else:
                            w = expert_w[0:MC, ds(e * (2 * D) + (E * 2 * MI + f * D), D)]
                        r = mm(psC[:, 0:D], hbT[q % 2][0:kk, f * P:(f + 1) * P], w, start=(f == 0), stop=(f == chunks - 1))
                    r.then_inc(b_m2, 1)

                def step(q, s, lo=-2, hi=None):
                    if hi is None or s + 2 < nb:
                        x_transpose((q + 2) % NX, s + 2)
                    if lo >= -1 and (hi is None or s + 1 < nb):
                        up((q + 1) % NX, s + 1)
                    if lo >= 0 and (hi is None or s < nb):
                        h_transpose(q, s)
                    if lo >= 1:
                        down((q - 1) % NX, s - 1)

                if kind != "shared":
                    pe.wait_ge(r_tab, m + 1)
                staggered(pe, nb, step)

            def moe(kind):
                f0, m = GROUPS * FFN[kind], MOE[kind]
                w = router0 if kind == "moe0" else gate3T
                for g in range(GROUPS):
                    G, R = f0 + g, GROUPS * m + g
                    pe.wait_ge(f_xn, G + 1)
                    if G:
                        pe.wait_ge(f_ln, G)
                    for t in range(4):
                        r = tr(pe, psL[:, t * P:(t + 1) * P], pay[:, 4 * g + t, 0, 0:D], P)
                    r.then_inc(f_lnp, 1)
                    pe.wait_ge(f_ln, G + 1)
                    for t in range(4):
                        r = mm(psO[:, t * E:(t + 1) * E], lnF[:, t * P:(t + 1) * P], w[:, :], start=True, stop=True)
                    r.then_inc(r_rt, 1)
                    pe.wait_ge(r_oh, R + 1)
                    mm(psQ[:, 0:4 * E], before[:, :], counted[:, :, :], start=True, stop=True)
                    mm(psQ[:, 4 * E:8 * E], ones[:, :], counted[:, :, :], start=True, stop=True).then_inc(r_cnt, 1)
                pe.wait_ge(r_slot, GROUPS * (m + 1))
                if kind == "moe3":
                    pe.wait_ge(ld_moe3, 16 * 6)
                    blocks("shared")
                else:
                    pe.wait_ge(ld_moe0, 16 * 9)
                blocks(kind)
                pe.wait_ge(b_ye, BLOCK0[kind] + NBLOCKS[kind])

            for ph in PHASES:
                if ph in ATT:
                    if ph:
                        pe.wait_ge(f_x, GROUPS * F_BEFORE[ph])
                    attention(ATT[ph])
                    continue
                if ph in F_AFTER_A:
                    pe.wait_ge(a_x, 16 * F_AFTER_A[ph])
                {"plain": plain, "lin": lambda k: linear(), "moe": moe}[KIND[ph]](ph)

        act = nc.scalar.activation

        @block.scalar
        def _(ac):
            loads = [(wqk0[:, 0, :], A["L0_xattn_Wq"]), (wqk0[:, 1, :], A["L0_xattn_Wk"]), (wqk0[:, 2, :], A["L0_xattn_Wv"]),
                     (wo0[0:64], A["L0_xattn_Wo"].rearrange("(h s) e -> s h e", h=2)),
                     (wo0[64:P], A["L0_xattn_Wo"].rearrange("(h s) e -> s h e", h=2)),
                     (bv_row[:], A["L0_xattn_bv"].partition_broadcast(P)),
                     (bias_out[:, 0, :], A["L0_xattn_bo"].partition_broadcast(P)),
                     (router0[:], A["L0_ffn_Wr"]), (br0[:], A["L0_ffn_br"].partition_broadcast(P))]
            assert len(loads) == 9
            for o, i in loads:
                ac.dma_start(o, i).then_inc(ld_a0, 16)
            loads = [(wraw3[:, n, :], A[f"L3_xattn_W{k}"]) for n, k in enumerate("qkvo")]
            loads += [(bias_out[:, 1, :], A["L3_xattn_bo"].partition_broadcast(P)),
                      (bias_out[:, 2, :], A["L2_ffn_b2"].partition_broadcast(P)),
                      (bias_out[:, 3, :], A["L1_xattn_b"].partition_broadcast(P)),
                      (bv_col[:], A["L3_xattn_bv"].rearrange("(p a) -> p a", a=1)),
                      (wqkv2[:, 0, :], A["L2_xattn_Wq"]),
                      (wqkv2[:, 1:3, :], A["L2_xattn_Wkv"].rearrange("p (a n) -> p a n", a=2)),
                      (wo2[:], A["L2_xattn_Wo"]), (w1raw[:], A["L1_xattn_W"]),
                      (gate3[:], A["L3_ffn_gate_w"]), (fc_raw[:], A["L1_ffn_w_fc"].rearrange("(t p) d -> p t d", p=P)),
                      (proj_raw[:], A["L1_ffn_w_proj"]), (u_raw[:], A["L1_ffn_u"].rearrange("(t p) r -> p t r", p=P)),
                      (v_raw[:], A["L1_ffn_v"]), (fast_raw[:], A["L1_ffn_fast_b"]),
                      (gate_col[:], A["L1_ffn_gate"].partition_broadcast(P)),
                      (u1[:], A["L2_ffn_U1"]), (v1r[:], A["L2_ffn_V1"]),
                      (u2[:], A["L2_ffn_U2"].rearrange("(t p) r -> p t r", p=P)), (v2r[:], A["L2_ffn_V2"]),
                      (rel_bias[:], A["L2_xattn_rel_bias"])]
            with nc.allow_non_contiguous_dma(reason="small bias vectors, a feature to a partition"):
                for n, layer in enumerate((0, 3)):
                    for t, k in ((bq, "bq"), (bk, "bk")):
                        for b in range(2):
                            ac.dma_start(t[b * 64:(b + 1) * 64, n, :],
                                         A[f"L{layer}_xattn_{k}"].rearrange("(h p) -> p h", h=2)).then_inc(ld_mask, 16)
                ac.dma_start(b1[:], A["L2_ffn_b1"].rearrange("(t p) -> p t", p=P)).then_inc(ld_mask, 16)
                for o, i in loads:
                    ac.dma_start(o, i).then_inc(ld_prep, 16)
            assert len(loads) == 24
            ac.wait_ge(ld_mask, 16 * 15)

            def ln_copy(cg):
                ac.wait_ge(a_lnp, cg + 1)
                if not (isinstance(cg, int) and cg == 0):
                    ac.wait_ge(a_qkp, cg)
                act(lnA[:, :], psL[:, 0:CH], ACT.Copy).then_inc(a_ln, 1)

            def qk_copy(a, n, cg, pair0):
                ac.wait_ge(a_qkp, cg + 1)
                if not (isinstance(cg, int) and cg < 2):
                    ac.wait_ge(a_sc, 2 * pair0 - 4)
                if not (isinstance(cg, int) and cg == 0):
                    ac.wait_ge(a_km, 2 * cg)
                q = psQ[:, 0:2 * P].rearrange("p (h u s) -> p h u s", h=2, u=2)
                k = psQ[:, 2 * P:4 * P].rearrange("p (h u s) -> p h u s", h=2, u=2)
                L = (0, None, 1)[a]
                for half in range(2):
                    for b in range(2):
                        r = slice(b * 64, b * 64 + 64)
                        act(q_diag[n][r, half, :, r], q[r, half], ACT.Identity,
                            bias=0.0 if L is None else bq[r, L, half:half + 1])
                    last = act(kT[:, half], k[:, half], ACT.Identity,
                               bias=0.0 if L is None else bk[:, L, half:half + 1])
                last.then_inc(a_q, 1)

            def v_high(n, cg, pair0):
                ac.wait_ge(a_v, cg + 1)
                if not (isinstance(cg, int) and cg < 2):
                    ac.wait_ge(a_pv, pair0 - 2)
                act(v_hi[n][:, :, :, :, 0:8].rearrange("p u b h d -> p (u b h) d"),
                    v_f32[:, :, :].rearrange("p c (h d) -> p (c h) d", d=8), ACT.Copy).then_inc(a_vhi, 1)

            def exponent(m, i):
                ac.wait_ge(a_sub, i + 1)
                act(sc[m], sc[m], ACT.Exp).then_inc(a_exp, 1)

            def p_high(i):
                for half in range(2):
                    ac.wait_ge(a_tr, 2 * i + half + 1)
                    if half == 0 and not (isinstance(i, int) and i == 0):
                        ac.wait_ge(a_pv, i)
                    act(p_hi[:, 4 * half:4 * half + 4, :].rearrange("p j t -> p (j t)"), psT[:, half, :],
                        ACT.Copy).then_inc(a_hi, 1)

            def cat_copy(i, ia):
                ac.wait_ge(a_ctp, ia + 1)
                act(catT[:, :], psC[:, 0:P], ACT.Copy).then_inc(a_ct, 1)

            def attention(a):
                def step(u, j, first=False, more=True, live=True):
                    i = 4 * j + u + 16 * a
                    c, n = 2 * j + u // 2 + 8 * a, u // 2
                    if not (first and u < 2):
                        p_high(i - 2)
                    if live and u % 2 == 0 and more:
                        ln_copy(c + 1)
                    if a and not (first and u < 3):
                        cat_copy(i - 3, i - 19)
                    if live and u % 2 == 1:
                        v_high(n, c, i - 1)
                    if not (first and u < 1):
                        exponent((u - 1) % 4, i - 1)
                    if live and u % 2 == 0 and more:
                        qk_copy(a, 1 - n, c + 1, i + 2)

                ln_copy(8 * a)
                qk_copy(a, 0, 8 * a, 16 * a)
                for u in range(4):
                    step(u, 0, first=True)
                with ac.Fori(1, 3) as j:
                    for u in range(4):
                        step(u, j)
                for u in range(4):
                    step(u, 3, more=(u < 2))
                for u in range(3):
                    i = 16 + u + 16 * a
                    if u < 2:
                        p_high(i - 2)
                    if a:
                        cat_copy(i - 3, i - 19)
                    if u < 1:
                        exponent((u - 1) % 4, i - 1)

            def ffn_ln(G, wait_read):
                ac.wait_ge(f_lnp, G + 1)
                wait_read()
                act(lnF[:, :], psL[:, :], ACT.Copy).then_inc(f_ln, 1)

            def ff_start(kind):
                f0 = GROUPS * FFN[kind]
                ffn_ln(f0, lambda: ac.wait_ge(f_x, f0) if f0 else None)

            def plain(kind):
                f0 = GROUPS * FFN[kind]
                up, read, hid, y = fs[kind]

                def group(g, last):
                    for f in range(FT):
                        ac.wait_ge(up, g * FT + (f + 1))
                        if f == 0 and not (isinstance(g, int) and g == 0):
                            ac.wait_ge(y, g)
                        if kind == "ffn1":
                            act(hT[:, f, :], psS[:, f % 2, :], ACT.Relu).then_inc(read, 1)
                        else:
                            act(hT[:, f, :], psS[:, f % 2, :], ACT.Gelu_apprx_tanh, bias=b1[:, f:f + 1]).then_inc(read, 1)
                    if not last:
                        ffn_ln(g + (f0 + 1), lambda: None)

                ff_start(kind)
                group(0, False)
                with ac.Fori(1, GROUPS - 1) as g:
                    group(g, False)
                group(GROUPS - 1, True)

            def linear():
                f0 = GROUPS * FFN["lin1"]
                y = fs["lin1"][3]
                ff_start("lin1")
                with ac.Fori(0, GROUPS - 1) as g:
                    ffn_ln(g + (f0 + 1), lambda: ac.wait_ge(y, g + 1))

            def blocks(kind):
                b0, nb = BLOCK0[kind], NBLOCKS[kind]

                def since(k, sm, v):
                    if not (isinstance(k, int) and k < 0):
                        ac.wait_ge(sm, v)

                def x_copy(q, b):
                    k = b + b0
                    ac.wait_ge(b_xt, k + 1)
                    since(k - 2, b_m1, k - 1)
                    act(xbT[q % 2], psQ[:, 0:P], ACT.Copy).then_inc(b_xc, 1)

                def activate(q, b):
                    k = b + b0
                    ac.wait_ge(b_m1, k + 1)
                    if kind == "moe0":
                        since(k - 2, b_t2, k - 1)
                        act(hb[q % 2], psS[:, q % 2, :], ACT.Gelu).then_inc(b_hd, 1)
                    else:
                        n = 4 * MC if kind == "shared" else MI
                        since(k - 2, b_hd, k - 1)
                        act(gated[q % 2][:, 0:n], psS[:, q % 2, 0:n], ACT.Silu).then_inc(b_sg, 1)

                def h_copy(q, b):
                    k = b + b0
                    ac.wait_ge(b_t2, k + 1)
                    since(k - 2, b_m2, k - 1)
                    n = (4 if kind == "shared" else 2) * P
                    act(hbT[q % 2][0:MC, 0:n], psH[q % 2][0:MC, 0:n], ACT.Copy).then_inc(b_hc, 1)

                def step(q, s, lo=-2, hi=None):
                    if hi is None or s + 2 < nb:
                        x_copy((q + 2) % NX, s + 2)
                    if lo >= -1 and (hi is None or s + 1 < nb):
                        activate((q + 1) % NX, s + 1)
                    if lo >= 0 and kind != "moe0" and (hi is None or s < nb):
                        h_copy(q, s)

                staggered(ac, nb, step)

            def moe(kind):
                f0, m = GROUPS * FFN[kind], MOE[kind]
                for g in range(GROUPS):
                    G, R = f0 + g, GROUPS * m + g
                    if kind == "moe3":
                        ac.wait_ge(f_xn, G + 1)
                        act(pay[:, 4 * g:4 * g + 4, 1, 0:D], pay[:, 4 * g:4 * g + 4, 0, 0:D], ACT.Copy).then_inc(r_dup, 1)
                    ac.wait_ge(f_lnp, G + 1)
                    if g == 0:
                        if f0:
                            ac.wait_ge(f_x, f0)
                    else:
                        ac.wait_ge(r_rt, R)
                    act(lnF[:, :], psL[:, :], ACT.Copy).then_inc(f_ln, 1)
                    ac.wait_ge(r_top, R + 1)
                    if kind == "moe0":
                        act(psum8[:, :], top8[:, :, 0], ACT.Exp, scale=-1.0).then_inc(r_e, 1)
                    else:
                        act(prob[:, :, :], prob[:, :, :], ACT.Exp).then_inc(r_e, 1)
                if kind == "moe3":
                    blocks("shared")
                blocks(kind)

            for ph in PHASES:
                if ph in ATT:
                    attention(ATT[ph])
                else:
                    {"plain": plain, "lin": lambda k: linear(), "moe": moe}[KIND[ph]](ph)

        @block.gpsimd
        def _(pool):
            nc.gpsimd.memset(minus_half[:], -0.5).then_inc(zeroed, 1)
            pool.wait_ge(zeroed, 1)
            pool.wait_ge(ld_const, 16 * 7)

            def ln_rstd(stat, done, mv, rs, k, nt):
                wait_apart(pool, stat, k + 1)
                nc.gpsimd.tensor_scalar(rs[:, 0:nt, 0], mv[:, 0:nt, 1], EPS, 1.0, ALU.add, ALU.mult).then_inc(done, 1)
                pool.wait_ge(done, 2 * k + 1)
                nc.gpsimd.tensor_tensor(rs[:, 0:nt, 1], rs[:, 0:nt, 0], minus_half[:, 0:nt], ALU.pow).then_inc(done, 1)

            def subtract(m, i):
                pool.wait_ge(a_mx, i + 1)
                nc.gpsimd.tensor_tensor(sc[m], sc[m],
                                        mx[m][:, :].unsqueeze(2).broadcast_to([P, H, S]), ALU.subtract).then_inc(a_sub, 1)

            def key_heads(n, cg, pair0, part):
                if part == 0:
                    pool.wait_ge(a_q, cg + 1)
                    if not (isinstance(cg, int) and cg < 2):
                        wait_apart(pool, a_sc, 2 * pair0 - 4)
                for r in range(4 * part, 4 * part + 4):
                    last = nc.gpsimd.tensor_scalar(k_heads[n][:, :, :, r, :].rearrange("p h u s -> p (h u) s"),
                                                   kT[:, :, :, :].rearrange("p h u s -> p (h u) s"),
                                                   head_mask[:, r:r + 1], 1.0, ALU.mult, ALU.mult)
                last.then_inc(a_km, 1)

            def add_bias(c, cg, a):
                pool.wait_ge(a_xn, cg + 1)
                xs = x[:, ds(c * CH, CH)].rearrange("p (t d) -> p t d", t=2)
                nc.gpsimd.tensor_tensor(xs, xs, bias_out[:, a // 2, :].unsqueeze(1).broadcast_to([P, 2, D]), ALU.add).then_inc(a_xb, 1)

            def attention(a):
                def ln(c, cg):
                    ln_rstd(a_stat, a_rstd, mvA, rsA, cg, 2)
                    if a != 1:
                        add_bias(c, cg, a)

                def step(u, j, more=True):
                    i = 4 * j + u + 16 * a
                    c, n = 2 * j + u // 2, u // 2
                    if u % 2 == 1 and more:
                        key_heads(1 - n, c + (8 * a + 1), i + 1, 1)
                    subtract(u, i)
                    if u % 2 == 0 and more:
                        key_heads(1 - n, c + (8 * a + 1), i + 2, 0)
                    if u % 2 == 1 and more is True:
                        ln(c + 2, c + (8 * a + 2))

                if a == 0:
                    pool.wait_ge(setup_ev, J_OUT_BIAS)
                ln(0, 8 * a)
                key_heads(0, 8 * a, 16 * a, 0)
                key_heads(0, 8 * a, 16 * a, 1)
                ln(1, 8 * a + 1)
                with pool.Fori(0, 3) as j:
                    for u in range(4):
                        step(u, j)
                for u in range(4):
                    step(u, 3, more="no ln" if u < 2 else False)

            def ffn_ln(g, G, bias):
                ln_rstd(f_stat, f_rstd, mvF, rsF, G, 4)
                if bias is not None:
                    pool.wait_ge(f_xn, G + 1)
                    xs = x[:, ds(g * GR, GR)]
                    if bias == "lin1":
                        nc.gpsimd.tensor_tensor(xs, xs, tok_in[:, ds(g * GR, GR)], ALU.add).then_inc(f_xb, 1)
                    else:
                        xs = xs.rearrange("p (t d) -> p t d", t=4)
                        nc.gpsimd.tensor_tensor(xs, xs, bias_out[:, 2, :].unsqueeze(1).broadcast_to([P, 4, D]), ALU.add).then_inc(f_xb, 1)

            def plain(kind):
                f0 = GROUPS * FFN[kind]
                if kind == "lin1":
                    pool.wait_ge(batch_in, 32)
                with pool.Fori(0, GROUPS) as g:
                    ffn_ln(g, g + f0, None if kind == "ffn1" else kind)

            def scatter(dst, places, src, s, limit):
                nc.gpsimd.indirect_dma_start(dst, bass.IndirectOffsetOnAxis(ap=places, axis=0), src, None,
                                             bounds_check=limit, oob_is_err=False).then_inc(s, 16)

            def moe(kind):
                f0, m = GROUPS * FFN[kind], MOE[kind]
                for g in range(GROUPS):
                    ln_rstd(f_stat, f_rstd, mvF, rsF, f0 + g, 4)
                    if g:
                        send(kind, m, g - 1)
                send(kind, m, GROUPS - 1)
                pool.wait_ge(r_tab, m + 1)
                pool.wait_ge(pad_ready, 1)
                for e in range(E):
                    scatter(dispatched, tail[:, e:e + 1], pad_row[:, :], r_tail, E * REGION - 1)
                b0, nb = BLOCK0[kind], NBLOCKS[kind]
                with pool.Fori(0, nb // NX) as j:
                    for n in range(NX):
                        wait_apart(pool, b_ye, NX * j + (b0 + n + 1))
                        scatter(results, xin[n][:, D + 1:D + 2].bitcast(U32), yb[n], b_sc[n], 2 * TOK - 1)

            def send(kind, m, g):
                pool.wait_ge(r_slot, GROUPS * m + g + 1)
                if kind == "moe3":
                    pool.wait_ge(r_dup, g + 1)
                for t in range(4 * g, 4 * g + 4):
                    for c in range(CHOICES[kind]):
                        scatter(dispatched, slot[:, c, t:t + 1], pay[:, t, c, :], r_sent, E * REGION - 1)

            for ph in PHASES:
                if ph in ATT:
                    attention(ATT[ph])
                else:
                    {"plain": plain, "lin": plain, "moe": moe}[KIND[ph]](ph)

        tt, ts_, stt = nc.vector.tensor_tensor, nc.vector.tensor_scalar, nc.vector.scalar_tensor_tensor

        @block.vector
        def _(v):
            nc.vector.memset(ones[:], 1.0)
            nc.vector.memset(pad_row[:], 0.0)
            for n in range(2):
                nc.vector.memset(q_diag[n][:], 0.0)
                nc.vector.memset(cat[n][:], 0.0)
                nc.vector.memset(v_hi[n][:], 0.0)
                nc.vector.memset(v_lo[n][:], 0.0).then_inc(zeroed_v, 1)
            v.wait_ge(zeroed_v, 2)
            v.wait_ge(ld_const, 16 * 7)
            for n in range(2):
                nc.vector.tensor_copy(v_hi[n][:, :, :, :, 8].rearrange("p u b h -> p (u b) h"),
                                      dup_mask[:, 0:P:8].unsqueeze(1).broadcast_to([P, 4, H])).then_inc(zeroed_v, 1)
            nc.vector.tensor_copy(pad_row[:, D + 1:D + 2].bitcast(U32), place_tab[:, 2 * TILES:2 * TILES + 1]).then_inc(pad_ready, 1)
            for c in range(2):
                nc.vector.tensor_copy(pay[:, :, c, D + 1].bitcast(U32), place_tab[:, c * TILES:(c + 1) * TILES])
            v.wait_ge(ld_mask, 16 * 15)
            v.wait_ge(ld_x, 16)

            def own(ins):
                chain[0] += 1
                ins.then_inc(dve_prep, 1)
                v.wait_ge(dve_prep, chain[0])
            chain = [0]
            m8 = mask_words[:, :, :].rearrange("p t k -> p (t k)").bitcast(U8)
            ts_(cap0[:, :], m8, 3.0e38, NEG, ALU.mult, ALU.add).then_inc(cap_ready, 1)

            v.wait_ge(ld_a0, 16 * 9)
            nc.vector.tensor_copy(bv_twice.rearrange("p h (b s) -> p h b s", b=2),
                                  bv_row[:, :].rearrange("p (s h) -> p h s", h=2).unsqueeze(2).broadcast_to([P, 2, 2, 64]))\
              .then_inc(bv_ready, 1)

            def job_range(a, b):
                for n in range(a, b):
                    v.wait_ge(setup_pe, n + 1)
                    JOBS[n][2](set_ps[n % 2]).then_inc(setup_ev, 1)
            job_range(0, J_OUT_BIAS)
            own(nc.vector.reduce_sum(ctx_sum[:, :], ctxT[:, :].rearrange("p (b s) -> p b s", b=B), axis=AX_X))
            assert chain[0] == PREP["ctx_sum"]
            p8 = pad_words[:, :, :].rearrange("p t k -> p (t k)").bitcast(U8)
            own(ts_(add3[:, :], p8, -3.0e38, 1.0e38, ALU.mult, ALU.mult))
            a3 = add3[:, :].rearrange("p (t k) -> p t k", t=TILES)
            own(tt(a3, a3, amask[:, :].unsqueeze(1).broadcast_to([P, TILES, S]), ALU.add))
            v.wait_ge(ld_prep, 16 * 24)

            def bitlinear(w, s, n, width):
                w3 = w.rearrange("p (n d) -> p n d", n=n)
                own(nc.vector.tensor_reduce(s[:, 0:n], w3, axis=AX_X, op=ALU.add, apply_absolute_value=True))
                own(ts_(s[:, 0:n], s[:, 0:n], 1.0 / width, 1e-5, ALU.mult, ALU.max))
                own(ts_(s[:, 4:4 + n], s[:, 0:n], 0.5, None, ALU.mult))
                half = s[:, 4:4 + n].unsqueeze(2).broadcast_to([P, n, width])
                t3 = tern[:, :, :].rearrange("p a b -> p (a b)").rearrange("p (n d) -> p n d", n=n)
                c3 = hT[:, 0, :].rearrange("p (n d) -> p n d", n=n)
                own(tt(t3, w3, half, ALU.is_gt))
                own(stt(c3, w3, -1.0, half, ALU.mult, ALU.is_gt))
                own(tt(t3, t3, c3, ALU.subtract))
                own(tt(t3, t3, w3, ALU.subtract))
                own(tt(t3, t3, w3, ALU.add))
                return t3, s[:, 0:n].unsqueeze(2).broadcast_to([P, n, width])

            t3, scl = bitlinear(fc_raw[:, :, :].rearrange("p a b -> p (a b)"), row_scale, FT, P)
            own(tt(t3, t3, scl, ALU.mult))
            PREP["fc"] = chain[0]
            job_range(J_OUT_BIAS, J_FC + 1)
            t3, scl = bitlinear(proj_raw[:, :], row_scale, 1, FF)
            own(tt(proj_raw[:, :], t3[:, 0, :], row_scale[:, 0:1].broadcast_to([P, FF]), ALU.mult))
            PREP["proj"] = chain[0]
            job_range(J_FC + 1, NJ)

            def stats(xs, nt, st, mv, stat, k, busy):
                for t in range(nt):
                    last = nc.vector.bn_stats(st[:, t, :], xs(t))
                last.then_inc(stat[0], 1)
                busy()
                wait_apart(v, stat[0], k + 1)
                for t in range(nt):
                    last = nc.vector.bn_aggr(mv[:, t, :], st[:, t, :])
                last.then_inc(stat[1], 1)

            def normalise(xs, nt, xn, mv, rs, rstd, k, done):
                v.wait_ge(rstd, 2 * k + 2)
                for t in range(nt):
                    last = ts_(xn[:, t, :], xs(t), mv[:, t, 0:1], rs[:, t, 1:2], ALU.subtract, ALU.mult)
                last.then_inc(done, 1)

            def a_stats(c, cg):
                stats(lambda t: x[:, ds(c * CH + t * D, D)], 2, stA, mvA, (a_bn, a_stat), cg,
                      lambda: None if isinstance(cg, int) and cg == 0 else v.wait_ge(a_xn, cg))

            def a_normalise(c, cg):
                if not (isinstance(cg, int) and cg == 0):
                    v.wait_ge(a_lnp, cg)
                normalise(lambda t: x[:, ds(c * CH + t * D, D)], 2, xnA, mvA, rsA, a_rstd, cg, a_xn)

            def evacuate(a, m, i, ii):
                if not (isinstance(i, int) and i < 4):
                    v.wait_ge(a_tr, 2 * i - 6)
                if a == 2:
                    v.wait_ge(a_side[m], 32 * (i - 32 - m) // 4 + 32 if isinstance(i, int) else (i - (32 + m)) * 8 + 32)
                    stt(side[m], side[m], 2.0,
                        add3[:, ds(ii * S, S)].unsqueeze(1).broadcast_to([P, H, S]), ALU.mult, ALU.add).then_inc(a_sidef, 1)
                    v.wait_ge(a_sidef, i - 31)
                for half in range(2):
                    v.wait_ge(a_sc, 2 * i + half + 1)
                    o = sc[m][:, 8 * half:8 * half + 8, :]
                    s = psS[:, half, :].rearrange("p (h k) -> p h k", h=8)
                    if a == 0:
                        r = stt(o, s, QK_SCALE, cap0[:, ds(ii * S, S)].unsqueeze(1).broadcast_to([P, 8, S]), ALU.mult, ALU.min)
                    elif a == 1:
                        r = tt(o, s, bias2[:, 8 * half:8 * half + 8, :], ALU.add)
                    else:
                        r = stt(o, s, QK_SCALE, side[m][:, 8 * half:8 * half + 8, :], ALU.mult, ALU.add)
                    r.then_inc(a_ev, 1)
                v.wait_ge(a_ev, 2 * i + 2)
                if not (isinstance(i, int) and i < 4):
                    v.wait_ge(a_sub, i - 3)
                nc.vector.reduce_max(mx[m][:, :], sc[m], axis=AX_X).then_inc(a_mx, 1)

            def values(n, cg):
                v.wait_ge(a_vp, cg + 1)
                if not (isinstance(cg, int) and cg == 0):
                    v.wait_ge(a_vhi, cg)
                tt(v_f32[:, :, :], psQ[:, :].rearrange("p (c d) -> p c d", c=4),
                   dup_mask[:, :].unsqueeze(1).broadcast_to([P, 4, D]), ALU.mult).then_inc(a_v, 1)

            def v_low(n, cg, pair0):
                v.wait_ge(a_vhi, cg + 1)
                if not (isinstance(cg, int) and cg < 2):
                    v.wait_ge(a_pv, pair0 - 2)
                tt(v_lo[n][:, :, :, :, 0:8].rearrange("p u b h d -> p (u b h) d"),
                   v_f32[:, :, :].rearrange("p c (h d) -> p (c h) d", d=8),
                   v_hi[n][:, :, :, :, 0:8].rearrange("p u b h d -> p (u b h) d"), ALU.subtract).then_inc(a_vlo, 1)

            def p_low(i):
                for half in range(2):
                    v.wait_ge(a_hi, 2 * i + half + 1)
                    if half == 0 and not (isinstance(i, int) and i == 0):
                        v.wait_ge(a_pv, i)
                    r = slice(4 * half, 4 * half + 4)
                    tt(p_lo[:, r, :].rearrange("p j t -> p (j t)"), psT[:, half, :],
                       p_hi[:, r, :].rearrange("p j t -> p (j t)"), ALU.subtract).then_inc(a_lo, 1)

            def concat(a, m, i, ia):
                v.wait_ge(a_pv, i + 1)
                if not (isinstance(i, int) and i < 2):
                    v.wait_ge(a_out, i - 1)
                o = psO[:, 0:2 * H * 9].rearrange("p (b h e) -> p b h e", b=2, h=H)
                for b in range(2):
                    r = slice(b * 64, b * 64 + 64)
                    last = nc.vector.reciprocal(rsum[r, :], o[r, b, :, 8])
                last.then_inc(a_rs, 1)
                v.wait_ge(a_rs, i + 1)
                for b in range(2):
                    r = slice(b * 64, b * 64 + 64)
                    if a == 0:
                        dst = cat[m][r, :, r].rearrange("p h2 (h d2) -> p h d2 h2", h=H)
                        src = o[r, b, :, 0:8].rearrange("p h (d2 h2) -> p h d2 h2", h2=2)
                        rr = rsum[r, :].unsqueeze(2).unsqueeze(3).broadcast_to([64, H, 4, 2])
                    else:
                        dst = cat[m][r, 0, :].rearrange("p (h d) -> p h d", h=H)
                        src = o[r, b, :, 0:8]
                        rr = rsum[r, :].unsqueeze(2).broadcast_to([64, H, 8])
                    last = tt(dst, src, rr, ALU.mult)
                last.then_inc(a_cat, 1)

            def residual(a, i, ii, cg):
                v.wait_ge(a_out, i + 1)
                if a != 1:
                    v.wait_ge(a_xb, cg + (1 if a == 0 else -7))
                xs = x[:, ds(ii * D, D)]
                tt(xs, xs, psC[:, P:2 * P], ALU.add).then_inc(a_x, 1)

            def attention(a):
                def step(u, j, first=False, more=True, live=True):
                    ii = 4 * j + u
                    i = ii + 16 * a
                    c, n = 2 * j + u // 2, u // 2
                    cg = c + 8 * a
                    if not (first and u < 2):
                        p_low(i - 2)
                    if live:
                        evacuate(a, u, i, ii)
                    if not (first and u < 3):
                        residual(a, i - 3, ii - 3, cg - 2 + u % 2)
                    if live and u % 2 == 1:
                        values(n, cg)
                        if more:
                            wait_x(c + 2)
                            a_stats(c + 2, cg + 2)
                    if not (first and u < 2):
                        concat(a, u % 2, i - 2, None)
                    if live and u % 2 == 1:
                        v_low(n, cg, i - 1)
                        if more:
                            a_normalise(c + 2, cg + 2)

                def wait_x(c):
                    if a:
                        f = GROUPS * (F_BEFORE[(0, 2, 3)[a]] - 1)
                        v.wait_ge(f_x, c // 2 + f + 1 if isinstance(c, int) else FXJ[0] + (f + 2))

                if a == 0:
                    v.wait_ge(cap_ready, 1)
                if a == 1:
                    v.wait_ge(rel_in, 32)
                for c in range(2):
                    if a:
                        v.wait_ge(f_x, GROUPS * (F_BEFORE[(0, 2, 3)[a]] - 1) + 1)
                    a_stats(c, 8 * a + c)
                    a_normalise(c, 8 * a + c)
                for u in range(4):
                    step(u, 0, first=True)
                with v.Fori(1, 3) as j:
                    FXJ[0] = j
                    for u in range(4):
                        step(u, j)
                for u in range(4):
                    step(u, 3, more=False)
                for u in range(3):
                    step(u, 4, live=False) if u < 2 else residual(a, 15 + 16 * a, 15, 8 * a + 7)

            FXJ = [0]

            def x_tile(g):
                return lambda t: x[:, ds(g * GR + t * D, D)]

            def f_stats(g, G, prev):
                prev(g)
                stats(x_tile(g), 4, stF, mvF, (f_bn, f_stat), G,
                      lambda: None if isinstance(G, int) and G == 0 else v.wait_ge(f_xn, G))

            def f_normalise(g, G):
                if not (isinstance(G, int) and G == 0):
                    v.wait_ge(f_lnp, G)
                normalise(x_tile(g), 4, xnF, mvF, rsF, f_rstd, G, f_xn)

            def before_phase(kind):
                if kind in F_AFTER_A:
                    k = 16 * (F_AFTER_A[kind] - 1)
                    return lambda g: v.wait_ge(a_x, g * 4 + (k + 4))
                k = GROUPS * (FFN[kind] - 1)
                return lambda g: v.wait_ge(f_x, g + (k + 1))

            def plain(kind):
                f0 = GROUPS * FFN[kind]
                _, read, hid, y = fs[kind]
                prev = before_phase(kind)

                def group(g, last):
                    if not last:
                        f_stats(g + 1, g + (f0 + 1), prev)
                    for f in range(FT):
                        if kind == "ffn1":
                            v.wait_ge(read, g * FT + (f + 1))
                            tt(hT[:, f, :], hT[:, f, :], hT[:, f, :], ALU.mult).then_inc(hid, 1)
                        if f == 1 and not last:
                            f_normalise(g + 1, g + (f0 + 1))
                    v.wait_ge(y, g + 1)
                    if kind != "ffn1":
                        v.wait_ge(f_xb, g + (GROUPS * (kind == "ffn2") + 1))
                    xs = x[:, ds(g * GR, GR)]
                    tt(xs, xs, psT[:, 0, :], ALU.add).then_inc(f_x, 1)

                f_stats(0, f0, prev)
                f_normalise(0, f0)
                with v.Fori(0, GROUPS - 1) as g:
                    group(g, False)
                group(GROUPS - 1, True)

            def route(kind, g, R):
                n = CHOICES[kind]
                v.wait_ge(r_rt, R + 1)
                lg = psO[:, 0:4 * E].rearrange("p (t e) -> p t e", t=4)
                if kind == "moe0":
                    own(tt(logit[:, :, :], lg, br0[:, :].unsqueeze(1).broadcast_to([P, 4, E]), ALU.add))
                    own(ts_(logit[:, :, :], logit[:, :, :], SATURATED, None, ALU.min))
                else:
                    own(nc.vector.tensor_copy(logit[:, :, :], lg))
                for t in range(4):
                    last = nc.vector.max(top8[:, t, :], logit[:, t, :])
                if kind == "moe0":
                    last.then_inc(r_top, 1)
                    v.wait_ge(r_top, R + 1)
                else:
                    own(last)
                    tt(prob[:, :, :], top8[:, :, :], top8[:, :, 0:1].broadcast_to([P, 4, E]), ALU.subtract).then_inc(r_top, 1)
                for t in range(4):
                    last = nc.vector.max_index(idx8[:, t, :], top8[:, t, :], logit[:, t, :])
                own(last)
                own(nc.vector.tensor_copy(idxf[:, 0:n, :].rearrange("p c t -> p t c"), idx8[:, :, 0:n]))
                for c in range(n):
                    last = tt(chosen[:, c, :, :], tab("iota").unsqueeze(1).broadcast_to([P, 4, E]),
                              idxf[:, c, :].unsqueeze(2).broadcast_to([P, 4, E]), ALU.is_equal)
                own(last)
                if n == 2:
                    tt(counted[:, :, :], chosen[:, 0], chosen[:, 1], ALU.add).then_inc(r_oh, 1)
                else:
                    nc.vector.tensor_copy(counted[:, :, :], chosen[:, 0]).then_inc(r_oh, 1)
                v.wait_ge(r_e, R + 1)
                if kind == "moe0":
                    own(ts_(psum8[:, :], psum8[:, :], 1.0, None, ALU.add))
                    own(nc.vector.reciprocal(pay[:, 4 * g:4 * g + 4, 0, D], psum8[:, :]))
                else:
                    own(nc.vector.reduce_sum(psum8[:, :], prob[:, :, :], axis=AX_X))
                    own(nc.vector.reciprocal(psum8[:, :], psum8[:, :]))
                    own(tt(pw[:, :, :], prob[:, :, 0:2], psum8[:, :].unsqueeze(2).broadcast_to([P, 4, 2]), ALU.mult))
                    own(nc.vector.reduce_sum(psum8[:, :], pw[:, :, :], axis=AX_X))
                    own(ts_(psum8[:, :], psum8[:, :], 1e-20, None, ALU.add))
                    own(nc.vector.reciprocal(psum8[:, :], psum8[:, :]))
                    own(tt(pay[:, 4 * g:4 * g + 4, :, D], pw[:, :, :], psum8[:, :].unsqueeze(2).broadcast_to([P, 4, 2]), ALU.mult))
                if g == 0:
                    own(nc.vector.tensor_copy(run[:, 0, :], tab("base")))
                else:
                    own(nc.vector.tensor_copy(run[:, 0, :], run[:, 4, :]))
                v.wait_ge(r_cnt, R + 1)
                for t in range(4):
                    own(tt(run[:, t + 1, :], run[:, t, :], psQ[:, (4 + t) * E:(5 + t) * E], ALU.add))
                own(tt(counted[:, :, :], psQ[:, 0:4 * E].rearrange("p (t e) -> p t e", t=4), run[:, 0:4, :], ALU.add))
                for c in range(n):
                    last = tt(spot[:, c], chosen[:, c], counted[:, :, :], ALU.mult)
                own(last)
                own(nc.vector.reduce_sum(slotf[:, 0:n, :], spot[:, 0:n], axis=AX_X))
                nc.vector.tensor_copy(slot[:, 0:n, 4 * g:4 * g + 4], slotf[:, 0:n, :]).then_inc(r_slot, 1)

            def block_table(kind, m):
                nb = NBLOCKS[kind]
                own(tt(cnt[:, :], run[:, 4, :], tab("base"), ALU.subtract))
                own(tt(cmp8[:, 0:TILES, :], cnt[:, :].unsqueeze(1).broadcast_to([P, TILES, E]),
                       tab("k128").unsqueeze(2).broadcast_to([P, TILES, E]), ALU.is_gt))
                own(nc.vector.reduce_sum(nblk[:, :], cmp8[:, 0:TILES, :].rearrange("p k e -> p e k"), axis=AX_X))
                own(tt(cmp8[:, 0:E, :], nblk[:, :].unsqueeze(1).broadcast_to([P, E, E]),
                       tab("le").rearrange("p (e f) -> p e f", e=E), ALU.mult))
                own(nc.vector.reduce_sum(cumb[:, :], cmp8[:, 0:E, :], axis=AX_X))
                own(tt(cmp8[:, 0:nb, :], cumb[:, :].unsqueeze(1).broadcast_to([P, nb, E]),
                       tab("k")[:, 0:nb].unsqueeze(2).broadcast_to([P, nb, E]), ALU.is_le))
                own(nc.vector.reduce_sum(blkf[:, 1, 0:nb], cmp8[:, 0:nb, :], axis=AX_X))
                own(tt(cmp8[:, 0:nb, :], cmp8[:, 0:nb, :], nblk[:, :].unsqueeze(1).broadcast_to([P, nb, E]), ALU.mult))
                own(nc.vector.reduce_sum(blkf[:, 0, 0:nb], cmp8[:, 0:nb, :], axis=AX_X))
                own(tt(blkf[:, 0, 0:nb], tab("k")[:, 0:nb], blkf[:, 0, 0:nb], ALU.subtract))
                own(ts_(blkf[:, 0, 0:nb], blkf[:, 0, 0:nb], float(P), None, ALU.mult))
                own(stt(blkf[:, 0, 0:nb], blkf[:, 1, 0:nb], float(REGION), blkf[:, 0, 0:nb], ALU.mult, ALU.add))
                own(ts_(blkf[:, 0, 0:nb], blkf[:, 0, 0:nb], float(E * REGION), None, ALU.min))
                own(ts_(blkf[:, 1, 0:nb], blkf[:, 1, 0:nb], float(E - 1), None, ALU.min))
                own(ts_(run[:, 4, :], run[:, 4, :], tab("part"), None, ALU.add))
                nc.vector.tensor_copy(tail[:, :], run[:, 4, :])
                nc.vector.tensor_copy(blk[:, :, 0:nb], blkf[:, :, 0:nb]).then_inc(r_tab, 1)

            def blocks(kind):
                b0, nb = BLOCK0[kind], NBLOCKS[kind]

                def since(k, sm, val):
                    if not (isinstance(k, int) and k < 0):
                        v.wait_ge(sm, val)

                def h_copy(q, b):
                    k = b + b0
                    v.wait_ge(b_t2, k + 1)
                    since(k - 2, b_m2, k - 1)
                    nc.vector.tensor_copy(hbT[q % 2], psH[q % 2][:, :]).then_inc(b_hc, 1)

                def gate(q, b):
                    k = b + b0
                    v.wait_ge(b_sg, k + (1 - BLOCK0["shared"]))
                    since(k - 2, b_t2, k - 1)
                    n = 4 * MC if kind == "shared" else MI
                    up = psT[:, q % 2, 0:n] if kind == "shared" else psS[:, q % 2, MI:2 * MI]
                    tt(hb[q % 2][:, 0:n], gated[q % 2][:, 0:n], up, ALU.mult).then_inc(b_hd, 1)

                def result(q, b):
                    k = b + b0
                    v.wait_ge(b_m2, k + 1)
                    if kind == "shared":
                        xs = x[:, ds(b * D, D)]
                        tt(xs, xs, psC[:, 0:D], ALU.add).then_inc(b_ye, 1)
                    else:
                        ts_(yb[q], psC[:, 0:D], xin[q][:, D:D + 1], None, ALU.mult).then_inc(b_ye, 1)

                def step(q, s, lo=-2, hi=None):
                    if kind == "moe0" and lo >= 0 and (hi is None or s < nb):
                        h_copy(q, s)
                    if kind != "moe0" and lo >= -1 and (hi is None or s + 1 < nb):
                        gate((q + 1) % NX, s + 1)
                    if lo >= 1:
                        result((q - 1) % NX, s - 1)

                staggered(v, nb, step)

            def moe(kind):
                f0, m = GROUPS * FFN[kind], MOE[kind]
                prev = before_phase(kind)

                def normal(g):
                    G = f0 + g
                    f_stats(g, G, prev)
                    v.wait_ge(f_rstd, 2 * G + 2)
                    if m and g == 0:
                        v.wait_ge(f_x, GROUPS)
                    xs = x_tile(g)
                    for t in range(4):
                        last = ts_(pay[:, 4 * g + t, 0, 0:D], xs(t), mvF[:, t, 0:1], rsF[:, t, 1:2], ALU.subtract, ALU.mult)
                    last.then_inc(f_xn, 1)

                if m:
                    v.wait_ge(f_x, GROUPS)
                    for c in range(2):
                        last = nc.vector.tensor_copy(pay[:, :, c, D + 1].bitcast(U32), place_tab[:, c * TILES:(c + 1) * TILES])
                    own(last)
                normal(0)
                for g in range(GROUPS):
                    if g + 1 < GROUPS:
                        normal(g + 1)
                    route(kind, g, GROUPS * m + g)
                block_table(kind, m)
                if kind == "moe3":
                    blocks("shared")
                blocks(kind)
                for g in range(GROUPS):
                    n = CHOICES[kind]
                    v.wait_ge(b_res[g], 16 * (1 if kind == "moe0" else 1 + n))
                    xs = x[:, g * GR:(g + 1) * GR]
                    if n == 2:
                        own(tt(xs, xs, pay_row[:, TOK + g * GR:TOK + (g + 1) * GR], ALU.add))
                    tt(xs, xs, pay_row[:, g * GR:(g + 1) * GR], ALU.add).then_inc(f_x, 1)


            for ph in PHASES:
                if ph in ATT:
                    attention(ATT[ph])
                else:
                    {"plain": plain, "lin": plain, "moe": moe}[KIND[ph]](ph)


_INS = ['x', 'ctx_1024', 'fside_Bx16xSxS2_0', 'fside_SxS2_0', 'mask_BxSxS2_bf1', 'mask_BxS2_bf0',
        'L0_xattn_Wq', 'L0_xattn_bq', 'L0_xattn_Wk', 'L0_xattn_bk', 'L0_xattn_Wv', 'L0_xattn_bv', 'L0_xattn_Wo',
        'L0_xattn_bo', 'L0_ffn_Wr', 'L0_ffn_br', 'L0_ffn_W1', 'L0_ffn_W2', 'L1_xattn_W', 'L1_xattn_b',
        'L1_ffn_fast_b', 'L1_ffn_w_fc', 'L1_ffn_w_proj', 'L1_ffn_u', 'L1_ffn_v', 'L1_ffn_gate', 'L2_xattn_Wq',
        'L2_xattn_Wkv', 'L2_xattn_Wo', 'L2_xattn_rel_bias', 'L2_ffn_U1', 'L2_ffn_V1', 'L2_ffn_b1', 'L2_ffn_U2',
        'L2_ffn_V2', 'L2_ffn_b2', 'L3_xattn_Wq', 'L3_xattn_bq', 'L3_xattn_Wk', 'L3_xattn_bk', 'L3_xattn_Wv',
        'L3_xattn_bv', 'L3_xattn_Wo', 'L3_xattn_bo', 'L3_ffn_gate_w', 'L3_ffn_wg', 'L3_ffn_wu', 'L3_ffn_wd',
        'L3_ffn_swg', 'L3_ffn_swu', 'L3_ffn_swd']


def constants():
    part = np.arange(P)
    rel = np.arange(-(S - 1), S)
    nb, exact = BUCKETS // 2, BUCKETS // 4
    dist = np.maximum(np.abs(rel), 1).astype(np.float32)
    large = exact + (np.log(dist / np.float32(exact)) / np.float32(np.log(128 / exact)) * np.float32(nb - exact)).astype(np.int32)
    bucket = (rel > 0) * nb + np.where(np.abs(rel) < exact, np.abs(rel), np.minimum(large, nb - 1))
    f = np.float32
    return {
        "ident": np.eye(P, dtype=f),
        "head_mask": (part[:, None] % 64 // DH == np.arange(8)[None, :]).astype(f),
        "dup_mask": (part[:, None] // 64 == part[None, :] // DH % 2).astype(f),
        "route_tab": np.concatenate([
            np.broadcast_to(t.astype(f).ravel(), (P, t.size)) for t in (
                np.arange(E), np.arange(E) * REGION, np.arange(TILES) * P,
                np.arange(E)[None, :] <= np.arange(E)[:, None], np.arange(40))] + [part[:, None].astype(f)], axis=1),
        "place_tab": np.concatenate([part[:, None] + P * np.arange(2 * TILES)[None, :],
                                     np.full((P, 1), NOWHERE)], axis=1).astype(np.uint32),
        "before": (part[:, None] < part[None, :]).astype(f),
        "rel_onehot": (np.arange(BUCKETS)[:, None] == bucket[None, :]).astype(f),
    }


def kernel(**inputs):
    import concourse.bacc as bacc
    from concourse.bass_utils import run_bass_kernel_spmd

    nc = bacc.Bacc("TRN2", target_bir_lowering=False, num_devices=1)
    arrays, args, consts = {}, {}, {}
    for name in _INS:
        a = np.ascontiguousarray(inputs[name])
        if a.ndim == 0:
            a = a.reshape(1)
        if a.dtype == np.bool_:
            a = a.view(np.uint32)
        arrays["in_" + name] = a
        args[name] = nc.dram_tensor("in_" + name, a.shape, mybir.dt.from_np(a.dtype), kind="ExternalInput").ap()
    for name, a in constants().items():
        arrays["const_" + name] = a
        consts[name] = nc.dram_tensor("const_" + name, a.shape, mybir.dt.from_np(a.dtype), kind="ExternalInput").ap()
    out = nc.dram_tensor("out_x", (B, S, D), F32, kind="ExternalOutput").ap()
    bass_transformer(nc, args, consts, out)
    r = run_bass_kernel_spmd(nc, [arrays], core_ids=[0])
    return r.results[0]["out_x"]
```

```python
from contextlib import ExitStack

import numpy as np

import concourse.bass as bass
from concourse import mybir

ALU = mybir.AluOpType
ACT = mybir.ActivationFunctionType
AX_X = mybir.AxisListType.X
F32 = mybir.dt.float32
F16 = mybir.dt.float16
U8 = mybir.dt.uint8
U32 = mybir.dt.uint32
ds = bass.ds

P = 128
B, S, D = 32, 64, 128
H, DH = 16, 8
TILES = B * S // P
CH = 2 * P
GR = 4 * P
GROUPS = TILES // 4
FF = 512
FT = FF // P
E = 8
MI = 176
MC = 88
EPS = 1e-5
QK_SCALE = float(DH) ** -0.5
NEG = -1e9
SATURATED = 16.635532
BUCKETS = 32
REL = 2 * S - 1
TOK = B * S
REGION = TOK + P
ROW = D + 2
RT_T = 8
NX = 8
NOWHERE = 1 << 20
RT = {"iota": (0, E), "base": (8, E), "k128": (16, TILES), "le": (32, E * E), "k": (96, 40), "part": (136, 1)}


PHASES = [0, "moe0", "lin1", "ffn1", 2, "ffn2", 3, "moe3"]


def bass_transformer(nc, A, K, out):
    ctx = ExitStack()
    with ctx:
        def sb(name, shape, dt=F32):
            return ctx.enter_context(nc.sbuf_tensor(name, shape, dt))

        def sem(name):
            return ctx.enter_context(nc.semaphore(name))

        def row(ap):
            return ap.rearrange("(a n) -> a n", a=1)

        ident = sb("ident", [P, P])
        head_mask = sb("head_mask", [P, 8])
        dup_mask = sb("dup_mask", [P, P])
        route_tab = sb("route_tab", [P, 137])
        place_tab = sb("place_tab", [P, 2 * TILES + 1], U32)
        before = sb("before", [P, P], F16)
        ones = sb("ones", [P, P], F16)
        rel_onehot = sb("rel_onehot", [BUCKETS, REL + 1])
        minus_half = sb("minus_half", [P, 4])
        x = sb("x", [P, TILES * D])
        ctxT = sb("ctxT", [P, B * S])
        tok_in = sb("tok_in", [P, TILES * D])
        wqk0 = sb("wqk0", [P, 3, D])
        wo0 = sb("wo0", [P, 2, D])
        wqkv2 = sb("wqkv2", [P, 3, D])
        wo2 = sb("wo2", [P, D])
        wraw3 = sb("wraw3", [P, 4, D])
        w3T = sb("w3T", [P, 4, D])
        w1raw = sb("w1raw", [P, 2 * D])
        w1T = sb("w1T", [P, 2, D])
        bq = sb("bq", [P, 2, 2])
        bk = sb("bk", [P, 2, 2])
        bv_row = sb("bv_row", [P, D])
        bv_col = sb("bv_col", [P, 1])
        bias_out = sb("bias_out", [P, 4, D])
        router0 = sb("router0", [P, E])
        br0 = sb("br0", [P, E])
        gate3 = sb("gate3", [E, D])
        gate3T = sb("gate3T", [P, E])
        expert_w = sb("expert_w", [P, 2 * E * FF])
        e_up = expert_w[:, 0:E * FF].rearrange("p (e f) -> p e f", e=E)
        e_down = expert_w[:, E * FF:2 * E * FF].rearrange("p (e t d) -> p e t d", e=E, t=FT)

        def carve(at, parts, *shape):
            n = int(np.prod(shape))
            v = expert_w[0:parts, at:at + n]
            return v.rearrange("p (a b) -> p a b", a=shape[0]) if len(shape) == 2 else v, at + n
        m_gu, at = carve(0, P, E, 2 * MI)
        m_down, at = carve(at, MC, 2 * E, D)
        s_gu, at = carve(at, P, 2, 4 * MC)
        s_down, at = carve(at, MC, 4, D)
        fc_raw = sb("fc_raw", [P, FT, D])
        proj_raw = sb("proj_raw", [P, FF])
        u_raw = sb("u_raw", [P, FT, 16])
        v_raw = sb("v_raw", [16, D])
        fast_raw = sb("fast_raw", [16, 16])
        fastT = sb("fastT", [16, 16])
        uT = sb("uT", [16, FF])
        fast_v = sb("fast_v", [16, D])
        gate_col = sb("gate_col", [P, 1])
        tern = sb("tern", [P, FT, P])
        row_scale = sb("row_scale", [P, 8])
        w1eff = sb("w1eff", [P, FF])
        w1out = sb("w1out", [P, FT, D])
        u1 = sb("u1", [P, 32])
        u1T = sb("u1T", [32, D])
        v1r = sb("v1r", [32, FF])
        u2 = sb("u2", [P, FT, 32])
        u2T = sb("u2T", [32, FF])
        v2r = sb("v2r", [32, D])
        b1 = sb("b1", [P, FT])
        w2in = sb("w2in", [P, FF])
        w2out = sb("w2out", [P, FT, D])
        rel_bias = sb("rel_bias", [BUCKETS, H])
        rel_row = sb("rel_row", [H, P])
        ctx_sum = sb("ctx_sum", [P, B])
        s_row = sb("s_row", [1, B])
        per_batch = sb("per_batch", [B, D])
        mask_words = sb("mask_words", [P, TILES, S // 4], U32)
        pad_words = sb("pad_words", [P, TILES, S // 4], U32)
        cap0 = sb("cap0", [P, TILES * S])
        add3 = sb("add3", [P, TILES * S])
        amask = sb("amask", [P, S])
        bias2 = sb("bias2", [P, H, S])

        xnA = sb("xnA", [P, 2, D])
        lnA = sb("lnA", [P, CH])
        stA = sb("stA", [P, 2, 6])
        mvA = sb("mvA", [P, 2, 2])
        rsA = sb("rsA", [P, 2, 2])
        ctxc = [sb(f"ctxc{n}", [P, 4, 2, S]) for n in range(2)]
        q_diag = [sb(f"q_diag{n}", [P, 2, 2, P]) for n in range(2)]
        kT = sb("kT", [P, 2, 2, S])
        k_heads = [sb(f"k_heads{n}", [P, 2, 2, 8, S]) for n in range(2)]
        v_f32 = sb("v_f32", [P, 4, D])
        v_hi = [sb(f"v_hi{n}", [P, 2, 2, H, 9], F16) for n in range(2)]
        v_lo = [sb(f"v_lo{n}", [P, 2, 2, H, 9], F16) for n in range(2)]
        work = sb("work", [P, 4 * H * S])
        sc = [work[:, n * H * S:(n + 1) * H * S].rearrange("p (h k) -> p h k", h=H) for n in range(4)]
        pay = sb("pay", [P, TILES, 2, ROW])
        pay_row = pay[:, :, :, :].rearrange("p t c r -> p (t c r)")
        side = [pay_row[:, n * H * S:(n + 1) * H * S].rearrange("p (h k) -> p h k", h=H) for n in range(4)]
        mx = [sb(f"mx{n}", [P, H]) for n in range(4)]
        p_hi = sb("p_hi", [P, 8, P], F16)
        p_lo = sb("p_lo", [P, 8, P], F16)
        rsum = sb("rsum", [P, H])
        cat = [sb(f"cat{n}", [P, 2, P]) for n in range(2)]
        catT = sb("catT", [P, P])
        xnF = sb("xnF", [P, 4, D])
        lnF = sb("lnF", [P, GR])
        stF = sb("stF", [P, 4, 6])
        mvF = sb("mvF", [P, 4, 2])
        rsF = sb("rsF", [P, 4, 2])
        hT = sb("hT", [P, FT, GR])
        pad_row = sb("pad_row", [P, ROW])
        stM = sb("stM", [P, TILES, 6])
        mvM = sb("mvM", [P, TILES, 2])
        rsM = sb("rsM", [P, TILES, 2])
        logit = sb("logit", [P, RT_T, E])
        top8 = sb("top8", [P, RT_T, E])
        idx8 = sb("idx8", [P, RT_T, E], U32)
        idxf = sb("idxf", [P, 2, RT_T])
        chosen = sb("chosen", [P, 2, RT_T, E])
        counted = sb("counted", [P, RT_T, E], F16)
        place = sb("place", [P, RT_T, E])
        prob = sb("prob", [P, RT_T, E])
        psum8 = sb("psum8", [P, RT_T])
        pw = sb("pw", [P, RT_T, 2])
        run = sb("run", [P, E])
        spot = sb("spot", [P, 2, RT_T, E])
        slotf = sb("slotf", [P, 2, RT_T])
        slot = sb("slot", [P, 2, TILES], U32)
        tail = sb("tail", [P, E], U32)
        cnt = sb("cnt", [P, E])
        nblk = sb("nblk", [P, E])
        cumb = sb("cumb", [P, E])
        cmp8 = sb("cmp8", [P, 40, E])
        blkf = sb("blkf", [P, 2, 40])
        blk = sb("blk", [P, 2, 40], U32)
        xin = [work[:, n * (ROW + D):n * (ROW + D) + ROW] for n in range(NX)]
        xbT = [xnF[:, n, :] for n in range(2)]
        gated = [sb(f"gated{n}", [P, 4 * MC]) for n in range(2)]
        hb = [hT[:, n, :] for n in range(2)]
        hbT = [hT[:, 2 + n, :] for n in range(2)]
        yb = [work[:, n * (ROW + D) + ROW:(n + 1) * (ROW + D)] for n in range(NX)]

        psS = ctx.enter_context(nc.psum_tensor("psS", [P, 2, 512], F32))
        psT = ctx.enter_context(nc.psum_tensor("psT", [P, 2, 512], F32))
        psO = ctx.enter_context(nc.psum_tensor("psO", [P, 512], F32))
        psL = ctx.enter_context(nc.psum_tensor("psL", [P, 512], F32))
        psQ = ctx.enter_context(nc.psum_tensor("psQ", [P, 512], F32))
        psC = ctx.enter_context(nc.psum_tensor("psC", [P, 512], F32))

        rel_dram = nc.dram_tensor("rel_scratch", (H, S, P), F32).ap()
        batch_dram = nc.dram_tensor("batch_scratch", (B, D), F32).ap()

        dispatched = nc.dram_tensor("dispatched", (E * REGION + P, ROW), F32).ap()
        results = nc.dram_tensor("results", (2 * TOK, D), F32).ap()

        r_rt = sem("r_rt")
        r_e = sem("r_e")
        r_cnt = sem("r_cnt")
        r_oh = sem("r_oh")
        r_dup = sem("r_dup")
        r_top = sem("r_top")
        r_slot = sem("r_slot")
        r_sent = sem("r_sent")
        r_tab = sem("r_tab")
        r_end = sem("r_end")
        pad_added = sem("pad_added")
        tern_ready = sem("tern_ready")
        r_tail = sem("r_tail")
        pad_ready = sem("pad_ready")
        pad_out = sem("pad_out")
        b_ld = [sem(f"b_ld{n}") for n in range(NX)]
        b_xt = sem("b_xt")
        b_xc = sem("b_xc")
        b_m1 = sem("b_m1")
        b_sg = sem("b_sg")
        b_hd = sem("b_hd")
        b_t2 = sem("b_t2")
        b_hc = sem("b_hc")
        b_m2 = sem("b_m2")
        b_ye = sem("b_ye")
        b_sc = [sem(f"b_sc{n}") for n in range(NX)]
        b_res = [sem(f"b_res{g}") for g in range(GROUPS)]
        ld_const = sem("ld_const")
        ld_x = sem("ld_x")
        ld_ctx = sem("ld_ctx")
        ld_a0 = sem("ld_a0")
        ld_mask = sem("ld_mask")
        ld_prep = sem("ld_prep")
        ld_moe0 = sem("ld_moe0")
        ld_moe3 = sem("ld_moe3")
        zeroed = sem("zeroed")
        setup_pe = sem("setup_pe")
        setup_ev = sem("setup_ev")
        dve_prep = sem("dve_prep")
        rel_out = sem("rel_out")
        rel_in = sem("rel_in")
        batch_out = sem("batch_out")
        batch_in = sem("batch_in")
        a_stat = sem("a_stat")
        a_rstd = sem("a_rstd")
        a_xn = sem("a_xn")
        a_lnp = sem("a_lnp")
        a_ln = sem("a_ln")
        a_xb = sem("a_xb")
        a_ctx = [sem(f"a_ctx{n}") for n in range(2)]
        a_qkp = sem("a_qkp")
        a_q = sem("a_q")
        a_km = sem("a_km")
        a_vp = sem("a_vp")
        a_v = sem("a_v")
        a_vhi = sem("a_vhi")
        a_vlo = sem("a_vlo")
        a_sc = sem("a_sc")
        a_ev = sem("a_ev")
        a_side = [sem(f"a_side{n}") for n in range(4)]
        a_sidef = sem("a_sidef")
        a_mx = sem("a_mx")
        a_sub = sem("a_sub")
        a_exp = sem("a_exp")
        a_tr = sem("a_tr")
        a_hi = sem("a_hi")
        a_lo = sem("a_lo")
        a_pv = sem("a_pv")
        a_rs = sem("a_rs")
        a_cat = sem("a_cat")
        a_ctp = sem("a_ctp")
        a_ct = sem("a_ct")
        a_out = sem("a_out")
        a_x = sem("a_x")
        f_stat = sem("f_stat")
        f_rstd = sem("f_rstd")
        f_xn = sem("f_xn")
        f_lnp = sem("f_lnp")
        f_ln = sem("f_ln")
        f_xb = sem("f_xb")
        f_bn = sem("f_bn")
        f_x = sem("f_x")
        a_bn = sem("a_bn")
        zeroed_v = sem("zeroed_v")
        cap_ready = sem("cap_ready")
        bv_ready = sem("bv_ready")
        fs = {}
        for k in ("lin1", "ffn1", "ffn2"):
            fs[k] = [sem(f"{k}_{w}") for w in (("up", "read", "hidden", "down") if k != "lin1" else ("down",))]
        fs["lin1"] = [None, None, None, fs["lin1"][0]]
        fs["ffn2"][2] = fs["ffn2"][1]
        stored = sem("stored")

        ATT = {0: 0, 2: 1, 3: 2}
        KIND = {"moe0": "moe", "lin1": "lin", "ffn1": "plain", "ffn2": "plain", "moe3": "moe"}
        FFN = {k: n for n, k in enumerate(p for p in PHASES if p in KIND)}
        F_BEFORE = {p: sum(q in KIND for q in PHASES[:n]) for n, p in enumerate(PHASES) if p in ATT}
        F_AFTER_A = {p: ATT[PHASES[n - 1]] + 1 for n, p in enumerate(PHASES) if p in KIND and PHASES[n - 1] in ATT}

        MOE = {"moe0": 0, "moe3": 1}
        CHOICES = {"moe0": 1, "moe3": 2}
        NBLOCKS = {k: -(-((CHOICES[k] * TOK + E * (P - 1)) // P) // NX) * NX for k in MOE}
        NBLOCKS["shared"] = TILES
        BLOCK0 = {"moe0": 0, "shared": NBLOCKS["moe0"], "moe3": NBLOCKS["moe0"] + TILES}
        SCATTERED = {"moe0": 0, "moe3": NBLOCKS["moe0"] // NX}
        SENT = {"moe0": 16 * TILES, "moe3": 16 * 3 * TILES}
        psH = [psO, psL]
        psR = [psO, psC]

        def tab(name):
            at, n = RT[name]
            return route_tab[:, at:at + n]

        set_ps = [psQ, psC]
        bv_twice = xnF[:, 0:2, :]

        def tr(pe, dst, src, k):
            return nc.tensor.transpose(dst, src, ident[0:k, 0:k])

        def setup_jobs():
            mm = nc.tensor.matmul
            dcopy = nc.vector.tensor_copy

            def acopy(dst, src, **kw):
                return nc.scalar.activation(dst, src, ACT.Copy, **kw)

            def flat(t):
                return t[:, :, :].rearrange("p a b -> p (a b)")

            def transposes(dst, srcs, k):
                def pe(ps):
                    for n, src in enumerate(srcs):
                        r = tr(None, ps[dst, n * k:(n + 1) * k], src, k)
                    return r
                return pe
            full = slice(0, P)
            jobs = []
            for q in range(4):
                jobs.append((f"ctx{q}", [(ld_ctx, 16)],
                             transposes(full, [tok_in[:, t * P:(t + 1) * P] for t in range(4 * q, 4 * q + 4)], P),
                             lambda ps, q=q: dcopy(ctxT[:, q * 512:(q + 1) * 512], ps[:, :])))

            def pe(ps):
                for t in range(TILES):
                    r = mm(ps[:, 2 * t:2 * t + 2], tok_in[:, t * P:(t + 1) * P], dup_mask[:, 0:2 * DH:DH], start=True, stop=True)
                return r
            jobs.append(("ctx_sum", [], pe, lambda ps: dcopy(ctx_sum[:, :], ps[:, 0:B])))

            def pe(ps):
                for h2 in range(2):
                    r = mm(ps[:, 0:D], bv_twice[0:64, h2, :], wo0[0:64, h2, :], start=(h2 == 0), stop=(h2 == 1))
                return r
            jobs.append(("bias0", [(ld_a0, 16 * 9), (bv_ready, 1)], pe,
                         lambda ps: nc.vector.tensor_tensor(bias_out[:, 0, :], ps[:, 0:D], bias_out[:, 0, :], ALU.add)))

            jobs.append(("w3T", [(ld_prep, 16 * 24)], transposes(full, [wraw3[:, n, :] for n in range(4)], P),
                         lambda ps: acopy(flat(w3T), ps[:, :])))
            jobs.append(("w1T", [], transposes(full, [w1raw[:, n * P:(n + 1) * P] for n in range(2)], P),
                         lambda ps: acopy(flat(w1T), ps[:, 0:2 * P])))
            jobs.append(("rel", [], lambda ps: mm(ps[0:H, 0:REL], rel_bias[:, :], rel_onehot[:, 0:REL], start=True, stop=True),
                         lambda ps: acopy(rel_row[:, 0:REL], ps[0:H, 0:REL])))
            jobs.append(("u1T", [], transposes(slice(0, 32), [u1[:, :]], P), lambda ps: acopy(u1T[:, :], ps[0:32, 0:P])))

            def pe(ps):
                mm(ps[0:B, 0:D], ctx_sum[:, :], w1T[:, 1, :], start=True, stop=False)
                return mm(ps[0:B, 0:D], s_row[0:1, :], bias_out[0:1, 3, :], start=False, stop=True)
            jobs.append(("batch", ["w1T"], pe, lambda ps: acopy(per_batch[:, :], ps[0:B, 0:D], scale=1.0 / S)))

            def pe(ps):
                mm(ps[:, 0:D], bv_col[:, 0:1].broadcast_to([P, P]), w3T[:, 3, :], start=True, stop=False)
                return mm(ps[:, 0:D], ident[:, :], bias_out[:, 1, :], start=False, stop=True)
            jobs.append(("bias3", ["w3T"], pe, lambda ps: acopy(bias_out[:, 1, :], ps[:, 0:D])))
            jobs.append(("gate3T", [], lambda ps: tr(None, ps[:, 0:E], gate3[:, :], E),
                         lambda ps: acopy(gate3T[:, :], ps[:, 0:E])))
            jobs.append(("u2T", [], transposes(slice(0, 32), [u2[:, n, :] for n in range(FT)], P),
                         lambda ps: acopy(u2T[:, :], ps[0:32, :])))
            jobs.append(("uT", [], transposes(slice(0, 16), [u_raw[:, n, :] for n in range(FT)], P),
                         lambda ps: acopy(uT[:, :], ps[0:16, :])))
            jobs.append(("fastT", [], lambda ps: tr(None, ps[0:16, 0:16], fast_raw[:, :], 16),
                         lambda ps: acopy(fastT[:, :], ps[0:16, 0:16])))
            jobs.append(("w2in", ["u1T"], lambda ps: mm(ps[:, :], u1T[:, :], v1r[:, :], start=True, stop=True),
                         lambda ps: acopy(w2in[:, :], ps[:, :])))
            jobs.append(("fast_v", ["fastT"], lambda ps: mm(ps[0:16, 0:D], fastT[:, :], v_raw[:, :], start=True, stop=True),
                         lambda ps: nc.scalar.activation(fast_v[:, :], ps[0:16, 0:D], ACT.Copy, scale=gate_col[0:16, 0:1])))

            def pe(ps):
                for n in range(FT):
                    r = mm(ps[:, n * P:(n + 1) * P], u2T[:, n * P:(n + 1) * P], v2r[:, :], start=True, stop=True)
                return r
            jobs.append(("w2out", ["u2T"], pe, lambda ps: acopy(flat(w2out), ps[:, :])))

            def pe(ps):
                for n in range(FT):
                    c = slice(n * P, (n + 1) * P)
                    mm(ps[:, c], tern[:, n, :], ident[:, :], start=True, stop=False)
                    r = mm(ps[:, c], fast_v[:, :], uT[:, c], start=False, stop=True)
                return r
            jobs.append(("w1in", ["uT", "fast_v", (tern_ready, 1)], pe, lambda ps: acopy(w1eff[:, :], ps[:, :])))
            jobs.append(("w1out", [(tern_ready, 2)], transposes(full, [proj_raw[:, n * P:(n + 1) * P] for n in range(FT)], P),
                         lambda ps: acopy(flat(w1out), ps[:, :])))
            return jobs

        JOBS = setup_jobs()
        NAMES = [j[0] for j in JOBS]
        FIRST = NAMES.index("bias0") + 1

        def job_done(name):
            return NAMES.index(name) + 1

        def staggered(engine, nb, step):
            for s in (-2, -1, 0):
                step(s % NX, s, lo=s)
            with engine.Fori(0, nb // NX - 1) as j:
                for u in range(NX):
                    step((u + 1) % NX, NX * j + (u + 1), lo=1)
            for s in range(nb - NX + 1, nb + 1):
                step(s % NX, s, lo=1, hi=True)

        def run_jobs(pe, lo, hi):
            for n in range(lo, hi):
                _, waits, job, _ = JOBS[n]
                if n >= 2:
                    pe.wait_ge(setup_ev, n - 1)
                for w in waits:
                    if isinstance(w, str):
                        pe.wait_ge(setup_ev, job_done(w))
                    else:
                        pe.wait_ge(*w)
                job(set_ps[n % 2]).then_inc(setup_pe, 1)

        def wait_apart(engine, s, value):
            at = value if isinstance(value, int) else engine.to_reg(value)
            engine.wait_ge(ld_const, 16 * 7)
            engine.wait_ge(s, at)

        block = ctx.enter_context(nc.Block())

        @block.sync
        def _(sp):
            for t, k in ((ident, "ident"), (head_mask, "head_mask"), (dup_mask, "dup_mask"), (route_tab, "route_tab"),
                         (place_tab, "place_tab"), (before, "before")):
                sp.dma_start(t[:], K[k]).then_inc(ld_const, 16)
            sp.dma_start(rel_onehot[:, 0:REL], K["rel_onehot"]).then_inc(ld_const, 16)
            sp.dma_start(tok_in[:].rearrange("p (t d) -> p t d", t=TILES),
                         A["ctx_1024"].rearrange("(t b) s d -> (b s) t d", b=2)).then_inc(ld_ctx, 16)
            sp.dma_start(x[:].rearrange("p (t d) -> p t d", t=TILES),
                         A["x"].rearrange("(t b) s d -> (b s) t d", b=2)).then_inc(ld_x, 16)
            for b in range(2):
                sp.dma_start(mask_words[b * S:(b + 1) * S], A["mask_BxSxS2_bf1"].rearrange(
                    "(t b) q k -> b q t k", b=2)[b]).then_inc(ld_mask, 16)
                sp.dma_start(pad_words[b * S:(b + 1) * S], A["mask_BxS2_bf0"].rearrange(
                    "(t b) k -> b t k", b=2)[b].partition_broadcast(S)).then_inc(ld_mask, 16)
                sp.dma_start(amask[b * S:(b + 1) * S], A["fside_SxS2_0"]).then_inc(ld_mask, 16)
            def chunk_load(n, c, cg):
                sp.wait_ge(a_vp, cg - 1)
                for d in range(2):
                    sp.dma_start(ctxc[n][:, :, d, :], ctxT[:, ds(c * CH, CH)].rearrange("p (b s) -> p b s", b=4)).then_inc(a_ctx[n], 16)

            def side_load(n, i):
                sp.wait_ge(a_ev, 2 * (32 + i - 4 + 1))
                for b in range(2):
                    sp.dma_start(side[n][b * S:(b + 1) * S],
                                 A["fside_Bx16xSxS2_0"][ds(2 * i + b, 1)].rearrange("a h q k -> q (a h) k"))\
                      .then_inc(a_side[n], 16)

            def moe(kind):
                m = MOE[kind]
                if kind == "moe3":
                    def load_tile(n, t, k):
                        if isinstance(t, int):
                            if t % 4 == 0:
                                sp.wait_ge(f_xn, GROUPS * FFN[kind] + t // 4 + 1)
                        wait_apart(sp, b_xt, k - (NX - 1))
                        sp.dma_start(xin[n][:, 0:D], pay_row[:, ds(t * 2 * ROW, D)]).then_inc(b_ld[n], 16)
                    b0 = BLOCK0["shared"]
                    for t in range(NX):
                        if t == 0:
                            sp.wait_ge(f_xn, GROUPS * FFN[kind] + GROUPS)
                        load_tile(t, t, b0 + t)
                    with sp.Fori(1, TILES // NX) as j:
                        for n in range(NX):
                            load_tile(n, NX * j + n, NX * j + (b0 + n))
                b0, nb = BLOCK0[kind], NBLOCKS[kind]
                sp.wait_ge(r_end, m + 1)
                for e in range(E):
                    end = sp.value_load(tail[0:1, e:e + 1], min_val=0, max_val=(E - 1) * REGION + TOK)
                    sp.dma_start(dispatched[ds(end, P), :], pad_row[:, :]).then_inc(r_tail, 16)
                sp.wait_ge(r_tab, m + 1)
                sp.wait_ge(r_sent, SENT[kind])
                sp.wait_ge(r_tail, 16 * E * (m + 1))
                sp.wait_ge(pad_out, 16)
                sc0 = SCATTERED[kind]

                def load_block(n, b, first):
                    row_at = sp.value_load(blk[0:1, 0, ds(b, 1)], min_val=0, max_val=E * REGION)
                    if not (first and b0 == 0):
                        wait_apart(sp, b_xt, b + (b0 - NX + 1))
                    if not first:
                        sp.wait_ge(b_sc[n], (b - n) * (16 // NX) + 16 * sc0)
                    sp.dma_start(xin[n], dispatched[ds(row_at, P), :]).then_inc(b_ld[n], 16)
                for n in range(NX):
                    load_block(n, n, True)
                with sp.Fori(1, nb // NX) as j:
                    for n in range(NX):
                        load_block(n, NX * j + n, False)
                for n in range(NX):
                    sp.wait_ge(b_sc[n], 16 * (sc0 + nb // NX))
                for g in range(GROUPS):
                    for c in range(CHOICES[kind]):
                        sp.dma_start(pay_row[:, c * TOK + g * GR:c * TOK + (g + 1) * GR].rearrange("p (t d) -> p t d", t=4),
                                     results[c * TOK + g * GR:c * TOK + (g + 1) * GR].rearrange("(t p) d -> p t d", p=P))\
                          .then_inc(b_res[g], 16)

            sp.wait_ge(pad_ready, 1)
            sp.dma_start(dispatched[E * REGION:E * REGION + P, :], pad_row[:, :]).then_inc(pad_out, 16)

            for a in range(3):
                if a == 1 and "moe0" in FFN:
                    moe("moe0")
                    for o, i in ((m_gu[:, :, 0:MI], A["L3_ffn_wg"].rearrange("e h i -> h e i")),
                                 (m_gu[:, :, MI:2 * MI], A["L3_ffn_wu"].rearrange("e h i -> h e i")),
                                 (m_down, A["L3_ffn_wd"].rearrange("e (c p) h -> p (e c) h", p=MC)),
                                 (s_gu[:, 0, :], A["L3_ffn_swg"]), (s_gu[:, 1, :], A["L3_ffn_swu"]),
                                 (s_down, A["L3_ffn_swd"].rearrange("(c p) h -> p c h", p=MC))):
                        sp.dma_start(o, i).then_inc(ld_moe3, 16)
                for n in range(2):
                    if a == 0:
                        if n == 0:
                            sp.wait_ge(setup_ev, job_done("ctx3"))
                        for d in range(2):
                            sp.dma_start(ctxc[n][:, :, d, :], ctxT[:, n * CH:(n + 1) * CH].rearrange("p (b s) -> p b s", b=4))\
                              .then_inc(a_ctx[n], 16)
                    else:
                        chunk_load(n, n, 8 * a + n)
                if a == 0:
                    sp.dma_start(e_up, A["L0_ffn_W1"].rearrange("e h f -> h e f")).then_inc(ld_moe0, 16)
                    for e in range(E):
                        sp.dma_start(e_down[:, e], A["L0_ffn_W2"][e].rearrange("(f p) h -> p f h", p=P)).then_inc(ld_moe0, 16)
                if a == 2:
                    for n in range(4):
                        for b in range(2):
                            sp.dma_start(side[n][b * S:(b + 1) * S],
                                         A["fside_Bx16xSxS2_0"][2 * n + b].rearrange("h q k -> q h k")).then_inc(a_side[n], 16)
                with sp.Fori(1, 4) as j:
                    for n in range(2):
                        chunk_load(n, 2 * j + n, 2 * j + (8 * a + n))
                        if a == 2:
                            for u in range(2):
                                side_load(2 * n + u, 4 * j + (2 * n + u))

            if "moe3" in FFN:
                moe("moe3")
            sp.wait_ge(f_x, GROUPS * len(FFN))
            sp.wait_ge(a_x, 3 * TILES)
            sp.dma_start(out.rearrange("(t b) s d -> (b s) t d", b=2),
                         x[:].rearrange("p (t d) -> p t d", t=TILES)).then_inc(stored, 16)
            sp.wait_ge(stored, 16)

        mm = nc.tensor.matmul

        @block.tensor
        def _(pe):
            pe.wait_ge(ld_const, 16 * 7)
            run_jobs(pe, 0, FIRST)

            def ln_transposes(cg):
                pe.wait_ge(a_xn, cg + 1)
                if not (isinstance(cg, int) and cg == 0):
                    pe.wait_ge(a_ln, cg)
                for t in range(2):
                    r = tr(pe, psL[:, t * P:(t + 1) * P], xnA[:, t, :], P)
                r.then_inc(a_lnp, 1)

            def project(a, n, cg):
                w = (wqk0, wqkv2, w3T)[a]
                pe.wait_ge(a_ln, cg + 1)
                pe.wait_ge(a_ctx[n], ctx_count(cg, n))
                if not (isinstance(cg, int) and cg == 0):
                    pe.wait_ge(a_q, cg)
                    if not (isinstance(cg, int) and cg == 1):
                        pe.wait_ge(a_v, cg if isinstance(cg, int) and cg % 8 == 0 else cg - 1)
                for qk in range(2):
                    toks = lnA[:, :] if qk == 0 else ctxc[n][:, :, 0, :]
                    toks = toks.rearrange("p (u b s) -> p u b s" if qk == 0 else "p (u b) s -> p u b s", u=2, b=2)
                    for half in range(2):
                        for b in range(2):
                            r = mm(psQ[b * 64:(b + 1) * 64, (2 * qk + half) * P:(2 * qk + half + 1) * P],
                                   w[:, qk, half * 64:(half + 1) * 64], toks[:, :, b, :], start=True, stop=True)
                r.then_inc(a_qkp, 1)

            def ctx_count(cg, n):
                if isinstance(cg, int):
                    return 32 * (cg // 2 + 1)
                return (cg - n) * 16 + 32

            def values(a, n, cg, more):
                w = (wqk0, wqkv2, w3T)[a]
                pe.wait_ge(a_q, cg + (2 if more else 1))
                pe.wait_ge(a_ctx[n], ctx_count(cg, n))
                for u in range(2):
                    for b in range(2):
                        tok = ctxc[n][:, 2 * u + b, :, :].rearrange("p d s -> p (d s)")
                        r = mm(psQ[:, (2 * u + b) * P:(2 * u + b + 1) * P], tok, w[:, 2, :], start=True, stop=True)
                r.then_inc(a_vp, 1)

            def scores(n, u, i, cg):
                pe.wait_ge(a_km, 2 * cg + 2)
                for half in range(2):
                    if not (isinstance(i, int) and i == 0):
                        pe.wait_ge(a_ev, 2 * i - 1 + half)
                    mm(psS[:, half, :], q_diag[n][:, half, u, :], k_heads[n][:, half, u, :, :],
                       start=True, stop=True).then_inc(a_sc, 1)

            def transposes(m, i):
                pe.wait_ge(a_exp, i + 1)
                for half in range(2):
                    if not (isinstance(i, int) and i == 0):
                        pe.wait_ge(a_lo, 2 * i - 1 + half)
                    for j in range(4):
                        g = 4 * half + j
                        r = tr(pe, psT[:, half, j * P:(j + 1) * P],
                               sc[m][:, 2 * g:2 * g + 2, :].rearrange("p h k -> p (h k)"), P)
                    r.then_inc(a_tr, 1)

            def apply_probs(n, u, i, cg):
                pe.wait_ge(a_lo, 2 * i + 2)
                pe.wait_ge(a_vlo, cg + 1)
                pe.wait_ge(a_vhi, cg + 1)
                if not (isinstance(i, int) and i == 0):
                    pe.wait_ge(a_cat, i)
                o = psO[:, 0:2 * H * 9].rearrange("p (b h e) -> p b h e", b=2, h=H)
                for j in range(8):
                    for k, (pp, vv) in enumerate(((p_hi, v_hi), (p_hi, v_lo), (p_lo, v_hi))):
                        r = mm(o[:, :, 2 * j:2 * j + 2, :], pp[:, j, :], vv[n][:, u, :, 2 * j:2 * j + 2, :],
                               start=(k == 0), stop=(k == 2))
                r.then_inc(a_pv, 1)

            def cat_transpose(m, i):
                pe.wait_ge(a_cat, i + 1)
                if not (isinstance(i, int) and i == 0):
                    pe.wait_ge(a_x, i)
                tr(pe, psC[:, 0:P], cat[m][:, 0, :], P).then_inc(a_ctp, 1)

            def project_out(a, m, i, ia):
                if a == 0:
                    pe.wait_ge(a_cat, i + 1)
                    if not (isinstance(i, int) and i == 0):
                        pe.wait_ge(a_x, i)
                    for h2 in range(2):
                        r = mm(psC[:, P:2 * P], cat[m][:, h2, :], wo0[:, h2, :], start=(h2 == 0), stop=(h2 == 1))
                else:
                    pe.wait_ge(a_ct, ia + 1)
                    r = mm(psC[:, P:2 * P], catT[:, :], wo2[:, :] if a == 1 else w3T[:, 3, :], start=True, stop=True)
                r.then_inc(a_out, 1)

            def attention(a):
                def step(u, j, first=False, more=True):
                    i = 4 * j + u + 16 * a
                    c, n = 2 * j + u // 2 + 8 * a, u // 2
                    scores(n, u % 2, i, c)
                    if u % 2 == 0 and more:
                        ln_transposes(c + 1)
                    if not (first and u < 2):
                        transposes((u - 2) % 4, i - 2)
                    if a and not (first and u < 3):
                        cat_transpose((u - 3) % 2, i - 3)
                    if u % 2 == 1:
                        values(a, n, c, more)
                    elif more:
                        project(a, 1 - n, c + 1)
                    if not (first and u < 3):
                        project_out(a, (u - 3) % 2, i - 3, i - 19)
                    if not (first and u < 2):
                        apply_probs(1 - n, u % 2, i - 2, c - 1)

                ln_transposes(8 * a)
                project(a, 0, 8 * a)
                for u in range(4):
                    step(u, 0, first=True)
                with pe.Fori(1, 3) as j:
                    for u in range(4):
                        step(u, j)
                for u in range(4):
                    step(u, 3, more=(u < 2))
                for u in range(3):
                    step_tail(a, u)

            def step_tail(a, u):
                i = 16 + u + 16 * a
                if u < 2:
                    transposes((u - 2) % 4, i - 2)
                if a:
                    cat_transpose((u - 3) % 2, i - 3)
                project_out(a, (u - 3) % 2, i - 3, i - 19)
                if u < 2:
                    apply_probs(1, u % 2, i - 2, 8 * a + 7)

            def ffn_ln(G):
                pe.wait_ge(f_xn, G + 1)
                if not (isinstance(G, int) and G == 0):
                    pe.wait_ge(f_ln, G)
                for t in range(4):
                    r = tr(pe, psL[:, t * P:(t + 1) * P], xnF[:, t, :], P)
                r.then_inc(f_lnp, 1)

            def plain(kind):
                f0 = GROUPS * FFN[kind]
                win, wout = (w1eff, w1out) if kind == "ffn1" else (w2in, w2out)
                up, read, hid, y = fs[kind]

                def group(g, last):
                    pe.wait_ge(f_ln, g + (f0 + 1))
                    for f in range(FT):
                        if f >= 2 or not isinstance(g, int) or g > 0:
                            pe.wait_ge(read, g * FT + (f - 1))
                        mm(psS[:, f % 2, :], win[:, f * P:(f + 1) * P], lnF[:, :], start=True, stop=True).then_inc(up, 1)
                    if not last:
                        ffn_ln(g + (f0 + 1))
                    pe.wait_ge(hid, g * FT + FT)
                    if not (isinstance(g, int) and g == 0):
                        pe.wait_ge(f_x, g + f0)
                    for t in range(4):
                        for f in range(FT):
                            r = mm(psT[:, 0, t * P:(t + 1) * P], hT[:, f, t * P:(t + 1) * P], wout[:, f, :],
                                   start=(f == 0), stop=(f == FT - 1))
                    r.then_inc(y, 1)

                ffn_ln(f0)
                group(0, False)
                with pe.Fori(1, GROUPS - 1) as g:
                    group(g, False)
                group(GROUPS - 1, True)

            def linear():
                f0 = GROUPS * FFN["lin1"]
                y = fs["lin1"][3]

                def group(g, last):
                    pe.wait_ge(f_ln, g + (f0 + 1))
                    if not (isinstance(g, int) and g == 0):
                        pe.wait_ge(f_x, g + f0)
                    for t in range(4):
                        r = mm(psT[:, 0, t * P:(t + 1) * P], lnF[:, t * P:(t + 1) * P], w1T[:, 0, :], start=True, stop=True)
                    r.then_inc(y, 1)
                    if not last:
                        ffn_ln(g + (f0 + 1))

                ffn_ln(f0)
                group(0, False)
                with pe.Fori(1, GROUPS - 1) as g:
                    group(g, False)
                group(GROUPS - 1, True)

            def blocks(kind):
                b0, nb = BLOCK0[kind], NBLOCKS[kind]
                m = 0 if kind == "moe0" else 1
                chunks, kk = {"moe0": (FT, P), "moe3": (2, MC), "shared": (4, MC)}[kind]

                def expert(b):
                    if kind == "shared":
                        return 0
                    return pe.value_load(blk[0:1, 1, ds(b, 1)], min_val=0, max_val=E - 1)

                def since(k, sm, v):
                    if not (isinstance(k, int) and k < 0):
                        pe.wait_ge(sm, v)

                def x_transpose(q, b):
                    k = b + b0
                    pe.wait_ge(b_ld[q], (k - q) * (16 // NX) + 16)
                    since(k - 1, b_xc, k)
                    tr(pe, psQ[:, 0:P], xin[q][:, 0:D], P).then_inc(b_xt, 1)

                def up(q, b):
                    k = b + b0
                    pe.wait_ge(b_xc, k + 1)
                    since(k - 2, b_hd, k - 1)
                    if kind == "shared":
                        mm(psT[:, q % 2, 0:4 * MC], xbT[q % 2], s_gu[:, 1, :], start=True, stop=True)
                        r = mm(psS[:, q % 2, 0:4 * MC], xbT[q % 2], s_gu[:, 0, :], start=True, stop=True)
                    else:
                        w = FF if kind == "moe0" else 2 * MI
                        r = mm(psS[:, q % 2, 0:w], xbT[q % 2], expert_w[:, ds(expert(b) * w, w)], start=True, stop=True)
                    r.then_inc(b_m1, 1)

                def h_transpose(q, b):
                    k = b + b0
                    pe.wait_ge(b_hd, k + 1)
                    since(k - 2, b_hc, k - 1)
                    for f in range(chunks):
                        r = tr(pe, psH[q % 2][0:kk, f * P:(f + 1) * P], hb[q % 2][:, f * kk:(f + 1) * kk], P)
                    r.then_inc(b_t2, 1)

                def down(q, b):
                    k = b + b0
                    e = expert(b)
                    pe.wait_ge(b_hc, k + 1)
                    since(k - 1, b_ye, k)
                    for f in range(chunks):
                        if kind == "shared":
                            w = s_down[:, f, :]
                        elif kind == "moe0":
                            w = expert_w[:, ds(e * (FT * D) + (E * FF + f * D), D)]
                        else:
                            w = expert_w[0:MC, ds(e * (2 * D) + (E * 2 * MI + f * D), D)]
                        r = mm(psC[:, 0:D], hbT[q % 2][0:kk, f * P:(f + 1) * P], w, start=(f == 0), stop=(f == chunks - 1))
                    r.then_inc(b_m2, 1)

                def step(q, s, lo=-2, hi=None):
                    if hi is None or s + 2 < nb:
                        x_transpose((q + 2) % NX, s + 2)
                    if lo >= -1 and (hi is None or s + 1 < nb):
                        up((q + 1) % NX, s + 1)
                    if lo >= 0 and (hi is None or s < nb):
                        h_transpose(q, s)
                    if lo >= 1:
                        down((q - 1) % NX, s - 1)

                if kind != "shared":
                    pe.wait_ge(r_tab, m + 1)
                staggered(pe, nb, step)

            def moe(kind):
                f0, m = GROUPS * FFN[kind], MOE[kind]
                w = router0 if kind == "moe0" else gate3T
                for g in range(GROUPS):
                    G, R = f0 + g, GROUPS * m + g
                    pe.wait_ge(f_xn, G + 1)
                    if G:
                        pe.wait_ge(f_ln, G)
                    for t in range(4):
                        r = tr(pe, psL[:, t * P:(t + 1) * P], pay[:, 4 * g + t, 0, 0:D], P)
                    r.then_inc(f_lnp, 1)
                    pe.wait_ge(f_ln, G + 1)
                    for t in range(4 * g, 4 * g + 4):
                        r = mm(psR[g // 2][:, t * E:(t + 1) * E], lnF[:, (t % 4) * P:(t % 4 + 1) * P], w[:, :], start=True, stop=True)
                    r.then_inc(r_rt, 1)
                for h in range(TILES // RT_T):
                    pe.wait_ge(r_oh, TILES // RT_T * m + h + 1)
                    mm(psQ[:, 0:RT_T * E], before[:, :], counted[:, :, :], start=True, stop=False)
                    for t in range(1, RT_T):
                        mm(psQ[:, t * E:RT_T * E], ones[:, :], counted[:, 0:RT_T - t, :], start=False, stop=(t == RT_T - 1))
                    for t in range(RT_T):
                        r = mm(psQ[:, RT_T * E:(RT_T + 1) * E], ones[:, :], counted[:, t, :], start=(t == 0), stop=(t == RT_T - 1))
                    r.then_inc(r_cnt, 1)
                pe.wait_ge(r_slot, TILES // RT_T * (m + 1))
                if kind == "moe0":
                    run_jobs(pe, FIRST, len(JOBS))
                    pe.wait_ge(setup_ev, len(JOBS))
                if kind == "moe3":
                    pe.wait_ge(ld_moe3, 16 * 6)
                    blocks("shared")
                else:
                    pe.wait_ge(ld_moe0, 16 * 9)
                blocks(kind)
                pe.wait_ge(b_ye, BLOCK0[kind] + NBLOCKS[kind])

            for ph in PHASES:
                if ph in ATT:
                    if ph:
                        pe.wait_ge(f_x, GROUPS * F_BEFORE[ph])
                    attention(ATT[ph])
                    continue
                if ph in F_AFTER_A:
                    pe.wait_ge(a_x, 16 * F_AFTER_A[ph])
                {"plain": plain, "lin": lambda k: linear(), "moe": moe}[KIND[ph]](ph)

        act = nc.scalar.activation

        @block.scalar
        def _(ac):
            loads = [(wqk0[:, 0, :], A["L0_xattn_Wq"]), (wqk0[:, 1, :], A["L0_xattn_Wk"]), (wqk0[:, 2, :], A["L0_xattn_Wv"]),
                     (wo0[0:64], A["L0_xattn_Wo"].rearrange("(h s) e -> s h e", h=2)),
                     (wo0[64:P], A["L0_xattn_Wo"].rearrange("(h s) e -> s h e", h=2)),
                     (bv_row[:], A["L0_xattn_bv"].partition_broadcast(P)),
                     (bias_out[:, 0, :], A["L0_xattn_bo"].partition_broadcast(P)),
                     (router0[:], A["L0_ffn_Wr"]), (br0[:], A["L0_ffn_br"].partition_broadcast(P))]
            assert len(loads) == 9
            for o, i in loads:
                ac.dma_start(o, i).then_inc(ld_a0, 16)
            loads = [(wraw3[:, n, :], A[f"L3_xattn_W{k}"]) for n, k in enumerate("qkvo")]
            loads += [(bias_out[:, 1, :], A["L3_xattn_bo"].partition_broadcast(P)),
                      (bias_out[:, 2, :], A["L2_ffn_b2"].partition_broadcast(P)),
                      (bias_out[:, 3, :], A["L1_xattn_b"].partition_broadcast(P)),
                      (bv_col[:], A["L3_xattn_bv"].rearrange("(p a) -> p a", a=1)),
                      (wqkv2[:, 0, :], A["L2_xattn_Wq"]),
                      (wqkv2[:, 1:3, :], A["L2_xattn_Wkv"].rearrange("p (a n) -> p a n", a=2)),
                      (wo2[:], A["L2_xattn_Wo"]), (w1raw[:], A["L1_xattn_W"]),
                      (gate3[:], A["L3_ffn_gate_w"]), (fc_raw[:], A["L1_ffn_w_fc"].rearrange("(t p) d -> p t d", p=P)),
                      (proj_raw[:], A["L1_ffn_w_proj"]), (u_raw[:], A["L1_ffn_u"].rearrange("(t p) r -> p t r", p=P)),
                      (v_raw[:], A["L1_ffn_v"]), (fast_raw[:], A["L1_ffn_fast_b"]),
                      (gate_col[:], A["L1_ffn_gate"].partition_broadcast(P)),
                      (u1[:], A["L2_ffn_U1"]), (v1r[:], A["L2_ffn_V1"]),
                      (u2[:], A["L2_ffn_U2"].rearrange("(t p) r -> p t r", p=P)), (v2r[:], A["L2_ffn_V2"]),
                      (rel_bias[:], A["L2_xattn_rel_bias"])]
            with nc.allow_non_contiguous_dma(reason="small bias vectors, a feature to a partition"):
                for n, layer in enumerate((0, 3)):
                    for t, k in ((bq, "bq"), (bk, "bk")):
                        for b in range(2):
                            ac.dma_start(t[b * 64:(b + 1) * 64, n, :],
                                         A[f"L{layer}_xattn_{k}"].rearrange("(h p) -> p h", h=2)).then_inc(ld_mask, 16)
                ac.dma_start(b1[:], A["L2_ffn_b1"].rearrange("(t p) -> p t", p=P)).then_inc(ld_mask, 16)
                for o, i in loads:
                    ac.dma_start(o, i).then_inc(ld_prep, 16)
            assert len(loads) == 24
            ac.wait_ge(ld_mask, 16 * 15)

            def ln_copy(cg):
                ac.wait_ge(a_lnp, cg + 1)
                if not (isinstance(cg, int) and cg == 0):
                    ac.wait_ge(a_qkp, cg)
                act(lnA[:, :], psL[:, 0:CH], ACT.Copy).then_inc(a_ln, 1)

            def qk_copy(a, n, cg, pair0):
                ac.wait_ge(a_qkp, cg + 1)
                if not (isinstance(cg, int) and cg < 2):
                    ac.wait_ge(a_sc, 2 * pair0 - 4)
                if not (isinstance(cg, int) and cg == 0):
                    ac.wait_ge(a_km, 2 * cg)
                q = psQ[:, 0:2 * P].rearrange("p (h u s) -> p h u s", h=2, u=2)
                k = psQ[:, 2 * P:4 * P].rearrange("p (h u s) -> p h u s", h=2, u=2)
                L = (0, None, 1)[a]
                for half in range(2):
                    for b in range(2):
                        r = slice(b * 64, b * 64 + 64)
                        act(q_diag[n][r, half, :, r], q[r, half], ACT.Identity,
                            bias=0.0 if L is None else bq[r, L, half:half + 1])
                    last = act(kT[:, half], k[:, half], ACT.Identity,
                               bias=0.0 if L is None else bk[:, L, half:half + 1])
                last.then_inc(a_q, 1)

            def v_high(n, cg, pair0):
                ac.wait_ge(a_v, cg + 1)
                if not (isinstance(cg, int) and cg < 2):
                    ac.wait_ge(a_pv, pair0 - 2)
                act(v_hi[n][:, :, :, :, 0:8].rearrange("p u b h d -> p (u b h) d"),
                    v_f32[:, :, :].rearrange("p c (h d) -> p (c h) d", d=8), ACT.Copy).then_inc(a_vhi, 1)

            def exponent(m, i):
                ac.wait_ge(a_sub, i + 1)
                act(sc[m], sc[m], ACT.Exp).then_inc(a_exp, 1)

            def p_high(i):
                for half in range(2):
                    ac.wait_ge(a_tr, 2 * i + half + 1)
                    if half == 0 and not (isinstance(i, int) and i == 0):
                        ac.wait_ge(a_pv, i)
                    act(p_hi[:, 4 * half:4 * half + 4, :].rearrange("p j t -> p (j t)"), psT[:, half, :],
                        ACT.Copy).then_inc(a_hi, 1)

            def cat_copy(i, ia):
                ac.wait_ge(a_ctp, ia + 1)
                act(catT[:, :], psC[:, 0:P], ACT.Copy).then_inc(a_ct, 1)

            def attention(a):
                def step(u, j, first=False, more=True, live=True):
                    i = 4 * j + u + 16 * a
                    c, n = 2 * j + u // 2 + 8 * a, u // 2
                    if live and u % 2 == 0 and more:
                        ln_copy(c + 1)
                    if not (first and u < 1):
                        exponent((u - 1) % 4, i - 1)
                    if not (first and u < 2):
                        p_high(i - 2)
                    if a and not (first and u < 3):
                        cat_copy(i - 3, i - 19)
                    if live and u % 2 == 1:
                        v_high(n, c, i - 1)
                    if live and u % 2 == 0 and more:
                        qk_copy(a, 1 - n, c + 1, i + 2)

                ln_copy(8 * a)
                qk_copy(a, 0, 8 * a, 16 * a)
                for u in range(4):
                    step(u, 0, first=True)
                with ac.Fori(1, 3) as j:
                    for u in range(4):
                        step(u, j)
                for u in range(4):
                    step(u, 3, more=(u < 2))
                for u in range(3):
                    i = 16 + u + 16 * a
                    if u < 1:
                        exponent((u - 1) % 4, i - 1)
                    if u < 2:
                        p_high(i - 2)
                    if a:
                        cat_copy(i - 3, i - 19)

            def ffn_ln(G, wait_read):
                ac.wait_ge(f_lnp, G + 1)
                wait_read()
                act(lnF[:, :], psL[:, :], ACT.Copy).then_inc(f_ln, 1)

            def ff_start(kind):
                f0 = GROUPS * FFN[kind]
                ffn_ln(f0, lambda: ac.wait_ge(f_x, f0) if f0 else None)

            def plain(kind):
                f0 = GROUPS * FFN[kind]
                up, read, hid, y = fs[kind]

                def group(g, last):
                    for f in range(FT):
                        ac.wait_ge(up, g * FT + (f + 1))
                        if f == 0 and not (isinstance(g, int) and g == 0):
                            ac.wait_ge(y, g)
                        if kind == "ffn1":
                            act(hT[:, f, :], psS[:, f % 2, :], ACT.Relu).then_inc(read, 1)
                        else:
                            act(hT[:, f, :], psS[:, f % 2, :], ACT.Gelu_apprx_tanh, bias=b1[:, f:f + 1]).then_inc(read, 1)
                    if not last:
                        ffn_ln(g + (f0 + 1), lambda: None)

                ff_start(kind)
                group(0, False)
                with ac.Fori(1, GROUPS - 1) as g:
                    group(g, False)
                group(GROUPS - 1, True)

            def linear():
                f0 = GROUPS * FFN["lin1"]
                y = fs["lin1"][3]
                ff_start("lin1")
                with ac.Fori(0, GROUPS - 1) as g:
                    ffn_ln(g + (f0 + 1), lambda: ac.wait_ge(y, g + 1))

            def blocks(kind):
                b0, nb = BLOCK0[kind], NBLOCKS[kind]

                def since(k, sm, v):
                    if not (isinstance(k, int) and k < 0):
                        ac.wait_ge(sm, v)

                def x_copy(q, b):
                    k = b + b0
                    ac.wait_ge(b_xt, k + 1)
                    since(k - 2, b_m1, k - 1)
                    act(xbT[q % 2], psQ[:, 0:P], ACT.Copy).then_inc(b_xc, 1)

                def activate(q, b):
                    k = b + b0
                    ac.wait_ge(b_m1, k + 1)
                    if kind == "moe0":
                        since(k - 2, b_t2, k - 1)
                        act(hb[q % 2], psS[:, q % 2, :], ACT.Gelu).then_inc(b_hd, 1)
                    else:
                        n = 4 * MC if kind == "shared" else MI
                        since(k - 2, b_hd, k - 1)
                        act(gated[q % 2][:, 0:n], psS[:, q % 2, 0:n], ACT.Silu).then_inc(b_sg, 1)

                def h_copy(q, b):
                    k = b + b0
                    ac.wait_ge(b_t2, k + 1)
                    since(k - 2, b_m2, k - 1)
                    n = (4 if kind == "shared" else 2) * P
                    act(hbT[q % 2][0:MC, 0:n], psH[q % 2][0:MC, 0:n], ACT.Copy).then_inc(b_hc, 1)

                def step(q, s, lo=-2, hi=None):
                    if hi is None or s + 2 < nb:
                        x_copy((q + 2) % NX, s + 2)
                    if lo >= -1 and (hi is None or s + 1 < nb):
                        activate((q + 1) % NX, s + 1)
                    if lo >= 0 and kind != "moe0" and (hi is None or s < nb):
                        h_copy(q, s)

                staggered(ac, nb, step)

            def moe(kind):
                f0, m = GROUPS * FFN[kind], MOE[kind]
                for g in range(GROUPS):
                    G, R = f0 + g, GROUPS * m + g
                    ac.wait_ge(f_lnp, G + 1)
                    if g == 0:
                        if f0:
                            ac.wait_ge(f_x, f0)
                    else:
                        ac.wait_ge(r_rt, R)
                    act(lnF[:, :], psL[:, :], ACT.Copy).then_inc(f_ln, 1)
                for h in range(TILES // RT_T):
                    R = TILES // RT_T * m + h
                    ac.wait_ge(r_top, R + 1)
                    if kind == "moe0":
                        act(psum8[:, :], top8[:, :, 0], ACT.Exp, scale=-1.0).then_inc(r_e, 1)
                    else:
                        act(prob[:, :, :], prob[:, :, :], ACT.Exp).then_inc(r_e, 1)
                        ac.wait_ge(f_xn, f0 + GROUPS // 2 * (h + 1))
                        ts = slice(RT_T * h, RT_T * (h + 1))
                        act(pay[:, ts, 1, 0:D], pay[:, ts, 0, 0:D], ACT.Copy).then_inc(r_dup, 1)
                if kind == "moe0":
                    for n in range(FIRST, len(JOBS)):
                        ac.wait_ge(setup_pe, n + 1)
                        JOBS[n][3](set_ps[n % 2]).then_inc(setup_ev, 1)
                        if NAMES[n] == "u1T":
                            ac.wait_ge(setup_ev, job_done("rel"))
                            ac.dma_start(rel_dram[:, :, 0:REL], rel_row[:, 0:REL].unsqueeze(1).broadcast_to([H, S, REL])).then_inc(rel_out, 16)
                        if NAMES[n] == "bias3":
                            ac.wait_ge(setup_ev, job_done("batch"))
                            ac.dma_start(batch_dram, per_batch[:, :]).then_inc(batch_out, 16)
                    ac.wait_ge(rel_out, 16)
                    skew = rel_dram.rearrange("h q j -> h (q j)")[:, 0:S * (P - 1)].rearrange("h (q j) -> q h j", j=P - 1)
                    for b in range(2):
                        ac.dma_start(bias2[b * S:(b + 1) * S], skew[:, :, S - 1:2 * S - 1]).then_inc(rel_in, 16)
                    ac.wait_ge(batch_out, 16)
                    for b in range(2):
                        ac.dma_start(tok_in[b * S:(b + 1) * S].rearrange("p (t d) -> p t d", t=TILES),
                                     batch_dram.rearrange("(t b) d -> b t d", b=2)[b].partition_broadcast(S)).then_inc(batch_in, 16)
                if kind == "moe3":
                    blocks("shared")
                blocks(kind)

            for ph in PHASES:
                if ph in ATT:
                    attention(ATT[ph])
                else:
                    {"plain": plain, "lin": lambda k: linear(), "moe": moe}[KIND[ph]](ph)

        @block.gpsimd
        def _(pool):
            nc.gpsimd.memset(minus_half[:], -0.5).then_inc(zeroed, 1)
            pool.wait_ge(zeroed, 1)
            pool.wait_ge(ld_const, 16 * 7)

            pool.wait_ge(ld_mask, 16 * 15)
            p8 = pad_words[:, :, :].rearrange("p t k -> p (t k)").bitcast(U8)
            nc.gpsimd.tensor_scalar(add3[:, :], p8, -3.0e38, 1.0e38, ALU.mult, ALU.mult).then_inc(pad_added, 1)
            a3 = add3[:, :].rearrange("p (t k) -> p t k", t=TILES)
            pool.wait_ge(pad_added, 1)
            nc.gpsimd.tensor_tensor(a3, a3, amask[:, :].unsqueeze(1).broadcast_to([P, TILES, S]), ALU.add).then_inc(pad_added, 1)

            def ln_rstd(stat, done, mv, rs, k, nt):
                wait_apart(pool, stat, k + 1)
                nc.gpsimd.tensor_scalar(rs[:, 0:nt, 0], mv[:, 0:nt, 1], EPS, 1.0, ALU.add, ALU.mult).then_inc(done, 1)
                pool.wait_ge(done, 2 * k + 1)
                nc.gpsimd.tensor_tensor(rs[:, 0:nt, 1], rs[:, 0:nt, 0], minus_half[:, 0:nt], ALU.pow).then_inc(done, 1)

            def subtract(m, i):
                pool.wait_ge(a_mx, i + 1)
                nc.gpsimd.tensor_tensor(sc[m], sc[m],
                                        mx[m][:, :].unsqueeze(2).broadcast_to([P, H, S]), ALU.subtract).then_inc(a_sub, 1)

            def key_heads(n, cg, pair0, part):
                if part == 0:
                    pool.wait_ge(a_q, cg + 1)
                    if not (isinstance(cg, int) and cg < 2):
                        wait_apart(pool, a_sc, 2 * pair0 - 4)
                for r in range(4 * part, 4 * part + 4):
                    last = nc.gpsimd.tensor_scalar(k_heads[n][:, :, :, r, :].rearrange("p h u s -> p (h u) s"),
                                                   kT[:, :, :, :].rearrange("p h u s -> p (h u) s"),
                                                   head_mask[:, r:r + 1], 1.0, ALU.mult, ALU.mult)
                last.then_inc(a_km, 1)

            def add_bias(c, cg, a):
                pool.wait_ge(a_xn, cg + 1)
                xs = x[:, ds(c * CH, CH)].rearrange("p (t d) -> p t d", t=2)
                nc.gpsimd.tensor_tensor(xs, xs, bias_out[:, a // 2, :].unsqueeze(1).broadcast_to([P, 2, D]), ALU.add).then_inc(a_xb, 1)

            def attention(a):
                def ln(cg):
                    ln_rstd(a_stat, a_rstd, mvA, rsA, cg, 2)

                def step(u, j, more=True):
                    i = 4 * j + u + 16 * a
                    c, n = 2 * j + u // 2, u // 2
                    if u % 2 == 1 and more:
                        key_heads(1 - n, c + (8 * a + 1), i + 1, 1)
                    subtract(u, i)
                    if u % 2 == 0 and more:
                        key_heads(1 - n, c + (8 * a + 1), i + 2, 0)
                    if u % 2 == 0 and more is True:
                        ln(c + (8 * a + 2))
                    if u % 2 == 1 and more is True and a != 1:
                        add_bias(c + 2, c + (8 * a + 2), a)

                if a == 0:
                    pool.wait_ge(setup_ev, job_done("bias0"))
                ln(8 * a)
                key_heads(0, 8 * a, 16 * a, 0)
                key_heads(0, 8 * a, 16 * a, 1)
                ln(8 * a + 1)
                if a != 1:
                    add_bias(0, 8 * a, a)
                    add_bias(1, 8 * a + 1, a)
                with pool.Fori(0, 3) as j:
                    for u in range(4):
                        step(u, j)
                for u in range(4):
                    step(u, 3, more="no ln" if u < 2 else False)

            def ffn_ln(g, G, bias):
                ln_rstd(f_stat, f_rstd, mvF, rsF, G, 4)
                if bias is not None:
                    pool.wait_ge(f_xn, G + 1)
                    xs = x[:, ds(g * GR, GR)]
                    if bias == "lin1":
                        nc.gpsimd.tensor_tensor(xs, xs, tok_in[:, ds(g * GR, GR)], ALU.add).then_inc(f_xb, 1)
                    else:
                        xs = xs.rearrange("p (t d) -> p t d", t=4)
                        nc.gpsimd.tensor_tensor(xs, xs, bias_out[:, 2, :].unsqueeze(1).broadcast_to([P, 4, D]), ALU.add).then_inc(f_xb, 1)

            def plain(kind):
                f0 = GROUPS * FFN[kind]
                if kind == "lin1":
                    pool.wait_ge(batch_in, 32)
                with pool.Fori(0, GROUPS) as g:
                    ffn_ln(g, g + f0, None if kind == "ffn1" else kind)

            def scatter(dst, places, src, s, limit):
                nc.gpsimd.indirect_dma_start(dst, bass.IndirectOffsetOnAxis(ap=places, axis=0), src, None,
                                             bounds_check=limit, oob_is_err=False).then_inc(s, 16)

            def moe(kind):
                f0, m = GROUPS * FFN[kind], MOE[kind]
                for g in range(GROUPS):
                    ts = slice(4 * g, 4 * g + 4)
                    ln_rstd(f_stat, f_rstd, mvM[:, ts], rsM[:, ts], f0 + g, 4)
                for h in range(TILES // RT_T):
                    send(kind, m, h)
                b0, nb = BLOCK0[kind], NBLOCKS[kind]
                with pool.Fori(0, nb // NX) as j:
                    for n in range(NX):
                        wait_apart(pool, b_ye, NX * j + (b0 + n + 1))
                        scatter(results, xin[n][:, D + 1:D + 2].bitcast(U32), yb[n], b_sc[n], 2 * TOK - 1)

            def send(kind, m, h):
                pool.wait_ge(r_slot, TILES // RT_T * m + h + 1)
                if kind == "moe3":
                    pool.wait_ge(r_dup, h + 1)
                for t in range(RT_T * h, RT_T * (h + 1)):
                    for c in range(CHOICES[kind]):
                        scatter(dispatched, slot[:, c, t:t + 1], pay[:, t, c, :], r_sent, E * REGION - 1)

            for ph in PHASES:
                if ph in ATT:
                    attention(ATT[ph])
                else:
                    {"plain": plain, "lin": plain, "moe": moe}[KIND[ph]](ph)

        tt, ts_, stt = nc.vector.tensor_tensor, nc.vector.tensor_scalar, nc.vector.scalar_tensor_tensor

        @block.vector
        def _(v):
            nc.vector.memset(ones[:], 1.0)
            nc.vector.memset(s_row[:], float(S))
            nc.vector.memset(pad_row[:], 0.0)
            for n in range(2):
                nc.vector.memset(q_diag[n][:], 0.0)
                nc.vector.memset(cat[n][:], 0.0)
                nc.vector.memset(v_hi[n][:], 0.0)
                nc.vector.memset(v_lo[n][:], 0.0).then_inc(zeroed_v, 1)
            v.wait_ge(zeroed_v, 2)
            v.wait_ge(ld_const, 16 * 7)
            for n in range(2):
                nc.vector.tensor_copy(v_hi[n][:, :, :, :, 8].rearrange("p u b h -> p (u b) h"),
                                      dup_mask[:, 0:P:8].unsqueeze(1).broadcast_to([P, 4, H])).then_inc(zeroed_v, 1)
            nc.vector.tensor_copy(pad_row[:, D + 1:D + 2].bitcast(U32), place_tab[:, 2 * TILES:2 * TILES + 1]).then_inc(pad_ready, 1)
            for c in range(2):
                nc.vector.tensor_copy(pay[:, :, c, D + 1].bitcast(U32), place_tab[:, c * TILES:(c + 1) * TILES])
            v.wait_ge(ld_mask, 16 * 15)
            v.wait_ge(ld_x, 16)

            def own(ins):
                chain[0] += 1
                ins.then_inc(dve_prep, 1)
                v.wait_ge(dve_prep, chain[0])
            chain = [0]
            m8 = mask_words[:, :, :].rearrange("p t k -> p (t k)").bitcast(U8)
            ts_(cap0[:, :], m8, 3.0e38, NEG, ALU.mult, ALU.add).then_inc(cap_ready, 1)

            v.wait_ge(ld_a0, 16 * 9)
            nc.vector.tensor_copy(bv_twice.rearrange("p h (b s) -> p h b s", b=2),
                                  bv_row[:, :].rearrange("p (s h) -> p h s", h=2).unsqueeze(2).broadcast_to([P, 2, 2, 64]))\
              .then_inc(bv_ready, 1)

            for n in range(FIRST):
                v.wait_ge(setup_pe, n + 1)
                JOBS[n][3](set_ps[n % 2]).then_inc(setup_ev, 1)

            def bitlinear(w, s, n, width, out):
                w3 = w.rearrange("p (n d) -> p n d", n=n)
                own(nc.vector.tensor_reduce(s[:, 0:n], w3, axis=AX_X, op=ALU.add, apply_absolute_value=True))
                own(ts_(s[:, 0:n], s[:, 0:n], 1.0 / width, 1e-5, ALU.mult, ALU.max))
                own(ts_(s[:, 4:4 + n], s[:, 0:n], 0.5, None, ALU.mult))
                half = s[:, 4:4 + n].unsqueeze(2).broadcast_to([P, n, width])
                t3 = hT[:, 1, :].rearrange("p (n d) -> p n d", n=n)
                c3 = hT[:, 0, :].rearrange("p (n d) -> p n d", n=n)
                own(tt(t3, w3, half, ALU.is_gt))
                own(stt(c3, w3, -1.0, half, ALU.mult, ALU.is_gt))
                own(tt(t3, t3, c3, ALU.subtract))
                own(tt(t3, t3, w3, ALU.subtract))
                own(tt(t3, t3, w3, ALU.add))
                tt(out.rearrange("p (n d) -> p n d", n=n), t3, s[:, 0:n].unsqueeze(2).broadcast_to([P, n, width]),
                   ALU.mult).then_inc(tern_ready, 1)

            def ternary_weights():
                bitlinear(fc_raw[:, :, :].rearrange("p a b -> p (a b)"), row_scale, FT, P,
                          tern[:, :, :].rearrange("p a b -> p (a b)"))
                v.wait_ge(tern_ready, 1)
                bitlinear(proj_raw[:, :], row_scale, 1, FF, proj_raw[:, :])

            def stats(xs, nt, st, mv, stat, k, busy):
                for t in range(nt):
                    last = nc.vector.bn_stats(st[:, t, :], xs(t))
                last.then_inc(stat[0], 1)
                busy()
                wait_apart(v, stat[0], k + 1)
                for t in range(nt):
                    last = nc.vector.bn_aggr(mv[:, t, :], st[:, t, :])
                last.then_inc(stat[1], 1)

            def normalise(xs, nt, xn, mv, rs, rstd, k, done):
                v.wait_ge(rstd, 2 * k + 2)
                for t in range(nt):
                    last = ts_(xn[:, t, :], xs(t), mv[:, t, 0:1], rs[:, t, 1:2], ALU.subtract, ALU.mult)
                last.then_inc(done, 1)

            def a_stats(c, cg):
                stats(lambda t: x[:, ds(c * CH + t * D, D)], 2, stA, mvA, (a_bn, a_stat), cg,
                      lambda: None if isinstance(cg, int) and cg == 0 else v.wait_ge(a_xn, cg))

            def a_normalise(c, cg):
                if not (isinstance(cg, int) and cg == 0):
                    v.wait_ge(a_lnp, cg)
                normalise(lambda t: x[:, ds(c * CH + t * D, D)], 2, xnA, mvA, rsA, a_rstd, cg, a_xn)

            def evacuate(a, m, i, ii):
                if not (isinstance(i, int) and i < 4):
                    v.wait_ge(a_tr, 2 * i - 6)
                if a == 2:
                    v.wait_ge(a_side[m], 32 * (i - 32 - m) // 4 + 32 if isinstance(i, int) else (i - (32 + m)) * 8 + 32)
                    stt(side[m], side[m], 2.0,
                        add3[:, ds(ii * S, S)].unsqueeze(1).broadcast_to([P, H, S]), ALU.mult, ALU.add).then_inc(a_sidef, 1)
                    v.wait_ge(a_sidef, i - 31)
                for half in range(2):
                    v.wait_ge(a_sc, 2 * i + half + 1)
                    o = sc[m][:, 8 * half:8 * half + 8, :]
                    s = psS[:, half, :].rearrange("p (h k) -> p h k", h=8)
                    if a == 0:
                        r = stt(o, s, QK_SCALE, cap0[:, ds(ii * S, S)].unsqueeze(1).broadcast_to([P, 8, S]), ALU.mult, ALU.min)
                    elif a == 1:
                        r = tt(o, s, bias2[:, 8 * half:8 * half + 8, :], ALU.add)
                    else:
                        r = stt(o, s, QK_SCALE, side[m][:, 8 * half:8 * half + 8, :], ALU.mult, ALU.add)
                    r.then_inc(a_ev, 1)
                v.wait_ge(a_ev, 2 * i + 2)
                if not (isinstance(i, int) and i < 4):
                    v.wait_ge(a_sub, i - 3)
                nc.vector.reduce_max(mx[m][:, :], sc[m], axis=AX_X).then_inc(a_mx, 1)

            def values(n, cg):
                v.wait_ge(a_vp, cg + 1)
                if not (isinstance(cg, int) and cg == 0):
                    v.wait_ge(a_vhi, cg)
                tt(v_f32[:, :, :], psQ[:, :].rearrange("p (c d) -> p c d", c=4),
                   dup_mask[:, :].unsqueeze(1).broadcast_to([P, 4, D]), ALU.mult).then_inc(a_v, 1)

            def v_low(n, cg, pair0):
                v.wait_ge(a_vhi, cg + 1)
                if not (isinstance(cg, int) and cg < 2):
                    v.wait_ge(a_pv, pair0 - 2)
                tt(v_lo[n][:, :, :, :, 0:8].rearrange("p u b h d -> p (u b h) d"),
                   v_f32[:, :, :].rearrange("p c (h d) -> p (c h) d", d=8),
                   v_hi[n][:, :, :, :, 0:8].rearrange("p u b h d -> p (u b h) d"), ALU.subtract).then_inc(a_vlo, 1)

            def p_low(i):
                for half in range(2):
                    v.wait_ge(a_hi, 2 * i + half + 1)
                    if half == 0 and not (isinstance(i, int) and i == 0):
                        v.wait_ge(a_pv, i)
                    r = slice(4 * half, 4 * half + 4)
                    tt(p_lo[:, r, :].rearrange("p j t -> p (j t)"), psT[:, half, :],
                       p_hi[:, r, :].rearrange("p j t -> p (j t)"), ALU.subtract).then_inc(a_lo, 1)

            def concat(a, m, i, ia):
                v.wait_ge(a_pv, i + 1)
                if not (isinstance(i, int) and i < 2):
                    v.wait_ge(a_out, i - 1)
                o = psO[:, 0:2 * H * 9].rearrange("p (b h e) -> p b h e", b=2, h=H)
                for b in range(2):
                    r = slice(b * 64, b * 64 + 64)
                    last = nc.vector.reciprocal(rsum[r, :], o[r, b, :, 8])
                last.then_inc(a_rs, 1)
                v.wait_ge(a_rs, i + 1)
                for b in range(2):
                    r = slice(b * 64, b * 64 + 64)
                    if a == 0:
                        dst = cat[m][r, :, r].rearrange("p h2 (h d2) -> p h d2 h2", h=H)
                        src = o[r, b, :, 0:8].rearrange("p h (d2 h2) -> p h d2 h2", h2=2)
                        rr = rsum[r, :].unsqueeze(2).unsqueeze(3).broadcast_to([64, H, 4, 2])
                    else:
                        dst = cat[m][r, 0, :].rearrange("p (h d) -> p h d", h=H)
                        src = o[r, b, :, 0:8]
                        rr = rsum[r, :].unsqueeze(2).broadcast_to([64, H, 8])
                    last = tt(dst, src, rr, ALU.mult)
                last.then_inc(a_cat, 1)

            def residual(a, i, ii, cg):
                v.wait_ge(a_out, i + 1)
                if a != 1:
                    v.wait_ge(a_xb, cg + (1 if a == 0 else -7))
                xs = x[:, ds(ii * D, D)]
                tt(xs, xs, psC[:, P:2 * P], ALU.add).then_inc(a_x, 1)

            def attention(a):
                def step(u, j, first=False, more=True, live=True):
                    ii = 4 * j + u
                    i = ii + 16 * a
                    c, n = 2 * j + u // 2, u // 2
                    cg = c + 8 * a
                    if live:
                        evacuate(a, u, i, ii)
                    if not (first and u < 2):
                        p_low(i - 2)
                    if not (first and u < 3):
                        residual(a, i - 3, ii - 3, cg - 2 + u % 2)
                    if live and u % 2 == 1:
                        values(n, cg)
                        if more:
                            a_normalise(c + 2, cg + 2)
                    if live and u % 2 == 0 and more:
                        wait_x(c + 2)
                        a_stats(c + 2, cg + 2)
                    if not (first and u < 2):
                        concat(a, u % 2, i - 2, None)
                    if live and u % 2 == 1:
                        v_low(n, cg, i - 1)

                def wait_x(c):
                    if a:
                        f = GROUPS * (F_BEFORE[(0, 2, 3)[a]] - 1)
                        v.wait_ge(f_x, c // 2 + f + 1 if isinstance(c, int) else FXJ[0] + (f + 2))

                if a == 0:
                    v.wait_ge(cap_ready, 1)
                if a == 1:
                    v.wait_ge(rel_in, 32)
                if a == 2:
                    v.wait_ge(pad_added, 2)
                for c in range(2):
                    if a:
                        v.wait_ge(f_x, GROUPS * (F_BEFORE[(0, 2, 3)[a]] - 1) + 1)
                    a_stats(c, 8 * a + c)
                    a_normalise(c, 8 * a + c)
                for u in range(4):
                    step(u, 0, first=True)
                with v.Fori(1, 3) as j:
                    FXJ[0] = j
                    for u in range(4):
                        step(u, j)
                for u in range(4):
                    step(u, 3, more=False)
                for u in range(3):
                    step(u, 4, live=False) if u < 2 else residual(a, 15 + 16 * a, 15, 8 * a + 7)

            FXJ = [0]

            def x_tile(g):
                return lambda t: x[:, ds(g * GR + t * D, D)]

            def f_stats(g, G, prev):
                prev(g)
                stats(x_tile(g), 4, stF, mvF, (f_bn, f_stat), G,
                      lambda: None if isinstance(G, int) and G == 0 else v.wait_ge(f_xn, G))

            def f_normalise(g, G):
                if not (isinstance(G, int) and G == 0):
                    v.wait_ge(f_lnp, G)
                normalise(x_tile(g), 4, xnF, mvF, rsF, f_rstd, G, f_xn)

            def before_phase(kind):
                if kind in F_AFTER_A:
                    k = 16 * (F_AFTER_A[kind] - 1)
                    return lambda g: v.wait_ge(a_x, g * 4 + (k + 4))
                k = GROUPS * (FFN[kind] - 1)
                return lambda g: v.wait_ge(f_x, g + (k + 1))

            def plain(kind):
                f0 = GROUPS * FFN[kind]
                _, read, hid, y = fs[kind]
                prev = before_phase(kind)

                def group(g, last):
                    if not last:
                        f_stats(g + 1, g + (f0 + 1), prev)
                    for f in range(FT):
                        if kind == "ffn1":
                            v.wait_ge(read, g * FT + (f + 1))
                            tt(hT[:, f, :], hT[:, f, :], hT[:, f, :], ALU.mult).then_inc(hid, 1)
                        if f == 1 and not last:
                            f_normalise(g + 1, g + (f0 + 1))
                    v.wait_ge(y, g + 1)
                    if kind != "ffn1":
                        v.wait_ge(f_xb, g + (GROUPS * (kind == "ffn2") + 1))
                    xs = x[:, ds(g * GR, GR)]
                    tt(xs, xs, psT[:, 0, :], ALU.add).then_inc(f_x, 1)

                f_stats(0, f0, prev)
                f_normalise(0, f0)
                with v.Fori(0, GROUPS - 1) as g:
                    group(g, False)
                group(GROUPS - 1, True)

            def route(kind, h, R):
                n = CHOICES[kind]
                ts = slice(RT_T * h, RT_T * (h + 1))
                v.wait_ge(r_rt, GROUPS * MOE[kind] + GROUPS // 2 * (h + 1))
                lg = psR[h][:, RT_T * E * h:RT_T * E * (h + 1)].rearrange("p (t e) -> p t e", t=RT_T)
                if kind == "moe0":
                    own(tt(logit[:, :, :], lg, br0[:, :].unsqueeze(1).broadcast_to([P, RT_T, E]), ALU.add))
                    own(ts_(logit[:, :, :], logit[:, :, :], SATURATED, None, ALU.min))
                else:
                    own(nc.vector.tensor_copy(logit[:, :, :], lg))
                for t in range(RT_T):
                    last = nc.vector.max(top8[:, t, :], logit[:, t, :])
                if kind == "moe0":
                    last.then_inc(r_top, 1)
                    v.wait_ge(r_top, R + 1)
                else:
                    own(last)
                    tt(prob[:, :, :], top8[:, :, :], top8[:, :, 0:1].broadcast_to([P, RT_T, E]), ALU.subtract).then_inc(r_top, 1)
                for t in range(RT_T):
                    last = nc.vector.max_index(idx8[:, t, :], top8[:, t, :], logit[:, t, :])
                own(last)
                own(nc.vector.tensor_copy(idxf[:, 0:n, :].rearrange("p c t -> p t c"), idx8[:, :, 0:n]))
                for c in range(n):
                    last = tt(chosen[:, c, :, :], tab("iota").unsqueeze(1).broadcast_to([P, RT_T, E]),
                              idxf[:, c, :].unsqueeze(2).broadcast_to([P, RT_T, E]), ALU.is_equal)
                own(last)
                if n == 2:
                    tt(counted[:, :, :], chosen[:, 0], chosen[:, 1], ALU.add).then_inc(r_oh, 1)
                else:
                    nc.vector.tensor_copy(counted[:, :, :], chosen[:, 0]).then_inc(r_oh, 1)
                v.wait_ge(r_e, R + 1)
                if kind == "moe0":
                    own(ts_(psum8[:, :], psum8[:, :], 1.0, None, ALU.add))
                    own(nc.vector.reciprocal(pay[:, ts, 0, D], psum8[:, :]))
                else:
                    own(nc.vector.reduce_sum(psum8[:, :], prob[:, :, :], axis=AX_X))
                    own(nc.vector.reciprocal(psum8[:, :], psum8[:, :]))
                    own(tt(pw[:, :, :], prob[:, :, 0:2], psum8[:, :].unsqueeze(2).broadcast_to([P, RT_T, 2]), ALU.mult))
                    own(nc.vector.reduce_sum(psum8[:, :], pw[:, :, :], axis=AX_X))
                    own(ts_(psum8[:, :], psum8[:, :], 1e-20, None, ALU.add))
                    own(nc.vector.reciprocal(psum8[:, :], psum8[:, :]))
                    own(tt(pay[:, ts, :, D], pw[:, :, :], psum8[:, :].unsqueeze(2).broadcast_to([P, RT_T, 2]), ALU.mult))
                if h == 0:
                    own(nc.vector.tensor_copy(run[:, :], tab("base")))
                v.wait_ge(r_cnt, R + 1)
                own(tt(place[:, :, :], psQ[:, 0:RT_T * E].rearrange("p (t e) -> p t e", t=RT_T),
                       run[:, :].unsqueeze(1).broadcast_to([P, RT_T, E]), ALU.add))
                own(tt(run[:, :], run[:, :], psQ[:, RT_T * E:(RT_T + 1) * E], ALU.add))
                for c in range(n):
                    last = tt(spot[:, c], chosen[:, c], place[:, :, :], ALU.mult)
                own(last)
                own(nc.vector.reduce_sum(slotf[:, 0:n, :], spot[:, 0:n], axis=AX_X))
                nc.vector.tensor_copy(slot[:, 0:n, ts], slotf[:, 0:n, :]).then_inc(r_slot, 1)

            def block_table(kind, m):
                nb = NBLOCKS[kind]
                nc.vector.tensor_copy(tail[:, :], run[:, :]).then_inc(r_end, 1)
                own(tt(cnt[:, :], run[:, :], tab("base"), ALU.subtract))
                own(tt(cmp8[:, 0:TILES, :], cnt[:, :].unsqueeze(1).broadcast_to([P, TILES, E]),
                       tab("k128").unsqueeze(2).broadcast_to([P, TILES, E]), ALU.is_gt))
                own(nc.vector.reduce_sum(nblk[:, :], cmp8[:, 0:TILES, :].rearrange("p k e -> p e k"), axis=AX_X))
                own(tt(cmp8[:, 0:E, :], nblk[:, :].unsqueeze(1).broadcast_to([P, E, E]),
                       tab("le").rearrange("p (e f) -> p e f", e=E), ALU.mult))
                own(nc.vector.reduce_sum(cumb[:, :], cmp8[:, 0:E, :], axis=AX_X))
                own(tt(cmp8[:, 0:nb, :], cumb[:, :].unsqueeze(1).broadcast_to([P, nb, E]),
                       tab("k")[:, 0:nb].unsqueeze(2).broadcast_to([P, nb, E]), ALU.is_le))
                own(nc.vector.reduce_sum(blkf[:, 1, 0:nb], cmp8[:, 0:nb, :], axis=AX_X))
                own(tt(cmp8[:, 0:nb, :], cmp8[:, 0:nb, :], nblk[:, :].unsqueeze(1).broadcast_to([P, nb, E]), ALU.mult))
                own(nc.vector.reduce_sum(blkf[:, 0, 0:nb], cmp8[:, 0:nb, :], axis=AX_X))
                own(tt(blkf[:, 0, 0:nb], tab("k")[:, 0:nb], blkf[:, 0, 0:nb], ALU.subtract))
                own(ts_(blkf[:, 0, 0:nb], blkf[:, 0, 0:nb], float(P), None, ALU.mult))
                own(stt(blkf[:, 0, 0:nb], blkf[:, 1, 0:nb], float(REGION), blkf[:, 0, 0:nb], ALU.mult, ALU.add))
                own(ts_(blkf[:, 0, 0:nb], blkf[:, 0, 0:nb], float(E * REGION), None, ALU.min))
                own(ts_(blkf[:, 1, 0:nb], blkf[:, 1, 0:nb], float(E - 1), None, ALU.min))
                nc.vector.tensor_copy(blk[:, :, 0:nb], blkf[:, :, 0:nb]).then_inc(r_tab, 1)

            def blocks(kind):
                b0, nb = BLOCK0[kind], NBLOCKS[kind]

                def since(k, sm, val):
                    if not (isinstance(k, int) and k < 0):
                        v.wait_ge(sm, val)

                def h_copy(q, b):
                    k = b + b0
                    v.wait_ge(b_t2, k + 1)
                    since(k - 2, b_m2, k - 1)
                    nc.vector.tensor_copy(hbT[q % 2], psH[q % 2][:, :]).then_inc(b_hc, 1)

                def gate(q, b):
                    k = b + b0
                    v.wait_ge(b_sg, k + (1 - BLOCK0["shared"]))
                    since(k - 2, b_t2, k - 1)
                    n = 4 * MC if kind == "shared" else MI
                    up = psT[:, q % 2, 0:n] if kind == "shared" else psS[:, q % 2, MI:2 * MI]
                    tt(hb[q % 2][:, 0:n], gated[q % 2][:, 0:n], up, ALU.mult).then_inc(b_hd, 1)

                def result(q, b):
                    k = b + b0
                    v.wait_ge(b_m2, k + 1)
                    if kind == "shared":
                        xs = x[:, ds(b * D, D)]
                        tt(xs, xs, psC[:, 0:D], ALU.add).then_inc(b_ye, 1)
                    else:
                        ts_(yb[q], psC[:, 0:D], xin[q][:, D:D + 1], None, ALU.mult).then_inc(b_ye, 1)

                def step(q, s, lo=-2, hi=None):
                    if kind == "moe0" and lo >= 0 and (hi is None or s < nb):
                        h_copy(q, s)
                    if kind != "moe0" and lo >= -1 and (hi is None or s + 1 < nb):
                        gate((q + 1) % NX, s + 1)
                    if lo >= 1:
                        result((q - 1) % NX, s - 1)

                staggered(v, nb, step)

            def moe(kind):
                f0, m = GROUPS * FFN[kind], MOE[kind]
                prev = before_phase(kind)

                def statistics(g):
                    ts = slice(4 * g, 4 * g + 4)
                    prev(g)
                    stats(x_tile(g), 4, stM[:, ts], mvM[:, ts], (f_bn, f_stat), f0 + g, lambda: None)

                def normal(g):
                    v.wait_ge(f_rstd, 2 * (f0 + g) + 2)
                    xs = x_tile(g)
                    for t in range(4 * g, 4 * g + 4):
                        last = ts_(pay[:, t, 0, 0:D], xs(t - 4 * g), mvM[:, t, 0:1], rsM[:, t, 1:2], ALU.subtract, ALU.mult)
                    last.then_inc(f_xn, 1)

                if m:
                    v.wait_ge(f_x, GROUPS)
                    for c in range(2):
                        last = nc.vector.tensor_copy(pay[:, :, c, D + 1].bitcast(U32), place_tab[:, c * TILES:(c + 1) * TILES])
                    own(last)
                statistics(0)
                for g in range(GROUPS):
                    if g + 1 < GROUPS:
                        statistics(g + 1)
                    normal(g)
                for h in range(TILES // RT_T):
                    route(kind, h, TILES // RT_T * m + h)
                block_table(kind, m)
                if kind == "moe0":
                    v.wait_ge(ld_prep, 16 * 24)
                    ternary_weights()
                if kind == "moe3":
                    blocks("shared")
                blocks(kind)
                for g in range(GROUPS):
                    n = CHOICES[kind]
                    v.wait_ge(b_res[g], 16 * (1 if kind == "moe0" else 1 + n))
                    xs = x[:, g * GR:(g + 1) * GR]
                    if n == 2:
                        own(tt(xs, xs, pay_row[:, TOK + g * GR:TOK + (g + 1) * GR], ALU.add))
                    tt(xs, xs, pay_row[:, g * GR:(g + 1) * GR], ALU.add).then_inc(f_x, 1)


            for ph in PHASES:
                if ph in ATT:
                    attention(ATT[ph])
                else:
                    {"plain": plain, "lin": plain, "moe": moe}[KIND[ph]](ph)


_INS = ['x', 'ctx_1024', 'fside_Bx16xSxS2_0', 'fside_SxS2_0', 'mask_BxSxS2_bf1', 'mask_BxS2_bf0',
        'L0_xattn_Wq', 'L0_xattn_bq', 'L0_xattn_Wk', 'L0_xattn_bk', 'L0_xattn_Wv', 'L0_xattn_bv', 'L0_xattn_Wo',
        'L0_xattn_bo', 'L0_ffn_Wr', 'L0_ffn_br', 'L0_ffn_W1', 'L0_ffn_W2', 'L1_xattn_W', 'L1_xattn_b',
        'L1_ffn_fast_b', 'L1_ffn_w_fc', 'L1_ffn_w_proj', 'L1_ffn_u', 'L1_ffn_v', 'L1_ffn_gate', 'L2_xattn_Wq',
        'L2_xattn_Wkv', 'L2_xattn_Wo', 'L2_xattn_rel_bias', 'L2_ffn_U1', 'L2_ffn_V1', 'L2_ffn_b1', 'L2_ffn_U2',
        'L2_ffn_V2', 'L2_ffn_b2', 'L3_xattn_Wq', 'L3_xattn_bq', 'L3_xattn_Wk', 'L3_xattn_bk', 'L3_xattn_Wv',
        'L3_xattn_bv', 'L3_xattn_Wo', 'L3_xattn_bo', 'L3_ffn_gate_w', 'L3_ffn_wg', 'L3_ffn_wu', 'L3_ffn_wd',
        'L3_ffn_swg', 'L3_ffn_swu', 'L3_ffn_swd']


def constants():
    part = np.arange(P)
    rel = np.arange(-(S - 1), S)
    nb, exact = BUCKETS // 2, BUCKETS // 4
    dist = np.maximum(np.abs(rel), 1).astype(np.float32)
    large = exact + (np.log(dist / np.float32(exact)) / np.float32(np.log(128 / exact)) * np.float32(nb - exact)).astype(np.int32)
    bucket = (rel > 0) * nb + np.where(np.abs(rel) < exact, np.abs(rel), np.minimum(large, nb - 1))
    f = np.float32
    return {
        "ident": np.eye(P, dtype=f),
        "head_mask": (part[:, None] % 64 // DH == np.arange(8)[None, :]).astype(f),
        "dup_mask": (part[:, None] // 64 == part[None, :] // DH % 2).astype(f),
        "route_tab": np.concatenate([
            np.broadcast_to(t.astype(f).ravel(), (P, t.size)) for t in (
                np.arange(E), np.arange(E) * REGION, np.arange(TILES) * P,
                np.arange(E)[None, :] <= np.arange(E)[:, None], np.arange(40))] + [part[:, None].astype(f)], axis=1),
        "place_tab": np.concatenate([part[:, None] + P * np.arange(2 * TILES)[None, :],
                                     np.full((P, 1), NOWHERE)], axis=1).astype(np.uint32),
        "before": (part[:, None] < part[None, :]).astype(np.float16),
        "rel_onehot": (np.arange(BUCKETS)[:, None] == bucket[None, :]).astype(f),
    }


def kernel(**inputs):
    import concourse.bacc as bacc
    from concourse.bass_utils import run_bass_kernel_spmd

    nc = bacc.Bacc("TRN2", target_bir_lowering=False, num_devices=1)
    arrays, args, consts = {}, {}, {}
    for name in _INS:
        a = np.ascontiguousarray(inputs[name])
        if a.ndim == 0:
            a = a.reshape(1)
        if a.dtype == np.bool_:
            a = a.view(np.uint32)
        arrays["in_" + name] = a
        args[name] = nc.dram_tensor("in_" + name, a.shape, mybir.dt.from_np(a.dtype), kind="ExternalInput").ap()
    for name, a in constants().items():
        arrays["const_" + name] = a
        consts[name] = nc.dram_tensor("const_" + name, a.shape, mybir.dt.from_np(a.dtype), kind="ExternalInput").ap()
    out = nc.dram_tensor("out_x", (B, S, D), F32, kind="ExternalOutput").ap()
    bass_transformer(nc, args, consts, out)
    r = run_bass_kernel_spmd(nc, [arrays], core_ids=[0])
    return r.results[0]["out_x"]
```

```python
from contextlib import ExitStack

import numpy as np

import concourse.bass as bass
from concourse import mybir

ALU = mybir.AluOpType
ACT = mybir.ActivationFunctionType
AX_X = mybir.AxisListType.X
F32 = mybir.dt.float32
F16 = mybir.dt.float16
U8 = mybir.dt.uint8
U32 = mybir.dt.uint32
ds = bass.ds

P = 128
B, S, D = 32, 64, 128
H, DH = 16, 8
TILES = B * S // P
CH = 2 * P
GR = 4 * P
GROUPS = TILES // 4
FF = 512
FT = FF // P
E = 8
MI = 176
MC = 88
EPS = 1e-5
QK_SCALE = float(DH) ** -0.5
NEG = -1e9
SATURATED = 16.635532
BUCKETS = 32
REL = 2 * S - 1
TOK = B * S
REGION = TOK + P
ROW = D + 2
RT_T = 8
NX = 8
NOWHERE = 1 << 20
RT = {"iota": (0, E), "base": (8, E), "k128": (16, TILES), "le": (32, E * E), "k": (96, 40), "part": (136, 1)}


PHASES = [0, "moe0", "ffn1", 2, "ffn2", 3, "moe3"]


def bass_transformer(nc, A, K, out):
    ctx = ExitStack()
    with ctx:
        def sb(name, shape, dt=F32):
            return ctx.enter_context(nc.sbuf_tensor(name, shape, dt))

        def sem(name):
            return ctx.enter_context(nc.semaphore(name))

        def row(ap):
            return ap.rearrange("(a n) -> a n", a=1)

        first_tab = sb("first_tab", [P, 2 * P + 8])
        ident = first_tab[:, 0:P]
        dup_mask = first_tab[:, P:2 * P]
        head_mask = first_tab[:, 2 * P:2 * P + 8]
        route_tab = sb("route_tab", [P, 137])
        place_tab = sb("place_tab", [P, 2 * TILES + 1], U32)
        before = sb("before", [P, P], F16)
        ones = sb("ones", [P, P], F16)
        rel_onehot = sb("rel_onehot", [BUCKETS, REL + 1])
        minus_half = sb("minus_half", [P, 4])
        x = sb("x", [P, TILES * D])
        ctxT = sb("ctxT", [P, B * S])
        tok_in = sb("tok_in", [P, TILES * D])
        wqk0 = sb("wqk0", [P, 3, D])
        wo0 = sb("wo0", [P, 2, D])
        wqkv2 = sb("wqkv2", [P, 3, D])
        wo2 = sb("wo2", [P, D])
        wraw3 = sb("wraw3", [P, 4, D])
        w3T = sb("w3T", [P, 4, D])
        w1raw = sb("w1raw", [P, 2 * D])
        w1T = sb("w1T", [P, 2, D])
        bq = sb("bq", [P, 2, 2])
        bk = sb("bk", [P, 2, 2])
        bv_row = sb("bv_row", [P, D])
        bv_col = sb("bv_col", [P, 1])
        bias_out = sb("bias_out", [P, 4, D])
        router0 = sb("router0", [P, E])
        br0 = sb("br0", [P, E])
        gate3 = sb("gate3", [E, D])
        gate3T = sb("gate3T", [P, E])
        expert_w = sb("expert_w", [P, 2 * E * FF])
        e_up = expert_w[:, 0:E * FF].rearrange("p (e f) -> p e f", e=E)
        e_down = expert_w[:, E * FF:2 * E * FF].rearrange("p (e t d) -> p e t d", e=E, t=FT)

        def carve(at, parts, *shape):
            n = int(np.prod(shape))
            v = expert_w[0:parts, at:at + n]
            return v.rearrange("p (a b) -> p a b", a=shape[0]) if len(shape) == 2 else v, at + n
        m_gu, at = carve(0, P, E, 2 * MI)
        m_down, at = carve(at, MC, 2 * E, D)
        s_gu, at = carve(at, P, 2, 4 * MC)
        s_down, at = carve(at, MC, 4, D)
        fc_raw = sb("fc_raw", [P, FT, D])
        proj_raw = sb("proj_raw", [P, FF])
        u_raw = sb("u_raw", [P, FT, 16])
        v_raw = sb("v_raw", [16, D])
        fast_raw = sb("fast_raw", [16, 16])
        fastT = sb("fastT", [16, 16])
        uT = sb("uT", [16, FF])
        fast_v = sb("fast_v", [16, D])
        gate_col = sb("gate_col", [P, 1])
        tern = sb("tern", [P, FT, P])
        row_scale = sb("row_scale", [P, 8])
        w1eff = sb("w1eff", [P, FF])
        w1out = sb("w1out", [P, FT, D])
        u1 = sb("u1", [P, 32])
        u1T = sb("u1T", [32, D])
        v1r = sb("v1r", [32, FF])
        u2 = sb("u2", [P, FT, 32])
        u2T = sb("u2T", [32, FF])
        v2r = sb("v2r", [32, D])
        b1 = sb("b1", [P, FT])
        w2in = sb("w2in", [P, FF])
        w2out = sb("w2out", [P, FT, D])
        rel_bias = sb("rel_bias", [BUCKETS, H])
        rel_row = sb("rel_row", [H, P])
        ctx_sum = sb("ctx_sum", [P, B])
        s_row = sb("s_row", [1, B])
        per_batch = sb("per_batch", [B, D])
        mask_words = sb("mask_words", [P, TILES, S // 4], U32)
        pad_words = sb("pad_words", [P, TILES, S // 4], U32)
        cap0 = sb("cap0", [P, TILES * S])
        add3 = sb("add3", [P, TILES * S])
        amask = sb("amask", [P, S])
        bias2 = sb("bias2", [P, H, S])

        xnA = sb("xnA", [P, 2, D])
        lnA = sb("lnA", [P, CH])
        stA = sb("stA", [P, 2, 6])
        mvA = sb("mvA", [P, 2, 2])
        rsA = sb("rsA", [P, 2, 2])
        ctxc = [sb(f"ctxc{n}", [P, 4, 2, S]) for n in range(2)]
        q_diag = [sb(f"q_diag{n}", [P, 2, 2, P]) for n in range(2)]
        kT = sb("kT", [P, 2, 2, S])
        k_heads = [sb(f"k_heads{n}", [P, 2, 2, 8, S]) for n in range(2)]
        v_hi = [sb(f"v_hi{n}", [P, 2, 2, H, 9], F16) for n in range(2)]
        v_lo = [sb(f"v_lo{n}", [P, 2, 2, H, 9], F16) for n in range(2)]
        work = sb("work", [P, 4 * H * S])
        sc = [work[:, n * H * S:(n + 1) * H * S].rearrange("p (h k) -> p h k", h=H) for n in range(4)]
        pay = sb("pay", [P, TILES, 2, ROW])
        pay_row = pay[:, :, :, :].rearrange("p t c r -> p (t c r)")
        side = [pay_row[:, n * H * S:(n + 1) * H * S].rearrange("p (h k) -> p h k", h=H) for n in range(4)]
        mx = [sb(f"mx{n}", [P, H]) for n in range(4)]
        p_hi = sb("p_hi", [P, 8, P], F16)
        p_lo = sb("p_lo", [P, 8, P], F16)
        rsum = sb("rsum", [P, H])
        cat = [sb(f"cat{n}", [P, 2, P]) for n in range(2)]
        catT = sb("catT", [P, P])
        xnF = sb("xnF", [P, 4, D])
        lnF = sb("lnF", [P, GR])
        stF = sb("stF", [P, 4, 6])
        mvF = sb("mvF", [P, 4, 2])
        rsF = sb("rsF", [P, 4, 2])
        hT = sb("hT", [P, FT, GR])
        pad_row = sb("pad_row", [P, ROW])
        xnL = k_heads[0][:, 0, 0, :, :].rearrange("p r k -> p (r k)").rearrange("p (t d) -> p t d", t=4)
        lnL = k_heads[0][:, 0, 1, :, :].rearrange("p r k -> p (r k)")
        stM = sb("stM", [P, TILES, 6])
        mvM = sb("mvM", [P, TILES, 2])
        rsM = sb("rsM", [P, TILES, 2])
        logit = sb("logit", [P, RT_T, E])
        top8 = sb("top8", [P, RT_T, E])
        idx8 = sb("idx8", [P, RT_T, E], U32)
        idxf = sb("idxf", [P, 2, RT_T])
        chosen = sb("chosen", [P, 2, RT_T, E])
        counted = sb("counted", [P, RT_T, E], F16)
        place = sb("place", [P, RT_T, E])
        prob = sb("prob", [P, RT_T, E])
        psum8 = sb("psum8", [P, RT_T])
        pw = sb("pw", [P, RT_T, 2])
        run = sb("run", [P, E])
        spot = sb("spot", [P, 2, RT_T, E])
        slotf = sb("slotf", [P, 2, RT_T])
        slot = sb("slot", [P, 2, TILES], U32)
        tail = sb("tail", [P, E], U32)
        cnt = sb("cnt", [P, E])
        nblk = sb("nblk", [P, E])
        cumb = sb("cumb", [P, E])
        cmp8 = sb("cmp8", [P, 40, E])
        blkf = sb("blkf", [P, 2, 40])
        blk = sb("blk", [P, 2, 40], U32)
        xin = [work[:, n * (ROW + D):n * (ROW + D) + ROW] for n in range(NX)]
        xbT = [xnF[:, n, :] for n in range(2)]
        gated = [sb(f"gated{n}", [P, 4 * MC]) for n in range(2)]
        hb = [hT[:, n, :] for n in range(2)]
        hbT = [hT[:, 2 + n, :] for n in range(2)]
        yb = [work[:, n * (ROW + D) + ROW:(n + 1) * (ROW + D)] for n in range(NX)]

        psS = ctx.enter_context(nc.psum_tensor("psS", [P, 2, 512], F32))
        psT = ctx.enter_context(nc.psum_tensor("psT", [P, 2, 512], F32))
        psO = ctx.enter_context(nc.psum_tensor("psO", [P, 512], F32))
        psL = ctx.enter_context(nc.psum_tensor("psL", [P, 512], F32))
        psQ = ctx.enter_context(nc.psum_tensor("psQ", [P, 512], F32))
        psC = ctx.enter_context(nc.psum_tensor("psC", [P, 512], F32))

        rel_dram = nc.dram_tensor("rel_scratch", (H, S, P), F32).ap()
        batch_dram = nc.dram_tensor("batch_scratch", (B, D), F32).ap()

        dispatched = nc.dram_tensor("dispatched", (E * REGION + P, ROW), F32).ap()
        results = nc.dram_tensor("results", (2 * TOK, D), F32).ap()

        r_rt = sem("r_rt")
        r_e = sem("r_e")
        r_cnt = sem("r_cnt")
        r_oh = sem("r_oh")
        r_dup = sem("r_dup")
        r_top = sem("r_top")
        r_slot = sem("r_slot")
        r_sent = sem("r_sent")
        r_tab = sem("r_tab")
        r_end = sem("r_end")
        pad_added = sem("pad_added")
        tern_ready = sem("tern_ready")
        r_tail = sem("r_tail")
        pad_ready = sem("pad_ready")
        pad_out = sem("pad_out")
        b_ld = [sem(f"b_ld{n}") for n in range(NX)]
        b_xt = sem("b_xt")
        b_xc = sem("b_xc")
        b_m1 = sem("b_m1")
        b_sg = sem("b_sg")
        b_hd = sem("b_hd")
        b_t2 = sem("b_t2")
        b_hc = sem("b_hc")
        b_m2 = sem("b_m2")
        b_ye = sem("b_ye")
        b_sc = [sem(f"b_sc{n}") for n in range(NX)]
        b_res = [sem(f"b_res{g}") for g in range(GROUPS)]
        ld_const = sem("ld_const")
        ld_x = sem("ld_x")
        ld_ctx = sem("ld_ctx")
        ld_qk = sem("ld_qk")
        ld_wo = sem("ld_wo")
        ld_fc = sem("ld_fc")
        ctx_summed = sem("ctx_summed")
        ld_mask = sem("ld_mask")
        ld_prep = sem("ld_prep")
        ld_moe0 = sem("ld_moe0")
        ld_moe3 = sem("ld_moe3")
        zeroed = sem("zeroed")
        setup_pe = sem("setup_pe")
        setup_ev = sem("setup_ev")
        dve_prep = sem("dve_prep")
        rel_out = sem("rel_out")
        rel_in = sem("rel_in")
        batch_out = sem("batch_out")
        batch_in = sem("batch_in")
        a_stat = sem("a_stat")
        a_rstd = sem("a_rstd")
        a_xn = sem("a_xn")
        a_lnp = sem("a_lnp")
        a_ln = sem("a_ln")
        a_xb = sem("a_xb")
        a_ctx = [sem(f"a_ctx{n}") for n in range(2)]
        a_qkp = sem("a_qkp")
        a_q = sem("a_q")
        a_km = sem("a_km")
        a_vp = sem("a_vp")
        a_vhi = sem("a_vhi")
        a_vlo = sem("a_vlo")
        a_sc = sem("a_sc")
        a_ev = sem("a_ev")
        a_side = [sem(f"a_side{n}") for n in range(4)]
        a_sidef = sem("a_sidef")
        a_mx = sem("a_mx")
        a_sub = sem("a_sub")
        a_exp = sem("a_exp")
        a_tr = sem("a_tr")
        a_hi = sem("a_hi")
        a_lo = sem("a_lo")
        a_pv = sem("a_pv")
        a_rs = sem("a_rs")
        a_cat = sem("a_cat")
        a_ctp = sem("a_ctp")
        a_ct = sem("a_ct")
        a_out = sem("a_out")
        a_x = sem("a_x")
        f_stat = sem("f_stat")
        f_rstd = sem("f_rstd")
        f_xn = sem("f_xn")
        f_lnp = sem("f_lnp")
        f_ln = sem("f_ln")
        f_xb = sem("f_xb")
        f_bn = sem("f_bn")
        f_x = sem("f_x")
        a_bn = sem("a_bn")
        zeroed_v = sem("zeroed_v")
        cap_ready = sem("cap_ready")
        bv_ready = sem("bv_ready")
        fs = {}
        for k in ("ffn1", "ffn2"):
            fs[k] = [sem(f"{k}_{w}") for w in ("up", "read", "hidden", "down")]
        l_bn, l_stat, l_rstd, l_xn = sem("l_bn"), sem("l_stat"), sem("l_rstd"), sem("l_xn")
        l_lnp, l_ln, l_y, l_x = sem("l_lnp"), sem("l_ln"), sem("l_y"), sem("l_x")
        fs["ffn2"][2] = fs["ffn2"][1]
        stored = sem("stored")

        ATT = {0: 0, 2: 1, 3: 2}
        KIND = {"moe0": "moe", "ffn1": "plain", "ffn2": "plain", "moe3": "moe"}
        FFN = {k: n for n, k in enumerate(p for p in PHASES if p in KIND)}
        NEXT = {ATT[p]: PHASES[n + 1] for n, p in enumerate(PHASES[:-1]) if p in ATT}
        F_BEFORE = {p: sum(q in KIND for q in PHASES[:n]) for n, p in enumerate(PHASES) if p in ATT}
        A_AFTER_F = {p: ATT[PHASES[n + 1]] for n, p in enumerate(PHASES[:-1]) if p in KIND and PHASES[n + 1] in ATT}
        F_AFTER_A = {p: ATT[PHASES[n - 1]] + 1 for n, p in enumerate(PHASES) if p in KIND and PHASES[n - 1] in ATT}

        MOE = {"moe0": 0, "moe3": 1}
        CHOICES = {"moe0": 1, "moe3": 2}
        NBLOCKS = {k: -(-((CHOICES[k] * TOK + E * (P - 1)) // P) // NX) * NX for k in MOE}
        NBLOCKS["shared"] = TILES
        BLOCK0 = {"moe0": 0, "shared": NBLOCKS["moe0"], "moe3": NBLOCKS["moe0"] + TILES}
        SCATTERED = {"moe0": 0, "moe3": NBLOCKS["moe0"] // NX}
        SENT = {"moe0": 16 * TILES, "moe3": 16 * 3 * TILES}
        psH = [psO, psL]
        routed = [lnF[:, :], lnL]
        psR = [psQ, psC]

        def tab(name):
            at, n = RT[name]
            return route_tab[:, at:at + n]

        set_ps = [psQ, psC]
        bv_twice = xnF[:, 0:2, :]

        def tr(pe, dst, src, k):
            return nc.tensor.transpose(dst, src, ident[0:k, 0:k])

        def setup_jobs():
            mm = nc.tensor.matmul

            def acopy(dst, src, **kw):
                return nc.scalar.activation(dst, src, ACT.Copy, **kw)

            def flat(t):
                return t[:, :, :].rearrange("p a b -> p (a b)")

            def transposes(dst, srcs, k):
                def pe(ps):
                    for n, src in enumerate(srcs):
                        r = tr(None, ps[dst, n * k:(n + 1) * k], src, k)
                    return r
                return pe
            full = slice(0, P)
            jobs = []
            for q in range(4):
                jobs.append((f"ctx{q}", [(ld_ctx, 16)],
                             transposes(full, [tok_in[:, t * P:(t + 1) * P] for t in range(4 * q, 4 * q + 4)], P),
                             lambda ps, q=q: acopy(ctxT[:, q * 512:(q + 1) * 512], ps[:, :])))

            def pe(ps):
                for h2 in range(2):
                    mm(ps[:, 0:D], bv_twice[0:64, h2, :], wo0[0:64, h2, :], start=(h2 == 0), stop=False)
                return mm(ps[:, 0:D], ident[:, :], bias_out[:, 0, :], start=False, stop=True)
            jobs.append(("bias0", [(ld_wo, 16 * 4), (bv_ready, 1)], pe,
                         lambda ps: acopy(bias_out[:, 0, :], ps[:, 0:D])))

            jobs.append(("w3T", [(ld_prep, PREP)], transposes(full, [wraw3[:, n, :] for n in range(4)], P),
                         lambda ps: acopy(flat(w3T), ps[:, :])))
            jobs.append(("w1T", [], transposes(full, [w1raw[:, n * P:(n + 1) * P] for n in range(2)], P),
                         lambda ps: acopy(flat(w1T), ps[:, 0:2 * P])))
            jobs.append(("rel", [], lambda ps: mm(ps[0:H, 0:REL], rel_bias[:, :], rel_onehot[:, 0:REL], start=True, stop=True),
                         lambda ps: acopy(rel_row[:, 0:REL], ps[0:H, 0:REL])))
            jobs.append(("u1T", [], transposes(slice(0, 32), [u1[:, :]], P), lambda ps: acopy(u1T[:, :], ps[0:32, 0:P])))

            def pe(ps):
                mm(ps[0:B, 0:D], ctx_sum[:, :], w1T[:, 1, :], start=True, stop=False)
                return mm(ps[0:B, 0:D], s_row[0:1, :], bias_out[0:1, 3, :], start=False, stop=True)
            jobs.append(("batch", ["w1T", (ctx_summed, 2)], pe, lambda ps: acopy(per_batch[:, :], ps[0:B, 0:D], scale=1.0 / S)))

            def pe(ps):
                mm(ps[:, 0:D], bv_col[:, 0:1].broadcast_to([P, P]), w3T[:, 3, :], start=True, stop=False)
                return mm(ps[:, 0:D], ident[:, :], bias_out[:, 1, :], start=False, stop=True)
            jobs.append(("bias3", ["w3T"], pe, lambda ps: acopy(bias_out[:, 1, :], ps[:, 0:D])))
            jobs.append(("gate3T", [], lambda ps: tr(None, ps[:, 0:E], gate3[:, :], E),
                         lambda ps: acopy(gate3T[:, :], ps[:, 0:E])))
            jobs.append(("u2T", [], transposes(slice(0, 32), [u2[:, n, :] for n in range(FT)], P),
                         lambda ps: acopy(u2T[:, :], ps[0:32, :])))
            jobs.append(("uT", [], transposes(slice(0, 16), [u_raw[:, n, :] for n in range(FT)], P),
                         lambda ps: acopy(uT[:, :], ps[0:16, :])))
            jobs.append(("fastT", [], lambda ps: tr(None, ps[0:16, 0:16], fast_raw[:, :], 16),
                         lambda ps: acopy(fastT[:, :], ps[0:16, 0:16])))
            jobs.append(("w2in", ["u1T"], lambda ps: mm(ps[:, :], u1T[:, :], v1r[:, :], start=True, stop=True),
                         lambda ps: acopy(w2in[:, :], ps[:, :])))
            jobs.append(("fast_v", ["fastT"], lambda ps: mm(ps[0:16, 0:D], fastT[:, :], v_raw[:, :], start=True, stop=True),
                         lambda ps: nc.scalar.activation(fast_v[:, :], ps[0:16, 0:D], ACT.Copy, scale=gate_col[0:16, 0:1])))

            def pe(ps):
                for n in range(FT):
                    r = mm(ps[:, n * P:(n + 1) * P], u2T[:, n * P:(n + 1) * P], v2r[:, :], start=True, stop=True)
                return r
            jobs.append(("w2out", ["u2T"], pe, lambda ps: acopy(flat(w2out), ps[:, :])))

            def pe(ps):
                for n in range(FT):
                    c = slice(n * P, (n + 1) * P)
                    mm(ps[:, c], tern[:, n, :], ident[:, :], start=True, stop=False)
                    r = mm(ps[:, c], fast_v[:, :], uT[:, c], start=False, stop=True)
                return r
            jobs.append(("w1in", ["uT", "fast_v", (tern_ready, 1)], pe, lambda ps: acopy(w1eff[:, :], ps[:, :])))
            jobs.append(("w1out", [(tern_ready, 2)], transposes(full, [proj_raw[:, n * P:(n + 1) * P] for n in range(FT)], P),
                         lambda ps: acopy(flat(w1out), ps[:, :])))
            return jobs

        PREP = 16 * 38
        JOBS = setup_jobs()
        NAMES = [j[0] for j in JOBS]
        FIRST = NAMES.index("bias0") + 1

        def job_done(name):
            return NAMES.index(name) + 1

        def v_part(v, r):
            return v[r * S:(r + 1) * S, :, :, r:H:2, 0:DH].rearrange("p u b h d -> p (u b) h d")

        def v_product(r):
            return psQ[r * S:(r + 1) * S, :].rearrange("p (c h d) -> p c h d", c=4, h=H)[:, :, r:H:2, :]

        def staggered(engine, nb, step, anew=lambda: None):
            for s in (-2, -1, 0):
                step(s % NX, s, lo=s)
            with engine.Fori(0, nb // NX - 1) as j:
                anew()
                for u in range(NX):
                    step((u + 1) % NX, NX * j + (u + 1), lo=1)
            anew()
            for s in range(nb - NX + 1, nb + 1):
                step(s % NX, s, lo=1, hi=True)

        def run_jobs(pe, lo, hi):
            for n in range(lo, hi):
                _, waits, job, _ = JOBS[n]
                if n >= 2:
                    pe.wait_ge(setup_ev, n - 1)
                for w in waits:
                    if isinstance(w, str):
                        pe.wait_ge(setup_ev, job_done(w))
                    else:
                        pe.wait_ge(*w)
                job(set_ps[n % 2]).then_inc(setup_pe, 1)

        def wait_apart(engine, s, value):
            at = value if isinstance(value, int) else engine.to_reg(value)
            engine.wait_ge(ld_const, 16)
            engine.wait_ge(s, at)

        block = ctx.enter_context(nc.Block())

        @block.sync
        def _(sp):
            def loads(s, *pairs):
                for o, i in pairs:
                    sp.dma_start(o, i).then_inc(s, 16)

            def bias_loads(s, n, layer):
                with nc.allow_non_contiguous_dma(reason="small bias vectors, a feature to a partition"):
                    for b in range(2):
                        loads(s, *((t[b * 64:(b + 1) * 64, n, :], A[f"L{layer}_xattn_{k}"].rearrange("(h p) -> p h", h=2))
                                   for t, k in ((bq, "bq"), (bk, "bk"))))
            loads(ld_const, (first_tab[:], K["first_tab"]))
            loads(ld_ctx, (tok_in[:].rearrange("p (t d) -> p t d", t=TILES),
                           A["ctx_1024"].rearrange("(t b) s d -> (b s) t d", b=2)))
            loads(ld_x, (x[:].rearrange("p (t d) -> p t d", t=TILES), A["x"].rearrange("(t b) s d -> (b s) t d", b=2)))
            loads(ld_qk, *((wqk0[:, n, :], A[f"L0_xattn_W{k}"]) for n, k in enumerate("qkv")))
            bias_loads(ld_qk, 0, 0)
            loads(ld_wo, (wo0[0:64], A["L0_xattn_Wo"].rearrange("(h s) e -> s h e", h=2)),
                  (wo0[64:P], A["L0_xattn_Wo"].rearrange("(h s) e -> s h e", h=2)),
                  (bv_row[:], A["L0_xattn_bv"].partition_broadcast(P)),
                  (bias_out[:, 0, :], A["L0_xattn_bo"].partition_broadcast(P)))
            loads(ld_mask, *((mask_words[b * S:(b + 1) * S], A["mask_BxSxS2_bf1"].rearrange("(t b) q k -> b q t k", b=2)[b])
                             for b in range(2)))

            loads(ld_fc, (fc_raw[:], A["L1_ffn_w_fc"].rearrange("(t p) d -> p t d", p=P)))

            def later_loads():
                pairs = [(route_tab[:], K["route_tab"]), (place_tab[:], K["place_tab"]), (before[:], K["before"]),
                         (rel_onehot[:, 0:REL], K["rel_onehot"]),
                         (router0[:], A["L0_ffn_Wr"]), (br0[:], A["L0_ffn_br"].partition_broadcast(P))]
                pairs += [(wraw3[:, n, :], A[f"L3_xattn_W{k}"]) for n, k in enumerate("qkvo")]
                pairs += [(bias_out[:, 1, :], A["L3_xattn_bo"].partition_broadcast(P)),
                          (bias_out[:, 2, :], A["L2_ffn_b2"].partition_broadcast(P)),
                          (bias_out[:, 3, :], A["L1_xattn_b"].partition_broadcast(P)),
                          (bv_col[:], A["L3_xattn_bv"].rearrange("(p a) -> p a", a=1)),
                          (wqkv2[:, 0, :], A["L2_xattn_Wq"]),
                          (wqkv2[:, 1:3, :], A["L2_xattn_Wkv"].rearrange("p (a n) -> p a n", a=2)),
                          (wo2[:], A["L2_xattn_Wo"]), (w1raw[:], A["L1_xattn_W"]),
                          (gate3[:], A["L3_ffn_gate_w"]),
                          (proj_raw[:], A["L1_ffn_w_proj"]), (u_raw[:], A["L1_ffn_u"].rearrange("(t p) r -> p t r", p=P)),
                          (v_raw[:], A["L1_ffn_v"]), (fast_raw[:], A["L1_ffn_fast_b"]),
                          (gate_col[:], A["L1_ffn_gate"].partition_broadcast(P)),
                          (u1[:], A["L2_ffn_U1"]), (v1r[:], A["L2_ffn_V1"]),
                          (u2[:], A["L2_ffn_U2"].rearrange("(t p) r -> p t r", p=P)), (v2r[:], A["L2_ffn_V2"]),
                          (rel_bias[:], A["L2_xattn_rel_bias"])]
                for b in range(2):
                    pairs += [(pad_words[b * S:(b + 1) * S], A["mask_BxS2_bf0"].rearrange(
                                  "(t b) k -> b t k", b=2)[b].partition_broadcast(S)),
                              (amask[b * S:(b + 1) * S], A["fside_SxS2_0"])]
                for n in range(0, len(pairs), 7):
                    loads(ld_prep, *pairs[n:n + 7])
                    yield
                bias_loads(ld_prep, 1, 3)
                with nc.allow_non_contiguous_dma(reason="a small bias vector, a feature to a partition"):
                    loads(ld_prep, (b1[:], A["L2_ffn_b1"].rearrange("(t p) -> p t", p=P)))
                assert 16 * (len(pairs) + 5) == PREP
                loads(ld_moe0, (e_up, A["L0_ffn_W1"].rearrange("e h f -> h e f")),
                      *((e_down[:, e], A["L0_ffn_W2"][e].rearrange("(f p) h -> p f h", p=P)) for e in range(E)))
                yield

            def chunk_load(n, c, cg):
                sp.wait_ge(a_vp, cg - 1)
                for d in range(2):
                    sp.dma_start(ctxc[n][:, :, d, :], ctxT[:, ds(c * CH, CH)].rearrange("p (b s) -> p b s", b=4)).then_inc(a_ctx[n], 16)

            def side_load(n, i):
                sp.wait_ge(a_ev, 2 * (32 + i - 4 + 1))
                for b in range(2):
                    sp.dma_start(side[n][b * S:(b + 1) * S],
                                 A["fside_Bx16xSxS2_0"][ds(2 * i + b, 1)].rearrange("a h q k -> q (a h) k"))\
                      .then_inc(a_side[n], 16)

            def moe(kind):
                m = MOE[kind]
                if kind == "moe3":
                    def load_tile(n, t, k):
                        if isinstance(t, int):
                            if t % 4 == 0:
                                sp.wait_ge(f_xn, GROUPS * FFN[kind] + t // 4 + 1)
                        wait_apart(sp, b_xt, k - (NX - 1))
                        sp.dma_start(xin[n][:, 0:D], pay_row[:, ds(t * 2 * ROW, D)]).then_inc(b_ld[n], 16)
                    b0 = BLOCK0["shared"]
                    for t in range(NX):
                        if t == 0:
                            sp.wait_ge(f_xn, GROUPS * FFN[kind] + GROUPS)
                        load_tile(t, t, b0 + t)
                    with sp.Fori(1, TILES // NX) as j:
                        for n in range(NX):
                            load_tile(n, NX * j + n, NX * j + (b0 + n))
                b0, nb = BLOCK0[kind], NBLOCKS[kind]
                if kind == "moe0":
                    sp.wait_ge(pad_ready, 1)
                    sp.dma_start(dispatched[E * REGION:E * REGION + P, :], pad_row[:, :]).then_inc(pad_out, 16)
                sp.wait_ge(r_end, m + 1)
                for e in range(E):
                    end = sp.value_load(tail[0:1, e:e + 1], min_val=0, max_val=(E - 1) * REGION + TOK)
                    sp.dma_start(dispatched[ds(end, P), :], pad_row[:, :]).then_inc(r_tail, 16)
                sp.wait_ge(r_tab, m + 1)
                sp.wait_ge(r_sent, SENT[kind])
                sp.wait_ge(r_tail, 16 * E * (m + 1))
                sp.wait_ge(pad_out, 16)
                sc0 = SCATTERED[kind]

                def load_block(n, b, first):
                    row_at = sp.value_load(blk[0:1, 0, ds(b, 1)], min_val=0, max_val=E * REGION)
                    if not (first and b0 == 0):
                        wait_apart(sp, b_xt, b + (b0 - NX + 1))
                    if not first:
                        sp.wait_ge(b_sc[n], (b - n) * (16 // NX) + 16 * sc0)
                    sp.dma_start(xin[n], dispatched[ds(row_at, P), :]).then_inc(b_ld[n], 16)
                for n in range(NX):
                    load_block(n, n, True)
                with sp.Fori(1, nb // NX) as j:
                    for n in range(NX):
                        load_block(n, NX * j + n, False)
                for n in range(NX):
                    sp.wait_ge(b_sc[n], 16 * (sc0 + nb // NX))
                for g in range(GROUPS):
                    for c in range(CHOICES[kind]):
                        sp.dma_start(pay_row[:, c * TOK + g * GR:c * TOK + (g + 1) * GR].rearrange("p (t d) -> p t d", t=4),
                                     results[c * TOK + g * GR:c * TOK + (g + 1) * GR].rearrange("(t p) d -> p t d", p=P))\
                          .then_inc(b_res[g], 16)

            for a in range(3):
                if a == 1 and "moe0" in FFN:
                    moe("moe0")
                    for o, i in ((m_gu[:, :, 0:MI], A["L3_ffn_wg"].rearrange("e h i -> h e i")),
                                 (m_gu[:, :, MI:2 * MI], A["L3_ffn_wu"].rearrange("e h i -> h e i")),
                                 (m_down, A["L3_ffn_wd"].rearrange("e (c p) h -> p (e c) h", p=MC)),
                                 (s_gu[:, 0, :], A["L3_ffn_swg"]), (s_gu[:, 1, :], A["L3_ffn_swu"]),
                                 (s_down, A["L3_ffn_swd"].rearrange("(c p) h -> p c h", p=MC))):
                        sp.dma_start(o, i).then_inc(ld_moe3, 16)
                for n in range(2):
                    if a == 0:
                        if n == 0:
                            sp.wait_ge(setup_ev, job_done("ctx3"))
                        for d in range(2):
                            sp.dma_start(ctxc[n][:, :, d, :], ctxT[:, n * CH:(n + 1) * CH].rearrange("p (b s) -> p b s", b=4))\
                              .then_inc(a_ctx[n], 16)
                    else:
                        chunk_load(n, n, 8 * a + n)
                if a == 0:
                    later = later_loads()
                    for c in range(2, 8):
                        next(later)
                        chunk_load(c % 2, c, c)
                    continue
                if a == 2:
                    for n in range(4):
                        for b in range(2):
                            sp.dma_start(side[n][b * S:(b + 1) * S],
                                         A["fside_Bx16xSxS2_0"][2 * n + b].rearrange("h q k -> q h k")).then_inc(a_side[n], 16)
                with sp.Fori(1, 4) as j:
                    for n in range(2):
                        chunk_load(n, 2 * j + n, 2 * j + (8 * a + n))
                        if a == 2:
                            for u in range(2):
                                side_load(2 * n + u, 4 * j + (2 * n + u))

            if "moe3" in FFN:
                moe("moe3")
            sp.wait_ge(a_x, 3 * TILES)
            for g in range(GROUPS):
                sp.wait_ge(f_x, GROUPS * (len(FFN) - 1) + g + 1)
                sp.dma_start(out[8 * g:8 * g + 8].rearrange("(t b) s d -> (b s) t d", b=2),
                             x[:, g * GR:(g + 1) * GR].rearrange("p (t d) -> p t d", t=4)).then_inc(stored, 16)
            sp.wait_ge(stored, 16 * GROUPS)

        mm = nc.tensor.matmul

        @block.tensor
        def _(pe):
            pe.wait_ge(ld_const, 16)
            run_jobs(pe, 0, FIRST)

            def ln_transposes(cg):
                pe.wait_ge(a_xn, cg + 1)
                if not (isinstance(cg, int) and cg == 0):
                    pe.wait_ge(a_ln, cg)
                for t in range(2):
                    r = tr(pe, psL[:, t * P:(t + 1) * P], xnA[:, t, :], P)
                r.then_inc(a_lnp, 1)

            def project(a, n, cg):
                w = (wqk0, wqkv2, w3T)[a]
                pe.wait_ge(a_ln, cg + 1)
                pe.wait_ge(a_ctx[n], ctx_count(cg, n))
                if not (isinstance(cg, int) and cg == 0):
                    pe.wait_ge(a_q, cg)
                    if not (isinstance(cg, int) and cg == 1):
                        pe.wait_ge(a_vlo, cg if isinstance(cg, int) and cg % 8 == 0 else cg - 1)
                for qk in range(2):
                    toks = lnA[:, :] if qk == 0 else ctxc[n][:, :, 0, :]
                    toks = toks.rearrange("p (u b s) -> p u b s" if qk == 0 else "p (u b) s -> p u b s", u=2, b=2)
                    for half in range(2):
                        for b in range(2):
                            r = mm(psQ[b * 64:(b + 1) * 64, (2 * qk + half) * P:(2 * qk + half + 1) * P],
                                   w[:, qk, half * 64:(half + 1) * 64], toks[:, :, b, :], start=True, stop=True)
                r.then_inc(a_qkp, 1)

            def ctx_count(cg, n):
                if isinstance(cg, int):
                    return 32 * (cg // 2 + 1)
                return (cg - n) * 16 + 32

            def values(a, n, cg, more):
                w = (wqk0, wqkv2, w3T)[a]
                pe.wait_ge(a_q, cg + (2 if more else 1))
                pe.wait_ge(a_ctx[n], ctx_count(cg, n))
                for u in range(2):
                    for b in range(2):
                        tok = ctxc[n][:, 2 * u + b, :, :].rearrange("p d s -> p (d s)")
                        r = mm(psQ[:, (2 * u + b) * P:(2 * u + b + 1) * P], tok, w[:, 2, :], start=True, stop=True)
                r.then_inc(a_vp, 1)

            def scores(n, u, i, cg):
                pe.wait_ge(a_km, 2 * cg + 2)
                for half in range(2):
                    if not (isinstance(i, int) and i == 0):
                        pe.wait_ge(a_ev, 2 * i - 1 + half)
                    mm(psS[:, half, :], q_diag[n][:, half, u, :], k_heads[n][:, half, u, :, :],
                       start=True, stop=True).then_inc(a_sc, 1)

            def transposes(m, i):
                pe.wait_ge(a_exp, i + 1)
                for half in range(2):
                    if not (isinstance(i, int) and i == 0):
                        pe.wait_ge(a_lo, 2 * i - 1 + half)
                    for j in range(4):
                        g = 4 * half + j
                        r = tr(pe, psT[:, half, j * P:(j + 1) * P],
                               sc[m][:, 2 * g:2 * g + 2, :].rearrange("p h k -> p (h k)"), P)
                    r.then_inc(a_tr, 1)

            def apply_probs(n, u, i, cg):
                pe.wait_ge(a_lo, 2 * i + 2)
                pe.wait_ge(a_vlo, cg + 1)
                pe.wait_ge(a_vhi, cg + 1)
                if not (isinstance(i, int) and i == 0):
                    pe.wait_ge(a_cat, i)
                o = psO[:, 0:2 * H * 9].rearrange("p (b h e) -> p b h e", b=2, h=H)
                for j in range(8):
                    for k, (pp, vv) in enumerate(((p_hi, v_hi), (p_hi, v_lo), (p_lo, v_hi))):
                        r = mm(o[:, :, 2 * j:2 * j + 2, :], pp[:, j, :], vv[n][:, u, :, 2 * j:2 * j + 2, :],
                               start=(k == 0), stop=(k == 2))
                r.then_inc(a_pv, 1)

            def cat_transpose(m, i):
                pe.wait_ge(a_cat, i + 1)
                if not (isinstance(i, int) and i == 0):
                    pe.wait_ge(a_x, i)
                tr(pe, psC[:, 0:P], cat[m][:, 0, :], P).then_inc(a_ctp, 1)

            def project_out(a, m, i, ia):
                if a == 0:
                    pe.wait_ge(a_cat, i + 1)
                    if not (isinstance(i, int) and i == 0):
                        pe.wait_ge(a_x, i)
                    for h2 in range(2):
                        r = mm(psC[:, P:2 * P], cat[m][:, h2, :], wo0[:, h2, :], start=(h2 == 0), stop=(h2 == 1))
                else:
                    pe.wait_ge(a_ct, ia + 1)
                    r = mm(psC[:, P:2 * P], catT[:, :], wo2[:, :] if a == 1 else w3T[:, 3, :], start=True, stop=True)
                r.then_inc(a_out, 1)

            def attention(a):
                def step(u, j, first=False, more=True):
                    i = 4 * j + u + 16 * a
                    c, n = 2 * j + u // 2 + 8 * a, u // 2
                    scores(n, u % 2, i, c)
                    if u % 2 == 0 and more:
                        ln_transposes(c + 1)
                    if not (first and u < 2):
                        transposes((u - 2) % 4, i - 2)
                    if a and not (first and u < 3):
                        cat_transpose((u - 3) % 2, i - 3)
                    if u % 2 == 1:
                        values(a, n, c, more)
                    elif more:
                        project(a, 1 - n, c + 1)
                    if not (first and u < 3):
                        project_out(a, (u - 3) % 2, i - 3, i - 19)
                    if not (first and u < 2):
                        apply_probs(1 - n, u % 2, i - 2, c - 1)

                if a == 0:
                    ln_transposes(0)
                    pe.wait_ge(ld_qk, 16 * 7)
                    project(0, 0, 0)
                for u in range(4):
                    step(u, 0, first=True)
                    if a == 0 and u == 0:
                        for t in range(TILES):
                            r = mm(psC[:, 2 * t:2 * t + 2], tok_in[:, t * P:(t + 1) * P], dup_mask[:, 0:2 * DH:DH], start=True, stop=True)
                        r.then_inc(ctx_summed, 1)
                    if a == 0 and u == 2:
                        pe.wait_ge(ctx_summed, 2)
                with pe.Fori(1, 3) as j:
                    for u in range(4):
                        step(u, j)
                for u in range(4):
                    step(u, 3, more=(u < 2))
                for u in range(3):
                    step_tail(a, u)

            def step_tail(a, u):
                i = 16 + u + 16 * a
                if u < 2:
                    transposes((u - 2) % 4, i - 2)
                if a:
                    cat_transpose((u - 3) % 2, i - 3)
                project_out(a, (u - 3) % 2, i - 3, i - 19)
                if u < 2:
                    apply_probs(1, u % 2, i - 2, 8 * a + 7)

            def ffn_ln(G):
                pe.wait_ge(f_xn, G + 1)
                if not (isinstance(G, int) and G == 0):
                    pe.wait_ge(f_ln, G)
                for t in range(4):
                    r = tr(pe, psL[:, t * P:(t + 1) * P], xnF[:, t, :], P)
                r.then_inc(f_lnp, 1)

            def plain(kind):
                f0 = GROUPS * FFN[kind]
                win, wout = (w1eff, w1out) if kind == "ffn1" else (w2in, w2out)
                up, read, hid, y = fs[kind]
                a = A_AFTER_F[kind]

                def group(g, last):
                    ahead = kind == "ffn1" and g + 2 < GROUPS
                    pe.wait_ge(f_ln, g + (f0 + 1))
                    for f in range(FT):
                        if f >= 2 or not isinstance(g, int) or g > 0:
                            pe.wait_ge(read, g * FT + (f - 1))
                        mm(psS[:, f % 2, :], win[:, f * P:(f + 1) * P], lnF[:, :], start=True, stop=True).then_inc(up, 1)
                    if ahead:
                        lin_ln(g + 2)
                    if not (isinstance(g, int) and g == 0):
                        pe.wait_ge(f_x, g + f0)
                    for f in range(FT):
                        if f == 2:
                            if ahead:
                                lin(g + 2)
                            if not last:
                                ffn_ln(g + (f0 + 1))
                        if last and f == FT - 1:
                            ln_transposes(8 * a)
                        pe.wait_ge(hid, g * FT + (f + 1))
                        for t in range(4):
                            r = mm(psT[:, 0, t * P:(t + 1) * P], hT[:, f, t * P:(t + 1) * P], wout[:, f, :],
                                   start=(f == 0 and t == 0), stop=(f == FT - 1 and t == 3))
                    r.then_inc(y, 1)
                    if last:
                        project(a, 0, 8 * a)

                if kind == "ffn1":
                    for g in range(2):
                        lin_ln(g)
                        lin(g)
                ffn_ln(f0)
                group(0, False)
                if kind == "ffn1":
                    for g in range(1, GROUPS - 1):
                        group(g, False)
                else:
                    with pe.Fori(1, GROUPS - 1) as g:
                        group(g, False)
                group(GROUPS - 1, True)

            def lin_ln(g):
                pe.wait_ge(l_xn, g + 1)
                if g:
                    pe.wait_ge(l_ln, g)
                for t in range(4):
                    r = tr(pe, psO[:, t * P:(t + 1) * P], xnL[:, t, :], P)
                r.then_inc(l_lnp, 1)

            def lin(g):
                pe.wait_ge(l_ln, g + 1)
                if g:
                    pe.wait_ge(l_x, g)
                for t in range(4):
                    r = mm(psT[:, 1, t * P:(t + 1) * P], lnL[:, t * P:(t + 1) * P], w1T[:, 0, :], start=True, stop=True)
                r.then_inc(l_y, 1)

            def blocks(kind):
                b0, nb = BLOCK0[kind], NBLOCKS[kind]
                m = 0 if kind == "moe0" else 1
                chunks, kk = {"moe0": (FT, P), "moe3": (2, MC), "shared": (4, MC)}[kind]

                held = {}

                def expert(q, b):
                    if q not in held:
                        held[q] = pe.value_load(blk[0:1, 1, ds(b, 1)], min_val=0, max_val=E - 1)
                    return held[q]

                def since(k, sm, v):
                    if not (isinstance(k, int) and k < 0):
                        pe.wait_ge(sm, v)

                def x_transpose(q, b):
                    k = b + b0
                    pe.wait_ge(b_ld[q], (k - q) * (16 // NX) + 16)
                    since(k - 1, b_xc, k)
                    tr(pe, psQ[:, 0:P], xin[q][:, 0:D], P).then_inc(b_xt, 1)

                def up(q, b):
                    k = b + b0
                    pe.wait_ge(b_xc, k + 1)
                    since(k - 2, b_hd, k - 1)
                    if kind == "shared":
                        mm(psT[:, q % 2, 0:4 * MC], xbT[q % 2], s_gu[:, 1, :], start=True, stop=True)
                        r = mm(psS[:, q % 2, 0:4 * MC], xbT[q % 2], s_gu[:, 0, :], start=True, stop=True)
                    else:
                        w = FF if kind == "moe0" else 2 * MI
                        r = mm(psS[:, q % 2, 0:w], xbT[q % 2], expert_w[:, ds(expert(q, b) * w, w)], start=True, stop=True)
                    r.then_inc(b_m1, 1)

                def h_transpose(q, b):
                    k = b + b0
                    pe.wait_ge(b_hd, k + 1)
                    since(k - 2, b_hc, k - 1)
                    for f in range(chunks):
                        r = tr(pe, psH[q % 2][0:kk, f * P:(f + 1) * P], hb[q % 2][:, f * kk:(f + 1) * kk], P)
                    r.then_inc(b_t2, 1)

                def down(q, b):
                    k = b + b0
                    e = None if kind == "shared" else expert(q, b)
                    pe.wait_ge(b_hc, k + 1)
                    since(k - 1, b_ye, k)
                    for f in range(chunks):
                        if kind == "shared":
                            w = s_down[:, f, :]
                        elif kind == "moe0":
                            w = expert_w[:, ds(e * (FT * D) + (E * FF + f * D), D)]
                        else:
                            w = expert_w[0:MC, ds(e * (2 * D) + (E * 2 * MI + f * D), D)]
                        r = mm(psC[:, 0:D], hbT[q % 2][0:kk, f * P:(f + 1) * P], w, start=(f == 0), stop=(f == chunks - 1))
                    r.then_inc(b_m2, 1)
                    held.pop(q, None)

                def step(q, s, lo=-2, hi=None):
                    if hi is None or s + 2 < nb:
                        x_transpose((q + 2) % NX, s + 2)
                    if lo >= -1 and (hi is None or s + 1 < nb):
                        up((q + 1) % NX, s + 1)
                    if kind != "shared" and (hi is None or s + 2 < nb):
                        expert((q + 2) % NX, s + 2)
                    if lo >= 0 and (hi is None or s < nb):
                        h_transpose(q, s)
                    if lo >= 1:
                        down((q - 1) % NX, s - 1)

                if kind != "shared":
                    pe.wait_ge(r_tab, m + 1)
                staggered(pe, nb, step, held.clear)

            def rows_in(kind, g):
                G = GROUPS * FFN[kind] + g
                pe.wait_ge(f_xn, G + 1)
                if g >= 2:
                    pe.wait_ge(f_ln, G - 1)
                elif G >= 2:
                    pe.wait_ge(f_ln, G - g)
                for t in range(4):
                    r = tr(pe, psH[1 - g % 2][:, t * P:(t + 1) * P], pay[:, 4 * g + t, 0, 0:D], P)
                r.then_inc(f_lnp, 1)

            def logits(kind, g):
                w = router0 if kind == "moe0" else gate3T
                pe.wait_ge(f_ln, GROUPS * FFN[kind] + g + 1)
                for t in range(4):
                    c = slice((4 * g + t) * E, (4 * g + t + 1) * E)
                    r = mm(psR[g // 2][:, c], routed[g % 2][:, t * P:(t + 1) * P], w[:, :], start=True, stop=True)
                r.then_inc(r_rt, 1)

            def moe(kind):
                f0, m = GROUPS * FFN[kind], MOE[kind]
                if kind == "moe0":
                    pe.wait_ge(ld_prep, PREP)
                rows_in(kind, 0)
                for g in range(GROUPS):
                    if g + 1 < GROUPS:
                        rows_in(kind, g + 1)
                    logits(kind, g)
                for h in range(TILES // RT_T):
                    pe.wait_ge(r_oh, TILES // RT_T * m + h + 1)
                    mm(psQ[:, 0:RT_T * E], before[:, :], counted[:, :, :], start=True, stop=False)
                    for t in range(1, RT_T):
                        mm(psQ[:, t * E:RT_T * E], ones[:, :], counted[:, 0:RT_T - t, :], start=False, stop=(t == RT_T - 1))
                    for t in range(RT_T):
                        r = mm(psQ[:, RT_T * E:(RT_T + 1) * E], ones[:, :], counted[:, t, :], start=(t == 0), stop=(t == RT_T - 1))
                    r.then_inc(r_cnt, 1)
                pe.wait_ge(r_slot, TILES // RT_T * (m + 1))
                if kind == "moe0":
                    run_jobs(pe, FIRST, len(JOBS))
                    pe.wait_ge(setup_ev, len(JOBS))
                if kind == "moe3":
                    pe.wait_ge(ld_moe3, 16 * 6)
                    blocks("shared")
                else:
                    pe.wait_ge(ld_moe0, 16 * 9)
                blocks(kind)
                pe.wait_ge(b_ye, BLOCK0[kind] + NBLOCKS[kind])

            for ph in PHASES:
                if ph in ATT:
                    if ph:
                        pe.wait_ge(f_x, GROUPS * F_BEFORE[ph])
                    attention(ATT[ph])
                    continue
                if ph in F_AFTER_A:
                    pe.wait_ge(a_x, 16 * F_AFTER_A[ph])
                {"plain": plain, "moe": moe}[KIND[ph]](ph)

        act = nc.scalar.activation

        @block.scalar
        def _(ac):
            def copy_jobs(lo, hi):
                for n in range(lo, hi):
                    ac.wait_ge(setup_pe, n + 1)
                    JOBS[n][3](set_ps[n % 2]).then_inc(setup_ev, 1)
                    yield NAMES[n]

            list(copy_jobs(0, FIRST))

            def ln_copy(cg):
                ac.wait_ge(a_lnp, cg + 1)
                if not (isinstance(cg, int) and cg == 0):
                    ac.wait_ge(a_qkp, cg)
                act(lnA[:, :], psL[:, 0:CH], ACT.Copy).then_inc(a_ln, 1)

            def qk_copy(a, n, cg, pair0):
                ac.wait_ge(a_qkp, cg + 1)
                if not (isinstance(cg, int) and cg < 2):
                    ac.wait_ge(a_sc, 2 * pair0 - 4)
                if not (isinstance(cg, int) and cg == 0):
                    ac.wait_ge(a_km, 2 * cg)
                q = psQ[:, 0:2 * P].rearrange("p (h u s) -> p h u s", h=2, u=2)
                k = psQ[:, 2 * P:4 * P].rearrange("p (h u s) -> p h u s", h=2, u=2)
                L = (0, None, 1)[a]
                for half in range(2):
                    for b in range(2):
                        r = slice(b * 64, b * 64 + 64)
                        act(q_diag[n][r, half, :, r], q[r, half], ACT.Identity,
                            bias=0.0 if L is None else bq[r, L, half:half + 1])
                    last = act(kT[:, half], k[:, half], ACT.Identity,
                               bias=0.0 if L is None else bk[:, L, half:half + 1])
                last.then_inc(a_q, 1)

            def key_heads(n, cg, part):
                ac.wait_ge(a_q, cg + 1)
                for r in range(4 * part, 4 * part + 4):
                    last = act(k_heads[n][:, :, :, r, :].rearrange("p h u s -> p (h u) s"),
                               kT[:, :, :, :].rearrange("p h u s -> p (h u) s"), ACT.Copy, scale=head_mask[:, r:r + 1])
                last.then_inc(a_km, 1)

            def v_high(n, cg, pair0):
                ac.wait_ge(a_vp, cg + 1)
                if not (isinstance(cg, int) and cg < 2):
                    ac.wait_ge(a_pv, pair0 - 2)
                for r in range(2):
                    last = act(v_part(v_hi[n], r), v_product(r), ACT.Copy)
                last.then_inc(a_vhi, 1)

            def exponent(a, m, i):
                ac.wait_ge(a_sub, i + 1)
                act(sc[m], sc[m], ACT.Exp, scale=2.0 if a == 2 else 1.0).then_inc(a_exp, 1)

            def p_high(i):
                for half in range(2):
                    ac.wait_ge(a_tr, 2 * i + half + 1)
                    if half == 0 and not (isinstance(i, int) and i == 0):
                        ac.wait_ge(a_pv, i)
                    act(p_hi[:, 4 * half:4 * half + 4, :].rearrange("p j t -> p (j t)"), psT[:, half, :],
                        ACT.Copy).then_inc(a_hi, 1)

            def cat_copy(i, ia):
                ac.wait_ge(a_ctp, ia + 1)
                act(catT[:, :], psC[:, 0:P], ACT.Copy).then_inc(a_ct, 1)

            def attention(a):
                def step(u, j, first=False, more=True, live=True):
                    i = 4 * j + u + 16 * a
                    c, n = 2 * j + u // 2 + 8 * a, u // 2
                    if live and u % 2 == 0 and more:
                        ln_copy(c + 1)
                    if not (first and u < 1):
                        exponent(a, (u - 1) % 4, i - 1)
                    if not (first and u < 2):
                        p_high(i - 2)
                    if a and not (first and u < 3):
                        cat_copy(i - 3, i - 19)
                    if live and u % 2 == 1:
                        v_high(n, c, i - 1)
                    if live and u % 2 == 0 and more:
                        qk_copy(a, 1 - n, c + 1, i + 2)
                    if live and more and a == 2:
                        key_heads(1 - n, c + 1, u % 2)

                ln_copy(8 * a)
                if a == 0:
                    ac.wait_ge(ld_qk, 16 * 7)
                    ac.wait_ge(zeroed_v, 4)
                qk_copy(a, 0, 8 * a, 16 * a)
                key_heads(0, 8 * a, 1)
                for u in range(4):
                    step(u, 0, first=True)
                    if a == 0 and u == 1:
                        ac.wait_ge(ctx_summed, 1)
                        act(ctx_sum[:, :], psC[:, 0:B], ACT.Copy).then_inc(ctx_summed, 1)
                with ac.Fori(1, 3) as j:
                    for u in range(4):
                        step(u, j)
                for u in range(4):
                    step(u, 3, more=(u < 2))
                for u in range(3):
                    i = 16 + u + 16 * a
                    if u < 1:
                        exponent(a, (u - 1) % 4, i - 1)
                    if u < 2:
                        p_high(i - 2)
                    if a:
                        cat_copy(i - 3, i - 19)

            def logits_in(kind, g):
                G, R = GROUPS * FFN[kind] + g, GROUPS * MOE[kind] + g
                ac.wait_ge(f_lnp, G + 1)
                if g >= 2:
                    ac.wait_ge(r_rt, R - 1)
                elif G >= 2:
                    ac.wait_ge(f_x, G - g)
                act(routed[g % 2], psH[1 - g % 2][:, :], ACT.Copy).then_inc(f_ln, 1)

            def ffn_ln(G, wait_read):
                ac.wait_ge(f_lnp, G + 1)
                wait_read()
                act(lnF[:, :], psL[:, :], ACT.Copy).then_inc(f_ln, 1)

            def ff_start(kind):
                f0 = GROUPS * FFN[kind]
                ffn_ln(f0, lambda: ac.wait_ge(f_x, f0) if f0 else None)

            def plain(kind):
                f0 = GROUPS * FFN[kind]
                up, read, hid, y = fs[kind]

                def group(g, last):
                    for f in range(FT):
                        ac.wait_ge(up, g * FT + (f + 1))
                        if f == 0 and not (isinstance(g, int) and g == 0):
                            ac.wait_ge(y, g)
                        if kind == "ffn1":
                            act(hT[:, f, :], psS[:, f % 2, :], ACT.Relu).then_inc(read, 1)
                        else:
                            act(hT[:, f, :], psS[:, f % 2, :], ACT.Gelu_apprx_tanh, bias=b1[:, f:f + 1]).then_inc(read, 1)
                    if kind == "ffn1" and g + 2 < GROUPS:
                        lin_ln(g + 2)
                    if not last:
                        ffn_ln(g + (f0 + 1), lambda: None)

                if kind == "ffn1":
                    for g in range(2):
                        lin_ln(g)
                ff_start(kind)
                group(0, False)
                if kind == "ffn1":
                    for g in range(1, GROUPS - 1):
                        group(g, False)
                else:
                    with ac.Fori(1, GROUPS - 1) as g:
                        group(g, False)
                group(GROUPS - 1, True)

            def lin_ln(g):
                ac.wait_ge(l_lnp, g + 1)
                if g:
                    ac.wait_ge(l_y, g)
                act(lnL, psO[:, :], ACT.Copy).then_inc(l_ln, 1)

            def blocks(kind):
                b0, nb = BLOCK0[kind], NBLOCKS[kind]

                def since(k, sm, v):
                    if not (isinstance(k, int) and k < 0):
                        ac.wait_ge(sm, v)

                def x_copy(q, b):
                    k = b + b0
                    ac.wait_ge(b_xt, k + 1)
                    since(k - 2, b_m1, k - 1)
                    act(xbT[q % 2], psQ[:, 0:P], ACT.Copy).then_inc(b_xc, 1)

                def activate(q, b):
                    k = b + b0
                    ac.wait_ge(b_m1, k + 1)
                    if kind == "moe0":
                        since(k - 2, b_t2, k - 1)
                        act(hb[q % 2], psS[:, q % 2, :], ACT.Gelu).then_inc(b_hd, 1)
                    else:
                        n = 4 * MC if kind == "shared" else MI
                        since(k - 2, b_hd, k - 1)
                        act(gated[q % 2][:, 0:n], psS[:, q % 2, 0:n], ACT.Silu).then_inc(b_sg, 1)

                def h_copy(q, b):
                    k = b + b0
                    ac.wait_ge(b_t2, k + 1)
                    since(k - 2, b_m2, k - 1)
                    n = (4 if kind == "shared" else 2) * P
                    act(hbT[q % 2][0:MC, 0:n], psH[q % 2][0:MC, 0:n], ACT.Copy).then_inc(b_hc, 1)

                def step(q, s, lo=-2, hi=None):
                    if hi is None or s + 2 < nb:
                        x_copy((q + 2) % NX, s + 2)
                    if lo >= -1 and (hi is None or s + 1 < nb):
                        activate((q + 1) % NX, s + 1)
                    if lo >= 0 and kind != "moe0" and (hi is None or s < nb):
                        h_copy(q, s)

                staggered(ac, nb, step)

            def moe(kind):
                f0, m = GROUPS * FFN[kind], MOE[kind]
                for g in range(GROUPS):
                    logits_in(kind, g)
                for h in range(TILES // RT_T):
                    R = TILES // RT_T * m + h
                    ac.wait_ge(r_top, R + 1)
                    if kind == "moe0":
                        act(psum8[:, :], top8[:, :, 0], ACT.Exp, scale=-1.0).then_inc(r_e, 1)
                    else:
                        act(prob[:, :, :], prob[:, :, :], ACT.Exp).then_inc(r_e, 1)
                        ac.wait_ge(f_xn, f0 + GROUPS // 2 * (h + 1))
                        ts = slice(RT_T * h, RT_T * (h + 1))
                        act(pay[:, ts, 1, 0:D], pay[:, ts, 0, 0:D], ACT.Copy).then_inc(r_dup, 1)
                if kind == "moe0":
                    ac.wait_ge(ld_prep, PREP)
                    for name in copy_jobs(FIRST, len(JOBS)):
                        if name == "u1T":
                            ac.wait_ge(setup_ev, job_done("rel"))
                            ac.dma_start(rel_dram[:, :, 0:REL], rel_row[:, 0:REL].unsqueeze(1).broadcast_to([H, S, REL])).then_inc(rel_out, 16)
                        if name == "bias3":
                            ac.wait_ge(setup_ev, job_done("batch"))
                            ac.dma_start(batch_dram, per_batch[:, :]).then_inc(batch_out, 16)
                    ac.wait_ge(rel_out, 16)
                    skew = rel_dram.rearrange("h q j -> h (q j)")[:, 0:S * (P - 1)].rearrange("h (q j) -> q h j", j=P - 1)
                    for b in range(2):
                        ac.dma_start(bias2[b * S:(b + 1) * S], skew[:, :, S - 1:2 * S - 1]).then_inc(rel_in, 16)
                    ac.wait_ge(batch_out, 16)
                    for b in range(2):
                        ac.dma_start(tok_in[b * S:(b + 1) * S].rearrange("p (t d) -> p t d", t=TILES),
                                     batch_dram.rearrange("(t b) d -> b t d", b=2)[b].partition_broadcast(S)).then_inc(batch_in, 16)
                if kind == "moe3":
                    blocks("shared")
                blocks(kind)

            for ph in PHASES:
                if ph in ATT:
                    attention(ATT[ph])
                else:
                    {"plain": plain, "moe": moe}[KIND[ph]](ph)

        @block.gpsimd
        def _(pool):
            nc.gpsimd.memset(minus_half[:], -0.5).then_inc(zeroed, 1)
            pool.wait_ge(zeroed, 1)
            pool.wait_ge(ld_const, 16)

            def ln_rstd(stat, done, mv, rs, k, nt):
                wait_apart(pool, stat, k + 1)
                nc.gpsimd.tensor_scalar(rs[:, 0:nt, 0], mv[:, 0:nt, 1], EPS, 1.0, ALU.add, ALU.mult).then_inc(done, 1)
                pool.wait_ge(done, 2 * k + 1)
                nc.gpsimd.tensor_tensor(rs[:, 0:nt, 1], rs[:, 0:nt, 0], minus_half[:, 0:nt], ALU.pow).then_inc(done, 1)

            def subtract(m, i):
                pool.wait_ge(a_mx, i + 1)
                nc.gpsimd.tensor_tensor(sc[m], sc[m],
                                        mx[m][:, :].unsqueeze(2).broadcast_to([P, H, S]), ALU.subtract).then_inc(a_sub, 1)

            def key_heads(n, cg, pair0, part):
                if part == 0:
                    pool.wait_ge(a_q, cg + 1)
                    if not (isinstance(cg, int) and cg < 2):
                        wait_apart(pool, a_sc, 2 * pair0 - 4)
                for r in range(4 * part, 4 * part + 4):
                    last = nc.gpsimd.tensor_scalar(k_heads[n][:, :, :, r, :].rearrange("p h u s -> p (h u) s"),
                                                   kT[:, :, :, :].rearrange("p h u s -> p (h u) s"),
                                                   head_mask[:, r:r + 1], 1.0, ALU.mult, ALU.mult)
                last.then_inc(a_km, 1)

            def side_sum(m, i, ii):
                if isinstance(i, int):
                    pool.wait_ge(a_side[m], 32 * ((i - 32 - m) // 4 + 1))
                else:
                    wait_apart(pool, a_side[m], (i - (32 + m)) * 8 + 32)
                nc.gpsimd.tensor_tensor(side[m], side[m], add3[:, ds(ii * S, S)].unsqueeze(1).broadcast_to([P, H, S]),
                                        ALU.add).then_inc(a_sidef, 1)

            def add_bias(c, cg, a):
                pool.wait_ge(a_xn, cg + 1)
                xs = x[:, ds(c * CH, CH)].rearrange("p (t d) -> p t d", t=2)
                nc.gpsimd.tensor_tensor(xs, xs, bias_out[:, a // 2, :].unsqueeze(1).broadcast_to([P, 2, D]), ALU.add).then_inc(a_xb, 1)

            def attention(a):
                def ln(cg):
                    ln_rstd(a_stat, a_rstd, mvA, rsA, cg, 2)

                def step(u, j, more=True):
                    i = 4 * j + u + 16 * a
                    c, n = 2 * j + u // 2, u // 2
                    if u % 2 == 1 and more and a != 2:
                        key_heads(1 - n, c + (8 * a + 1), i + 1, 1)
                    if a == 2 and not (u == 3 and more is False):
                        side_sum((u + 1) % 4, i + 1, 4 * j + (u + 1))
                    subtract(u, i)
                    if u % 2 == 0 and more and a != 2:
                        key_heads(1 - n, c + (8 * a + 1), i + 2, 0)
                    if u % 2 == 0 and more is True:
                        ln(c + (8 * a + 2))
                    if u % 2 == 1 and more is True and a != 1:
                        add_bias(c + 2, c + (8 * a + 2), a)

                ln(8 * a)
                if a == 2:
                    pool.wait_ge(pad_added, 3)
                    side_sum(0, 32, 0)
                key_heads(0, 8 * a, 16 * a, 0)
                ln(8 * a + 1)
                if a == 0:
                    pool.wait_ge(setup_ev, job_done("bias0"))
                if a != 1:
                    add_bias(0, 8 * a, a)
                    add_bias(1, 8 * a + 1, a)
                with pool.Fori(0, 3) as j:
                    for u in range(4):
                        step(u, j)
                for u in range(4):
                    step(u, 3, more="no ln" if u < 2 else False)

            def ffn_ln(g, G, kind):
                ln_rstd(f_stat, f_rstd, mvF, rsF, G, 4)
                if kind == "ffn2":
                    pool.wait_ge(f_xn, G + 1)
                    xs = x[:, ds(g * GR, GR)].rearrange("p (t d) -> p t d", t=4)
                    nc.gpsimd.tensor_tensor(xs, xs, bias_out[:, 2, :].unsqueeze(1).broadcast_to([P, 4, D]), ALU.add).then_inc(f_xb, 1)

            def lin_rstd(g):
                ts = slice(4 * g, 4 * g + 4)
                ln_rstd(l_stat, l_rstd, mvM[:, ts], rsM[:, ts], g, 4)

            def lin_term(g):
                pool.wait_ge(l_xn, g + 1)
                xs = x[:, g * GR:(g + 1) * GR]
                nc.gpsimd.tensor_tensor(xs, xs, tok_in[:, g * GR:(g + 1) * GR], ALU.add).then_inc(f_xb, 1)

            def plain(kind):
                f0 = GROUPS * FFN[kind]
                if kind == "ffn1":
                    pool.wait_ge(batch_in, 32)
                    lin_rstd(0)
                    lin_rstd(1)
                    lin_term(0)
                    lin_term(1)
                    ffn_ln(0, f0, kind)
                    for g in range(GROUPS - 1):
                        if g + 2 < GROUPS:
                            lin_rstd(g + 2)
                        ffn_ln(g + 1, g + 1 + f0, kind)
                        if g + 2 < GROUPS:
                            lin_term(g + 2)
                else:
                    with pool.Fori(0, GROUPS) as g:
                        ffn_ln(g, g + f0, kind)

            def scatter(dst, places, src, s, limit):
                nc.gpsimd.indirect_dma_start(dst, bass.IndirectOffsetOnAxis(ap=places, axis=0), src, None,
                                             bounds_check=limit, oob_is_err=False).then_inc(s, 16)

            def moe(kind):
                f0, m = GROUPS * FFN[kind], MOE[kind]
                for g in range(GROUPS):
                    ts = slice(4 * g, 4 * g + 4)
                    ln_rstd(f_stat, f_rstd, mvM[:, ts], rsM[:, ts], f0 + g, 4)
                if kind == "moe0":
                    pool.wait_ge(ld_prep, PREP)
                    p8 = pad_words[:, :, :].rearrange("p t k -> p (t k)").bitcast(U8)
                    nc.gpsimd.tensor_scalar(add3[:, :], p8, -3.0e38, 1.0e38, ALU.mult, ALU.mult).then_inc(pad_added, 1)
                    nc.gpsimd.tensor_scalar(amask[:, :], amask[:, :], 0.5, 1.0, ALU.mult, ALU.mult).then_inc(pad_added, 1)
                    a3 = add3[:, :].rearrange("p (t k) -> p t k", t=TILES)
                    pool.wait_ge(pad_added, 2)
                    nc.gpsimd.tensor_tensor(a3, a3, amask[:, :].unsqueeze(1).broadcast_to([P, TILES, S]), ALU.add).then_inc(pad_added, 1)
                for h in range(TILES // RT_T):
                    send(kind, m, h)
                b0, nb = BLOCK0[kind], NBLOCKS[kind]
                with pool.Fori(0, nb // NX) as j:
                    for n in range(NX):
                        wait_apart(pool, b_ye, NX * j + (b0 + n + 1))
                        scatter(results, xin[n][:, D + 1:D + 2].bitcast(U32), yb[n], b_sc[n], 2 * TOK - 1)

            def send(kind, m, h):
                pool.wait_ge(r_slot, TILES // RT_T * m + h + 1)
                if kind == "moe3":
                    pool.wait_ge(r_dup, h + 1)
                for t in range(RT_T * h, RT_T * (h + 1)):
                    for c in range(CHOICES[kind]):
                        scatter(dispatched, slot[:, c, t:t + 1], pay[:, t, c, :], r_sent, E * REGION - 1)

            for ph in PHASES:
                if ph in ATT:
                    attention(ATT[ph])
                else:
                    {"plain": plain, "moe": moe}[KIND[ph]](ph)

        tt, ts_, stt = nc.vector.tensor_tensor, nc.vector.tensor_scalar, nc.vector.scalar_tensor_tensor

        @block.vector
        def _(v):
            nc.vector.memset(ones[:], 1.0)
            nc.vector.memset(s_row[:], float(S))
            nc.vector.memset(pad_row[:], 0.0)
            for n in range(2):
                nc.vector.memset(q_diag[n][:], 0.0)
                nc.vector.memset(cat[n][:], 0.0)
                nc.vector.memset(v_hi[n][:], 0.0)
                nc.vector.memset(v_lo[n][:], 0.0).then_inc(zeroed_v, 1)
            v.wait_ge(zeroed_v, 2)
            v.wait_ge(ld_const, 16)
            for n in range(2):
                nc.vector.tensor_copy(v_hi[n][:, :, :, :, 8].rearrange("p u b h -> p (u b) h"),
                                      dup_mask[:, 0:P:8].unsqueeze(1).broadcast_to([P, 4, H])).then_inc(zeroed_v, 1)
            def own(ins):
                chain[0] += 1
                ins.then_inc(dve_prep, 1)
                v.wait_ge(dve_prep, chain[0])
            chain = [0]
            v.wait_ge(ld_wo, 16 * 4)
            nc.vector.tensor_copy(bv_twice.rearrange("p h (b s) -> p h b s", b=2),
                                  bv_row[:, :].rearrange("p (s h) -> p h s", h=2).unsqueeze(2).broadcast_to([P, 2, 2, 64]))\
              .then_inc(bv_ready, 1)

            def bitlinear(w, s, n, width, out):
                w3 = w.rearrange("p (n d) -> p n d", n=n)
                own(nc.vector.tensor_reduce(s[:, 0:n], w3, axis=AX_X, op=ALU.add, apply_absolute_value=True))
                own(ts_(s[:, 0:n], s[:, 0:n], 1.0 / width, 1e-5, ALU.mult, ALU.max))
                own(ts_(s[:, 4:4 + n], s[:, 0:n], 0.5, None, ALU.mult))
                half = s[:, 4:4 + n].unsqueeze(2).broadcast_to([P, n, width])
                t3 = hT[:, 1, :].rearrange("p (n d) -> p n d", n=n)
                c3 = hT[:, 0, :].rearrange("p (n d) -> p n d", n=n)
                own(tt(t3, w3, half, ALU.is_gt))
                own(stt(c3, w3, -1.0, half, ALU.mult, ALU.is_gt))
                own(tt(t3, t3, c3, ALU.subtract))
                own(tt(t3, t3, w3, ALU.subtract))
                own(tt(t3, t3, w3, ALU.add))
                tt(out.rearrange("p (n d) -> p n d", n=n), t3, s[:, 0:n].unsqueeze(2).broadcast_to([P, n, width]),
                   ALU.mult).then_inc(tern_ready, 1)

            def ternary_in():
                v.wait_ge(ld_fc, 16)
                bitlinear(fc_raw[:, :, :].rearrange("p a b -> p (a b)"), row_scale, FT, P,
                          tern[:, :, :].rearrange("p a b -> p (a b)"))

            def ternary_out():
                v.wait_ge(tern_ready, 1)
                bitlinear(proj_raw[:, :], row_scale, 1, FF, proj_raw[:, :])

            def stats(xs, nt, st, mv, stat, k, busy):
                for t in range(nt):
                    last = nc.vector.bn_stats(st[:, t, :], xs(t))
                last.then_inc(stat[0], 1)
                busy()
                wait_apart(v, stat[0], k + 1)
                for t in range(nt):
                    last = nc.vector.bn_aggr(mv[:, t, :], st[:, t, :])
                last.then_inc(stat[1], 1)

            def normalise(xs, nt, xn, mv, rs, rstd, k, done):
                v.wait_ge(rstd, 2 * k + 2)
                for t in range(nt):
                    last = ts_(xn[:, t, :], xs(t), mv[:, t, 0:1], rs[:, t, 1:2], ALU.subtract, ALU.mult)
                last.then_inc(done, 1)

            def a_stats(c, cg):
                stats(lambda t: x[:, ds(c * CH + t * D, D)], 2, stA, mvA, (a_bn, a_stat), cg,
                      lambda: None if isinstance(cg, int) and cg == 0 else v.wait_ge(a_xn, cg))

            def a_normalise(c, cg):
                if not (isinstance(cg, int) and cg == 0):
                    v.wait_ge(a_lnp, cg)
                normalise(lambda t: x[:, ds(c * CH + t * D, D)], 2, xnA, mvA, rsA, a_rstd, cg, a_xn)

            def evacuate(a, m, i, ii):
                if not (isinstance(i, int) and i < 4):
                    v.wait_ge(a_tr, 2 * i - 6)
                if a == 2:
                    v.wait_ge(a_sidef, i - 31)
                for half in range(2):
                    v.wait_ge(a_sc, 2 * i + half + 1)
                    o = sc[m][:, 8 * half:8 * half + 8, :]
                    s = psS[:, half, :].rearrange("p (h k) -> p h k", h=8)
                    if a == 0:
                        r = stt(o, s, QK_SCALE, cap0[:, ds(ii * S, S)].unsqueeze(1).broadcast_to([P, 8, S]), ALU.mult, ALU.min)
                    elif a == 1:
                        r = tt(o, s, bias2[:, 8 * half:8 * half + 8, :], ALU.add)
                    else:
                        r = stt(o, s, QK_SCALE / 2, side[m][:, 8 * half:8 * half + 8, :], ALU.mult, ALU.add)
                    r.then_inc(a_ev, 1)
                v.wait_ge(a_ev, 2 * i + 2)
                if not (isinstance(i, int) and i < 4):
                    v.wait_ge(a_sub, i - 3)
                nc.vector.reduce_max(mx[m][:, :], sc[m], axis=AX_X).then_inc(a_mx, 1)

            def v_low(n, cg, pair0):
                v.wait_ge(a_vhi, cg + 1)
                if not (isinstance(cg, int) and cg < 2):
                    v.wait_ge(a_pv, pair0 - 2)
                for r in range(2):
                    last = tt(v_part(v_lo[n], r), v_product(r), v_part(v_hi[n], r), ALU.subtract)
                last.then_inc(a_vlo, 1)

            def p_low(i):
                for half in range(2):
                    v.wait_ge(a_hi, 2 * i + half + 1)
                    if half == 0 and not (isinstance(i, int) and i == 0):
                        v.wait_ge(a_pv, i)
                    r = slice(4 * half, 4 * half + 4)
                    tt(p_lo[:, r, :].rearrange("p j t -> p (j t)"), psT[:, half, :],
                       p_hi[:, r, :].rearrange("p j t -> p (j t)"), ALU.subtract).then_inc(a_lo, 1)

            def concat(a, m, i, ia):
                v.wait_ge(a_pv, i + 1)
                if not (isinstance(i, int) and i < 2):
                    v.wait_ge(a_out, i - 1)
                o = psO[:, 0:2 * H * 9].rearrange("p (b h e) -> p b h e", b=2, h=H)
                for b in range(2):
                    r = slice(b * 64, b * 64 + 64)
                    last = nc.vector.reciprocal(rsum[r, :], o[r, b, :, 8])
                last.then_inc(a_rs, 1)
                v.wait_ge(a_rs, i + 1)
                for b in range(2):
                    r = slice(b * 64, b * 64 + 64)
                    if a == 0:
                        dst = cat[m][r, :, r].rearrange("p h2 (h d2) -> p h d2 h2", h=H)
                        src = o[r, b, :, 0:8].rearrange("p h (d2 h2) -> p h d2 h2", h2=2)
                        rr = rsum[r, :].unsqueeze(2).unsqueeze(3).broadcast_to([64, H, 4, 2])
                    else:
                        dst = cat[m][r, 0, :].rearrange("p (h d) -> p h d", h=H)
                        src = o[r, b, :, 0:8]
                        rr = rsum[r, :].unsqueeze(2).broadcast_to([64, H, 8])
                    last = tt(dst, src, rr, ALU.mult)
                last.then_inc(a_cat, 1)

            def residual(a, i, ii, cg):
                v.wait_ge(a_out, i + 1)
                if a != 1:
                    v.wait_ge(a_xb, cg + (1 if a == 0 else -7))
                xs = x[:, ds(ii * D, D)]
                tt(xs, xs, psC[:, P:2 * P], ALU.add).then_inc(a_x, 1)

            def attention(a):
                def step(u, j, first=False, more=True, live=True):
                    ii = 4 * j + u
                    i = ii + 16 * a
                    c, n = 2 * j + u // 2, u // 2
                    cg = c + 8 * a
                    if live:
                        evacuate(a, u, i, ii)
                    if not (first and u < 2):
                        p_low(i - 2)
                    if not (first and u < 3):
                        residual(a, i - 3, ii - 3, cg - 2 + u % 2)
                    if live and u % 2 == 1 and more:
                        a_normalise(c + 2, cg + 2)
                    if live and u % 2 == 0 and more:
                        wait_x(c + 2)
                        a_stats(c + 2, cg + 2)
                    if not (first and u < 2):
                        concat(a, u % 2, i - 2, None)
                    if live and u % 2 == 1:
                        v_low(n, cg, i - 1)

                def wait_x(c):
                    if a:
                        f = GROUPS * (F_BEFORE[(0, 2, 3)[a]] - 1)
                        v.wait_ge(f_x, c // 2 + f + 1 if isinstance(c, int) else FXJ[0] + (f + 2))

                if a == 0:
                    v.wait_ge(ld_x, 16)
                if a == 1:
                    v.wait_ge(rel_in, 32)
                for c in range(2):
                    if a:
                        v.wait_ge(f_x, GROUPS * (F_BEFORE[(0, 2, 3)[a]] - 1) + 1)
                    if a and c == 0:
                        continue
                    a_stats(c, 8 * a + c)
                    if a == 0 and c == 1:
                        ternary_in()
                    a_normalise(c, 8 * a + c)
                if a == 0:
                    v.wait_ge(ld_mask, 32)
                    m8 = mask_words[:, :, :].rearrange("p t k -> p (t k)").bitcast(U8)
                    ts_(cap0[:, :], m8, 3.0e38, NEG, ALU.mult, ALU.add).then_inc(cap_ready, 1)
                    v.wait_ge(cap_ready, 1)
                for u in range(4):
                    step(u, 0, first=True)
                with v.Fori(1, 3) as j:
                    FXJ[0] = j
                    for u in range(4):
                        step(u, j)
                for u in range(4):
                    step(u, 3, more=False)
                for u in range(3):
                    step(u, 4, live=False) if u < 2 else residual(a, 15 + 16 * a, 15, 8 * a + 7)
                    if u < 2 and a in NEXT:
                        early(NEXT[a], u)

            FXJ = [0]

            def x_tile(g):
                return lambda t: x[:, ds(g * GR + t * D, D)]

            def f_stats(g, G, prev):
                prev(g)
                stats(x_tile(g), 4, stF, mvF, (f_bn, f_stat), G,
                      lambda: None if isinstance(G, int) and G == 0 else v.wait_ge(f_xn, G))

            def f_normalise(g, G):
                if not (isinstance(G, int) and G == 0):
                    v.wait_ge(f_lnp, G)
                normalise(x_tile(g), 4, xnF, mvF, rsF, f_rstd, G, f_xn)

            def lin_stats(g):
                ts = slice(4 * g, 4 * g + 4)
                v.wait_ge(f_x, GROUPS * (FFN["ffn1"] - 1) + g + 1)
                stats(x_tile(g), 4, stM[:, ts], mvM[:, ts], (l_bn, l_stat), g, lambda: None)

            def lin_normalise(g):
                ts = slice(4 * g, 4 * g + 4)
                if g:
                    v.wait_ge(l_lnp, g)
                normalise(x_tile(g), 4, xnL, mvM[:, ts], rsM[:, ts], l_rstd, g, l_xn)

            def lin_end(g):
                v.wait_ge(l_y, g + 1)
                v.wait_ge(f_xb, g + 1)
                xs = x[:, g * GR:(g + 1) * GR]
                tt(xs, xs, psT[:, 1, :], ALU.add).then_inc(l_x, 1)

            def before_phase(kind):
                if kind == "ffn1":
                    return lambda g: v.wait_ge(l_x, g + 1)
                if kind in F_AFTER_A:
                    k = 16 * (F_AFTER_A[kind] - 1)
                    return lambda g: v.wait_ge(a_x, g * 4 + (k + 4))
                k = GROUPS * (FFN[kind] - 1)
                return lambda g: v.wait_ge(f_x, g + (k + 1))

            def plain(kind):
                f0 = GROUPS * FFN[kind]
                _, read, hid, y = fs[kind]
                prev = before_phase(kind)

                cg = 8 * A_AFTER_F[kind]

                def group(g, last):
                    if last:
                        a_stats(0, cg)
                    ahead = kind == "ffn1" and g + 2 < GROUPS
                    if ahead:
                        lin_stats(g + 2)
                    if not last:
                        f_stats(g + 1, g + (f0 + 1), prev)
                    for f in range(FT):
                        if kind == "ffn1":
                            v.wait_ge(read, g * FT + (f + 1))
                            tt(hT[:, f, :], hT[:, f, :], hT[:, f, :], ALU.mult).then_inc(hid, 1)
                        if f == 1 and ahead:
                            lin_normalise(g + 2)
                        if f == 2 and last:
                            a_normalise(0, cg)
                        if f == 2 and not last:
                            f_normalise(g + 1, g + (f0 + 1))
                    if ahead:
                        lin_end(g + 2)
                    v.wait_ge(y, g + 1)
                    if kind == "ffn2":
                        v.wait_ge(f_xb, g + (GROUPS + 1))
                    xs = x[:, ds(g * GR, GR)]
                    tt(xs, xs, psT[:, 0, :], ALU.add).then_inc(f_x, 1)

                if kind == "ffn1":
                    lin_normalise(1)
                    lin_end(0)
                if kind == "ffn1":
                    f_stats(0, f0, prev)
                    f_normalise(0, f0)
                    lin_end(1)
                    for g in range(GROUPS - 1):
                        group(g, False)
                else:
                    with v.Fori(0, GROUPS - 1) as g:
                        group(g, False)
                group(GROUPS - 1, True)

            def route(kind, h, R):
                n = CHOICES[kind]
                ts = slice(RT_T * h, RT_T * (h + 1))
                v.wait_ge(r_rt, GROUPS * MOE[kind] + GROUPS // 2 * (h + 1))
                lg = psR[h][:, RT_T * E * h:RT_T * E * (h + 1)].rearrange("p (t e) -> p t e", t=RT_T)
                if kind == "moe0":
                    own(tt(logit[:, :, :], lg, br0[:, :].unsqueeze(1).broadcast_to([P, RT_T, E]), ALU.add))
                    own(ts_(logit[:, :, :], logit[:, :, :], SATURATED, None, ALU.min))
                else:
                    own(nc.vector.tensor_copy(logit[:, :, :], lg))
                for t in range(RT_T):
                    last = nc.vector.max(top8[:, t, :], logit[:, t, :])
                if kind == "moe0":
                    last.then_inc(r_top, 1)
                    v.wait_ge(r_top, R + 1)
                else:
                    own(last)
                    tt(prob[:, :, :], top8[:, :, :], top8[:, :, 0:1].broadcast_to([P, RT_T, E]), ALU.subtract).then_inc(r_top, 1)
                for t in range(RT_T):
                    last = nc.vector.max_index(idx8[:, t, :], top8[:, t, :], logit[:, t, :])
                own(last)
                own(nc.vector.tensor_copy(idxf[:, 0:n, :].rearrange("p c t -> p t c"), idx8[:, :, 0:n]))
                for c in range(n):
                    last = tt(chosen[:, c, :, :], tab("iota").unsqueeze(1).broadcast_to([P, RT_T, E]),
                              idxf[:, c, :].unsqueeze(2).broadcast_to([P, RT_T, E]), ALU.is_equal)
                own(last)
                if n == 2:
                    tt(counted[:, :, :], chosen[:, 0], chosen[:, 1], ALU.add).then_inc(r_oh, 1)
                else:
                    nc.vector.tensor_copy(counted[:, :, :], chosen[:, 0]).then_inc(r_oh, 1)
                v.wait_ge(r_e, R + 1)
                if kind == "moe0":
                    own(ts_(psum8[:, :], psum8[:, :], 1.0, None, ALU.add))
                    own(nc.vector.reciprocal(pay[:, ts, 0, D], psum8[:, :]))
                else:
                    own(nc.vector.reduce_sum(psum8[:, :], prob[:, :, :], axis=AX_X))
                    own(nc.vector.reciprocal(psum8[:, :], psum8[:, :]))
                    own(tt(pw[:, :, :], prob[:, :, 0:2], psum8[:, :].unsqueeze(2).broadcast_to([P, RT_T, 2]), ALU.mult))
                    own(nc.vector.reduce_sum(psum8[:, :], pw[:, :, :], axis=AX_X))
                    own(ts_(psum8[:, :], psum8[:, :], 1e-20, None, ALU.add))
                    own(nc.vector.reciprocal(psum8[:, :], psum8[:, :]))
                    own(tt(pay[:, ts, :, D], pw[:, :, :], psum8[:, :].unsqueeze(2).broadcast_to([P, RT_T, 2]), ALU.mult))
                if h == 0:
                    own(nc.vector.tensor_copy(run[:, :], tab("base")))
                v.wait_ge(r_cnt, R + 1)
                own(tt(place[:, :, :], psQ[:, 0:RT_T * E].rearrange("p (t e) -> p t e", t=RT_T),
                       run[:, :].unsqueeze(1).broadcast_to([P, RT_T, E]), ALU.add))
                own(tt(run[:, :], run[:, :], psQ[:, RT_T * E:(RT_T + 1) * E], ALU.add))
                for c in range(n):
                    last = tt(spot[:, c], chosen[:, c], place[:, :, :], ALU.mult)
                own(last)
                own(nc.vector.reduce_sum(slotf[:, 0:n, :], spot[:, 0:n], axis=AX_X))
                nc.vector.tensor_copy(slot[:, 0:n, ts], slotf[:, 0:n, :]).then_inc(r_slot, 1)

            def block_table(kind, m):
                nb = NBLOCKS[kind]
                nc.vector.tensor_copy(tail[:, :], run[:, :]).then_inc(r_end, 1)
                own(tt(cnt[:, :], run[:, :], tab("base"), ALU.subtract))
                own(tt(cmp8[:, 0:TILES, :], cnt[:, :].unsqueeze(1).broadcast_to([P, TILES, E]),
                       tab("k128").unsqueeze(2).broadcast_to([P, TILES, E]), ALU.is_gt))
                own(nc.vector.reduce_sum(nblk[:, :], cmp8[:, 0:TILES, :].rearrange("p k e -> p e k"), axis=AX_X))
                own(tt(cmp8[:, 0:E, :], nblk[:, :].unsqueeze(1).broadcast_to([P, E, E]),
                       tab("le").rearrange("p (e f) -> p e f", e=E), ALU.mult))
                own(nc.vector.reduce_sum(cumb[:, :], cmp8[:, 0:E, :], axis=AX_X))
                own(tt(cmp8[:, 0:nb, :], cumb[:, :].unsqueeze(1).broadcast_to([P, nb, E]),
                       tab("k")[:, 0:nb].unsqueeze(2).broadcast_to([P, nb, E]), ALU.is_le))
                own(nc.vector.reduce_sum(blkf[:, 1, 0:nb], cmp8[:, 0:nb, :], axis=AX_X))
                own(tt(cmp8[:, 0:nb, :], cmp8[:, 0:nb, :], nblk[:, :].unsqueeze(1).broadcast_to([P, nb, E]), ALU.mult))
                own(nc.vector.reduce_sum(blkf[:, 0, 0:nb], cmp8[:, 0:nb, :], axis=AX_X))
                own(tt(blkf[:, 0, 0:nb], tab("k")[:, 0:nb], blkf[:, 0, 0:nb], ALU.subtract))
                own(ts_(blkf[:, 0, 0:nb], blkf[:, 0, 0:nb], float(P), None, ALU.mult))
                own(stt(blkf[:, 0, 0:nb], blkf[:, 1, 0:nb], float(REGION), blkf[:, 0, 0:nb], ALU.mult, ALU.add))
                own(ts_(blkf[:, 0, 0:nb], blkf[:, 0, 0:nb], float(E * REGION), None, ALU.min))
                own(ts_(blkf[:, 1, 0:nb], blkf[:, 1, 0:nb], float(E - 1), None, ALU.min))
                nc.vector.tensor_copy(blk[:, :, 0:nb], blkf[:, :, 0:nb]).then_inc(r_tab, 1)

            def blocks(kind):
                b0, nb = BLOCK0[kind], NBLOCKS[kind]

                def since(k, sm, val):
                    if not (isinstance(k, int) and k < 0):
                        v.wait_ge(sm, val)

                def h_copy(q, b):
                    k = b + b0
                    v.wait_ge(b_t2, k + 1)
                    since(k - 2, b_m2, k - 1)
                    nc.vector.tensor_copy(hbT[q % 2], psH[q % 2][:, :]).then_inc(b_hc, 1)

                def gate(q, b):
                    k = b + b0
                    v.wait_ge(b_sg, k + (1 - BLOCK0["shared"]))
                    since(k - 2, b_t2, k - 1)
                    n = 4 * MC if kind == "shared" else MI
                    up = psT[:, q % 2, 0:n] if kind == "shared" else psS[:, q % 2, MI:2 * MI]
                    tt(hb[q % 2][:, 0:n], gated[q % 2][:, 0:n], up, ALU.mult).then_inc(b_hd, 1)

                def result(q, b):
                    k = b + b0
                    v.wait_ge(b_m2, k + 1)
                    if kind == "shared":
                        xs = x[:, ds(b * D, D)]
                        tt(xs, xs, psC[:, 0:D], ALU.add).then_inc(b_ye, 1)
                    else:
                        ts_(yb[q], psC[:, 0:D], xin[q][:, D:D + 1], None, ALU.mult).then_inc(b_ye, 1)

                def step(q, s, lo=-2, hi=None):
                    if kind == "moe0" and lo >= 0 and (hi is None or s < nb):
                        h_copy(q, s)
                    if kind != "moe0" and lo >= -1 and (hi is None or s + 1 < nb):
                        gate((q + 1) % NX, s + 1)
                    if lo >= 1:
                        result((q - 1) % NX, s - 1)

                staggered(v, nb, step)

            def early(kind, u):
                if KIND[kind] != "moe":
                    if u == 0:
                        f_stats(0, GROUPS * FFN[kind], before_phase(kind))
                    else:
                        f_normalise(0, GROUPS * FFN[kind])
                elif u == 0:
                    if kind == "moe0":
                        v.wait_ge(ld_prep, PREP)
                        nc.vector.tensor_copy(pad_row[:, D + 1:D + 2].bitcast(U32), place_tab[:, 2 * TILES:2 * TILES + 1]).then_inc(pad_ready, 1)
                    for c in range(2):
                        nc.vector.tensor_copy(pay[:, :, c, D + 1].bitcast(U32), place_tab[:, c * TILES:(c + 1) * TILES])
                    statistics(kind, 0)
                    statistics(kind, 1)
                else:
                    normal(kind, 0)
                    statistics(kind, 2)

            def statistics(kind, g):
                ts = slice(4 * g, 4 * g + 4)
                before_phase(kind)(g)
                stats(x_tile(g), 4, stM[:, ts], mvM[:, ts], (f_bn, f_stat), GROUPS * FFN[kind] + g, lambda: None)

            def normal(kind, g):
                v.wait_ge(f_rstd, 2 * (GROUPS * FFN[kind] + g) + 2)
                xs = x_tile(g)
                for t in range(4 * g, 4 * g + 4):
                    last = ts_(pay[:, t, 0, 0:D], xs(t - 4 * g), mvM[:, t, 0:1], rsM[:, t, 1:2], ALU.subtract, ALU.mult)
                last.then_inc(f_xn, 1)

            def moe(kind):
                m = MOE[kind]

                normal(kind, 1)
                statistics(kind, 3)
                normal(kind, 2)
                normal(kind, 3)
                for h in range(TILES // RT_T):
                    route(kind, h, TILES // RT_T * m + h)
                block_table(kind, m)
                if kind == "moe0":
                    ternary_out()
                if kind == "moe3":
                    blocks("shared")
                blocks(kind)
                for g in range(GROUPS):
                    n = CHOICES[kind]
                    v.wait_ge(b_res[g], 16 * (1 if kind == "moe0" else 1 + n))
                    xs = x[:, g * GR:(g + 1) * GR]
                    if n == 2:
                        own(tt(xs, xs, pay_row[:, TOK + g * GR:TOK + (g + 1) * GR], ALU.add))
                    tt(xs, xs, pay_row[:, g * GR:(g + 1) * GR], ALU.add).then_inc(f_x, 1)
                    if kind == "moe0" and g < 2:
                        if g == 1:
                            lin_normalise(0)
                        lin_stats(g)

            for ph in PHASES:
                if ph in ATT:
                    attention(ATT[ph])
                else:
                    {"plain": plain, "moe": moe}[KIND[ph]](ph)


_INS = ['x', 'ctx_1024', 'fside_Bx16xSxS2_0', 'fside_SxS2_0', 'mask_BxSxS2_bf1', 'mask_BxS2_bf0',
        'L0_xattn_Wq', 'L0_xattn_bq', 'L0_xattn_Wk', 'L0_xattn_bk', 'L0_xattn_Wv', 'L0_xattn_bv', 'L0_xattn_Wo',
        'L0_xattn_bo', 'L0_ffn_Wr', 'L0_ffn_br', 'L0_ffn_W1', 'L0_ffn_W2', 'L1_xattn_W', 'L1_xattn_b',
        'L1_ffn_fast_b', 'L1_ffn_w_fc', 'L1_ffn_w_proj', 'L1_ffn_u', 'L1_ffn_v', 'L1_ffn_gate', 'L2_xattn_Wq',
        'L2_xattn_Wkv', 'L2_xattn_Wo', 'L2_xattn_rel_bias', 'L2_ffn_U1', 'L2_ffn_V1', 'L2_ffn_b1', 'L2_ffn_U2',
        'L2_ffn_V2', 'L2_ffn_b2', 'L3_xattn_Wq', 'L3_xattn_bq', 'L3_xattn_Wk', 'L3_xattn_bk', 'L3_xattn_Wv',
        'L3_xattn_bv', 'L3_xattn_Wo', 'L3_xattn_bo', 'L3_ffn_gate_w', 'L3_ffn_wg', 'L3_ffn_wu', 'L3_ffn_wd',
        'L3_ffn_swg', 'L3_ffn_swu', 'L3_ffn_swd']


def constants():
    part = np.arange(P)
    rel = np.arange(-(S - 1), S)
    nb, exact = BUCKETS // 2, BUCKETS // 4
    dist = np.maximum(np.abs(rel), 1).astype(np.float32)
    large = exact + (np.log(dist / np.float32(exact)) / np.float32(np.log(128 / exact)) * np.float32(nb - exact)).astype(np.int32)
    bucket = (rel > 0) * nb + np.where(np.abs(rel) < exact, np.abs(rel), np.minimum(large, nb - 1))
    f = np.float32
    return {
        "first_tab": np.concatenate([np.eye(P), part[:, None] // 64 == part[None, :] // DH % 2,
                                     part[:, None] % 64 // DH == np.arange(8)[None, :]], axis=1).astype(f),
        "route_tab": np.concatenate([
            np.broadcast_to(t.astype(f).ravel(), (P, t.size)) for t in (
                np.arange(E), np.arange(E) * REGION, np.arange(TILES) * P,
                np.arange(E)[None, :] <= np.arange(E)[:, None], np.arange(40))] + [part[:, None].astype(f)], axis=1),
        "place_tab": np.concatenate([part[:, None] + P * np.arange(2 * TILES)[None, :],
                                     np.full((P, 1), NOWHERE)], axis=1).astype(np.uint32),
        "before": (part[:, None] < part[None, :]).astype(np.float16),
        "rel_onehot": (np.arange(BUCKETS)[:, None] == bucket[None, :]).astype(f),
    }


def kernel(**inputs):
    import concourse.bacc as bacc
    from concourse.bass_utils import run_bass_kernel_spmd

    nc = bacc.Bacc("TRN2", target_bir_lowering=False, num_devices=1)
    arrays, args, consts = {}, {}, {}
    for name in _INS:
        a = np.ascontiguousarray(inputs[name])
        if a.ndim == 0:
            a = a.reshape(1)
        if a.dtype == np.bool_:
            a = a.view(np.uint32)
        arrays["in_" + name] = a
        args[name] = nc.dram_tensor("in_" + name, a.shape, mybir.dt.from_np(a.dtype), kind="ExternalInput").ap()
    for name, a in constants().items():
        arrays["const_" + name] = a
        consts[name] = nc.dram_tensor("const_" + name, a.shape, mybir.dt.from_np(a.dtype), kind="ExternalInput").ap()
    out = nc.dram_tensor("out_x", (B, S, D), F32, kind="ExternalOutput").ap()
    bass_transformer(nc, args, consts, out)
    r = run_bass_kernel_spmd(nc, [arrays], core_ids=[0])
    return r.results[0]["out_x"]
```
